# Optimizing a Trainium2 kernel written in Bass

```python
import numpy as np
import jax
import jax.numpy as jnp

def _softmax(x, axis=-1):
    return jax.nn.softmax(x, axis=axis)

def _gelu(x):
    return jax.nn.gelu(x, approximate=True)

def _silu(x):
    return jax.nn.silu(x)

def _sigmoid(x):
    return jax.nn.sigmoid(x)

def _layernorm(x, axis=-1, eps=1e-05):
    m = jnp.mean(x, axis=axis, keepdims=True)
    v = jnp.var(x, axis=axis, keepdims=True)
    return (x - m) / jnp.sqrt(v + eps)

def _scatter_add(tgt, idx, src, axis=0):
    return tgt.at[idx].add(src)

def _segment_sum(src, seg, n):
    return jax.ops.segment_sum(src, seg, n)
kernel_name = 'mk_xattn_seq_d4_seqx_r4_00201e'

def setup_inputs(seed: int=0):
    np.random.seed(seed)
    _w = jnp.asarray

    def _rec_inputs():
        import jax
        import jax.numpy as jnp
        _rk = jax.random.key(seed)
        x = 0.0003765 + 1 * jax.random.normal(jax.random.fold_in(_rk, 1), (32, 128, 256), jnp.float32)
        _lenS = 128 - jax.random.randint(jax.random.fold_in(_rk, 7), (32,), 0, max(1, 128 // 4) + 1, jnp.int32)
        _lenS2 = 128 - jax.random.randint(jax.random.fold_in(_rk, 8), (32,), 0, max(1, 128 // 4) + 1, jnp.int32)
        _ctx_1024P = jax.random.normal(jax.random.fold_in(_rk, 11), (32, 16, 256), jnp.float32)
        _ctx_1024c = jax.random.dirichlet(jax.random.fold_in(_rk, 511), 0.3 * jnp.ones((16,), jnp.float32), (32, 128))
        _ctx_1024t = jnp.einsum('bsk,bkd->bsd', _ctx_1024c, _ctx_1024P)
        _ctx_1024t = _ctx_1024t * jax.lax.rsqrt(jnp.mean(jnp.square(_ctx_1024t)) + 1e-12) * 0.953939
        ctx_1024 = -0.000292821 + 1.00034 * (_ctx_1024t + 0.3 * jax.random.normal(jax.random.fold_in(_rk, 611), (32, 128, 256), jnp.float32))
        _validS = jnp.arange(128)[None, :] < _lenS[:, None]
        _validS2 = jnp.arange(128)[None, :] < _lenS2[:, None]
        _causal = jnp.tril(jnp.ones((128, 128), dtype=bool))
        mask_Bx1x1xS2_if1 = jnp.where(jnp.ones((32, 1, 1, 128), dtype=bool), 1, 0).astype(jnp.int32)
        return (x, ctx_1024, mask_Bx1x1xS2_if1)
    x, ctx_1024, mask_Bx1x1xS2_if1 = _rec_inputs()

    def _L0_xattn_setup():
        import jax, jax.numpy as jnp
        import numpy as np
        EMBED = 256
        HEADS = 16
        HEAD_DIM = EMBED // HEADS
        FF = 4 * EMBED
        EPS = 1e-05

        def layernorm(x, g, b):
            mu = jnp.mean(x, axis=-1, keepdims=True)
            var = jnp.mean((x - mu) ** 2, axis=-1, keepdims=True)
            return (x - mu) * jax.lax.rsqrt(var + EPS) * g + b
        key = jax.random.key(seed)
        ks = jax.random.split(key, 16)
        B, S = (2, 512)
        f32 = jnp.float32
        inp = {'value': jax.random.normal(ks[0], (B, S, EMBED), f32), 'key': jax.random.normal(ks[1], (B, S, EMBED), f32), 'query': jax.random.normal(ks[2], (B, S, EMBED), f32), 'mask': jnp.ones((B, 1, 1, S), jnp.int32), 'wv': jax.random.normal(ks[3], (HEAD_DIM, HEAD_DIM), f32) * 0.02, 'wk': jax.random.normal(ks[4], (HEAD_DIM, HEAD_DIM), f32) * 0.02, 'wq': jax.random.normal(ks[5], (HEAD_DIM, HEAD_DIM), f32) * 0.02, 'w_out': jax.random.normal(ks[6], (EMBED, EMBED), f32) * 0.02, 'b_out': jnp.zeros((EMBED,), f32), 'g1': jnp.ones((EMBED,), f32), 'beta1': jnp.zeros((EMBED,), f32), 'w_ff1': jax.random.normal(ks[7], (EMBED, FF), f32) * 0.02, 'b_ff1': jnp.zeros((FF,), f32), 'w_ff2': jax.random.normal(ks[8], (FF, EMBED), f32) * 0.02, 'b_ff2': jnp.zeros((EMBED,), f32), 'g2': jnp.ones((EMBED,), f32), 'beta2': jnp.zeros((EMBED,), f32)}
        return inp
    _L0_xattn_all = _L0_xattn_setup()
    _L0_xattn_in = {k: v for k, v in _L0_xattn_all.items() if k in ('wv', 'wk', 'wq', 'w_out', 'b_out', 'g1', 'beta1', 'w_ff1', 'b_ff1', 'w_ff2', 'b_ff2', 'g2', 'beta2')}
    del _L0_xattn_all

    def _L1_xattn_setup():
        import jax, jax.numpy as jnp
        import numpy as np
        EMB_DIM = 256
        H = 16
        HEAD_DIM = EMB_DIM // H
        B = 2
        S = 512
        LN_EPS = 1e-05
        key = jax.random.key(seed)
        ks = jax.random.split(key, 8)
        scale_in = 1.0 / np.sqrt(EMB_DIM)
        scale_o = 1.0 / np.sqrt(H * HEAD_DIM)
        return {'enc_out': jax.random.normal(ks[0], (B, S, EMB_DIM), jnp.float32), 'dec_out': jax.random.normal(ks[1], (B, S, EMB_DIM), jnp.float32), 'Wq': jax.random.uniform(ks[2], (H, EMB_DIM, HEAD_DIM), jnp.float32, -scale_in, scale_in), 'Wk': jax.random.uniform(ks[3], (H, EMB_DIM, HEAD_DIM), jnp.float32, -scale_in, scale_in), 'Wv': jax.random.uniform(ks[4], (H, EMB_DIM, HEAD_DIM), jnp.float32, -scale_in, scale_in), 'Wo': jax.random.uniform(ks[5], (H * HEAD_DIM, EMB_DIM), jnp.float32, -scale_o, scale_o), 'gamma': jnp.ones((EMB_DIM,), jnp.float32), 'beta': jnp.zeros((EMB_DIM,), jnp.float32)}
    _L1_xattn_all = _L1_xattn_setup()
    _L1_xattn_in = {k: v for k, v in _L1_xattn_all.items() if k in ('Wq', 'Wk', 'Wv', 'Wo', 'gamma', 'beta')}
    del _L1_xattn_all

    def _L2_xattn_setup():
        import jax, jax.numpy as jnp
        import numpy as np
        B, S, SE, D, H, FF, E, K = (2, 512, 512, 256, 16, 1024, 8, 2)
        HD = D // H

        def _layernorm(x, g, b):
            m = x.mean(-1, keepdims=True)
            v = ((x - m) ** 2).mean(-1, keepdims=True)
            return (x - m) / jnp.sqrt(v + 1e-05) * g + b

        def _attn(q_in, k_in, v_in, wq, bq, wk, bk, wv, bv, wo, bo, causal):
            Bq, Sq, Dm = q_in.shape
            Sk = k_in.shape[1]
            Q = (q_in @ wq + bq).reshape(Bq, Sq, H, HD)
            Kp = (k_in @ wk + bk).reshape(Bq, Sk, H, HD)
            V = (v_in @ wv + bv).reshape(Bq, Sk, H, HD)
            scores = jnp.einsum('bqhd,bkhd->bhqk', Q, Kp) / jnp.sqrt(jnp.float32(HD))
            if causal:
                mask = jnp.tril(jnp.ones((Sq, Sk), bool))
                scores = jnp.where(mask, scores, -jnp.inf)
            a = jax.nn.softmax(scores, axis=-1)
            o = jnp.einsum('bhqk,bkhd->bqhd', a, V).reshape(Bq, Sq, Dm)
            return o @ wo + bo

        def _moe(x, rw, rb, w1, b1, w2, b2):
            T = x.shape[0] * x.shape[1]
            xf = x.reshape(T, D)
            router_weights = jax.nn.softmax(xf @ rw + rb, axis=-1)
            topw, topi = jax.lax.top_k(router_weights, K)
            topw = jax.nn.softmax(topw, axis=-1)
            combine = jnp.zeros((T, E), xf.dtype).at[jnp.arange(T)[:, None], topi].add(topw)
            h = jax.nn.gelu(jnp.einsum('td,edf->etf', xf, w1) + b1[:, None, :], approximate=False)
            eo = jnp.einsum('etf,efd->etd', h, w2) + b2[:, None, :]
            out = jnp.einsum('etd,te->td', eo, combine)
            return out.reshape(x.shape)
        key = jax.random.key(seed)
        ks = jax.random.split(key, 32)
        w = lambda k, shape: jax.random.normal(k, shape, jnp.float32) * 0.02
        inp = {'x': jax.random.normal(ks[0], (B, S, D), jnp.float32), 'encoder_output': jax.random.normal(ks[1], (B, SE, D), jnp.float32), 'sa_wq': w(ks[2], (D, D)), 'sa_bq': jnp.zeros((D,), jnp.float32), 'sa_wk': w(ks[3], (D, D)), 'sa_bk': jnp.zeros((D,), jnp.float32), 'sa_wv': w(ks[4], (D, D)), 'sa_bv': jnp.zeros((D,), jnp.float32), 'sa_wo': w(ks[5], (D, D)), 'sa_bo': jnp.zeros((D,), jnp.float32), 'ca_wq': w(ks[6], (D, D)), 'ca_bq': jnp.zeros((D,), jnp.float32), 'ca_wk': w(ks[7], (D, D)), 'ca_bk': jnp.zeros((D,), jnp.float32), 'ca_wv': w(ks[8], (D, D)), 'ca_bv': jnp.zeros((D,), jnp.float32), 'ca_wo': w(ks[9], (D, D)), 'ca_bo': jnp.zeros((D,), jnp.float32), 'ln1_g': jnp.ones((D,), jnp.float32), 'ln1_b': jnp.zeros((D,), jnp.float32), 'ln2_g': jnp.ones((D,), jnp.float32), 'ln2_b': jnp.zeros((D,), jnp.float32), 'ln3_g': jnp.ones((D,), jnp.float32), 'ln3_b': jnp.zeros((D,), jnp.float32), 'router_w': w(ks[10], (D, E)), 'router_b': jnp.zeros((E,), jnp.float32), 'e_w1': w(ks[11], (E, D, FF)), 'e_b1': jnp.zeros((E, FF), jnp.float32), 'e_w2': w(ks[12], (E, FF, D)), 'e_b2': jnp.zeros((E, D), jnp.float32)}
        return inp
    _L2_xattn_all = _L2_xattn_setup()
    _L2_xattn_in = {k: v for k, v in _L2_xattn_all.items() if k in ('sa_wq', 'sa_bq', 'sa_wk', 'sa_bk', 'sa_wv', 'sa_bv', 'sa_wo', 'sa_bo', 'ca_wq', 'ca_bq', 'ca_wk', 'ca_bk', 'ca_wv', 'ca_bv', 'ca_wo', 'ca_bo', 'ln1_g', 'ln1_b', 'ln2_g', 'ln2_b', 'ln3_g', 'ln3_b', 'router_w', 'router_b', 'e_w1', 'e_b1', 'e_w2', 'e_b2')}
    del _L2_xattn_all

    def _L3_xattn_setup():
        import jax, jax.numpy as jnp
        import numpy as np
        D_MODEL = 256
        N_HEADS = 16
        N_KV_HEADS = 1
        HEAD_DIM = D_MODEL // N_HEADS
        WINDOW = 128
        EPS = 1e-06
        NEG = -1000000000.0

        def _window_mask(S):
            i = jnp.arange(S)[:, None]
            j = jnp.arange(S)[None, :]
            half = WINDOW // 2
            return (j >= i - half) & (j < i + half + 1)
        key = jax.random.key(seed)
        ks = jax.random.split(key, 16)
        B, S, D = (2, 512, D_MODEL)
        kv_out = HEAD_DIM * N_KV_HEADS
        s = 0.02
        return {'query': jax.random.normal(ks[0], (B, S, D), jnp.float32), 'key': jax.random.normal(ks[1], (B, S, D), jnp.float32), 'value': jax.random.normal(ks[2], (B, S, D), jnp.float32), 'Wq': jax.random.normal(ks[3], (D, D), jnp.float32) * s, 'bq': jnp.zeros((D,), jnp.float32), 'Wk': jax.random.normal(ks[4], (D, kv_out), jnp.float32) * s, 'bk': jnp.zeros((kv_out,), jnp.float32), 'Wv': jax.random.normal(ks[5], (D, kv_out), jnp.float32) * s, 'bv': jnp.zeros((kv_out,), jnp.float32), 'Wo': jax.random.normal(ks[6], (D, D), jnp.float32) * s, 'bo': jnp.zeros((D,), jnp.float32), 'Wg': jax.random.normal(ks[7], (2 * D, D), jnp.float32) * s, 'bg': jnp.zeros((D,), jnp.float32), 'rms_w': jnp.ones((D,), jnp.float32)}
    _L3_xattn_all = _L3_xattn_setup()
    _L3_xattn_in = {k: v for k, v in _L3_xattn_all.items() if k in ('Wq', 'bq', 'Wk', 'bk', 'Wv', 'bv', 'Wo', 'bo', 'Wg', 'bg', 'rms_w')}
    del _L3_xattn_all
    return {'x': x, 'ctx_1024': ctx_1024, 'mask_Bx1x1xS2_if1': mask_Bx1x1xS2_if1, 'L0_xattn_wv': _L0_xattn_in['wv'], 'L0_xattn_wk': _L0_xattn_in['wk'], 'L0_xattn_wq': _L0_xattn_in['wq'], 'L0_xattn_w_out': _L0_xattn_in['w_out'], 'L0_xattn_b_out': _L0_xattn_in['b_out'], 'L0_xattn_g1': _L0_xattn_in['g1'], 'L0_xattn_beta1': _L0_xattn_in['beta1'], 'L0_xattn_w_ff1': _L0_xattn_in['w_ff1'], 'L0_xattn_b_ff1': _L0_xattn_in['b_ff1'], 'L0_xattn_w_ff2': _L0_xattn_in['w_ff2'], 'L0_xattn_b_ff2': _L0_xattn_in['b_ff2'], 'L0_xattn_g2': _L0_xattn_in['g2'], 'L0_xattn_beta2': _L0_xattn_in['beta2'], 'L1_xattn_Wq': _L1_xattn_in['Wq'], 'L1_xattn_Wk': _L1_xattn_in['Wk'], 'L1_xattn_Wv': _L1_xattn_in['Wv'], 'L1_xattn_Wo': _L1_xattn_in['Wo'], 'L1_xattn_gamma': _L1_xattn_in['gamma'], 'L1_xattn_beta': _L1_xattn_in['beta'], 'L2_xattn_sa_wq': _L2_xattn_in['sa_wq'], 'L2_xattn_sa_bq': _L2_xattn_in['sa_bq'], 'L2_xattn_sa_wk': _L2_xattn_in['sa_wk'], 'L2_xattn_sa_bk': _L2_xattn_in['sa_bk'], 'L2_xattn_sa_wv': _L2_xattn_in['sa_wv'], 'L2_xattn_sa_bv': _L2_xattn_in['sa_bv'], 'L2_xattn_sa_wo': _L2_xattn_in['sa_wo'], 'L2_xattn_sa_bo': _L2_xattn_in['sa_bo'], 'L2_xattn_ca_wq': _L2_xattn_in['ca_wq'], 'L2_xattn_ca_bq': _L2_xattn_in['ca_bq'], 'L2_xattn_ca_wk': _L2_xattn_in['ca_wk'], 'L2_xattn_ca_bk': _L2_xattn_in['ca_bk'], 'L2_xattn_ca_wv': _L2_xattn_in['ca_wv'], 'L2_xattn_ca_bv': _L2_xattn_in['ca_bv'], 'L2_xattn_ca_wo': _L2_xattn_in['ca_wo'], 'L2_xattn_ca_bo': _L2_xattn_in['ca_bo'], 'L2_xattn_ln1_g': _L2_xattn_in['ln1_g'], 'L2_xattn_ln1_b': _L2_xattn_in['ln1_b'], 'L2_xattn_ln2_g': _L2_xattn_in['ln2_g'], 'L2_xattn_ln2_b': _L2_xattn_in['ln2_b'], 'L2_xattn_ln3_g': _L2_xattn_in['ln3_g'], 'L2_xattn_ln3_b': _L2_xattn_in['ln3_b'], 'L2_xattn_router_w': _L2_xattn_in['router_w'], 'L2_xattn_router_b': _L2_xattn_in['router_b'], 'L2_xattn_e_w1': _L2_xattn_in['e_w1'], 'L2_xattn_e_b1': _L2_xattn_in['e_b1'], 'L2_xattn_e_w2': _L2_xattn_in['e_w2'], 'L2_xattn_e_b2': _L2_xattn_in['e_b2'], 'L3_xattn_Wq': _L3_xattn_in['Wq'], 'L3_xattn_bq': _L3_xattn_in['bq'], 'L3_xattn_Wk': _L3_xattn_in['Wk'], 'L3_xattn_bk': _L3_xattn_in['bk'], 'L3_xattn_Wv': _L3_xattn_in['Wv'], 'L3_xattn_bv': _L3_xattn_in['bv'], 'L3_xattn_Wo': _L3_xattn_in['Wo'], 'L3_xattn_bo': _L3_xattn_in['bo'], 'L3_xattn_Wg': _L3_xattn_in['Wg'], 'L3_xattn_bg': _L3_xattn_in['bg'], 'L3_xattn_rms_w': _L3_xattn_in['rms_w']}

def reference(x, ctx_1024, mask_Bx1x1xS2_if1, L0_xattn_wv, L0_xattn_wk, L0_xattn_wq, L0_xattn_w_out, L0_xattn_b_out, L0_xattn_g1, L0_xattn_beta1, L0_xattn_w_ff1, L0_xattn_b_ff1, L0_xattn_w_ff2, L0_xattn_b_ff2, L0_xattn_g2, L0_xattn_beta2, L1_xattn_Wq, L1_xattn_Wk, L1_xattn_Wv, L1_xattn_Wo, L1_xattn_gamma, L1_xattn_beta, L2_xattn_sa_wq, L2_xattn_sa_bq, L2_xattn_sa_wk, L2_xattn_sa_bk, L2_xattn_sa_wv, L2_xattn_sa_bv, L2_xattn_sa_wo, L2_xattn_sa_bo, L2_xattn_ca_wq, L2_xattn_ca_bq, L2_xattn_ca_wk, L2_xattn_ca_bk, L2_xattn_ca_wv, L2_xattn_ca_bv, L2_xattn_ca_wo, L2_xattn_ca_bo, L2_xattn_ln1_g, L2_xattn_ln1_b, L2_xattn_ln2_g, L2_xattn_ln2_b, L2_xattn_ln3_g, L2_xattn_ln3_b, L2_xattn_router_w, L2_xattn_router_b, L2_xattn_e_w1, L2_xattn_e_b1, L2_xattn_e_w2, L2_xattn_e_b2, L3_xattn_Wq, L3_xattn_bq, L3_xattn_Wk, L3_xattn_bk, L3_xattn_Wv, L3_xattn_bv, L3_xattn_Wo, L3_xattn_bo, L3_xattn_Wg, L3_xattn_bg, L3_xattn_rms_w):
    import jax
    import jax.numpy as jnp

    def _L0_xattn_ref(value, key, query, mask, wv, wk, wq, w_out, b_out, g1, beta1, w_ff1, b_ff1, w_ff2, b_ff2, g2, beta2):
        import jax, jax.numpy as jnp
        import numpy as np
        EMBED = 256
        HEADS = 16
        HEAD_DIM = EMBED // HEADS
        FF = 4 * EMBED
        EPS = 1e-05

        def layernorm(x, g, b):
            mu = jnp.mean(x, axis=-1, keepdims=True)
            var = jnp.mean((x - mu) ** 2, axis=-1, keepdims=True)
            return (x - mu) * jax.lax.rsqrt(var + EPS) * g + b
        B, S, E = query.shape
        v = value.reshape(B, -1, HEADS, HEAD_DIM) @ wv
        k = key.reshape(B, -1, HEADS, HEAD_DIM) @ wk
        q = query.reshape(B, -1, HEADS, HEAD_DIM) @ wq
        scores = jnp.einsum('bqhd,bkhd->bhqk', q, k)
        scores = jnp.where(mask == 0, jnp.float32(-1e+20), scores)
        attn = jax.nn.softmax(scores / jnp.sqrt(jnp.float32(EMBED)), axis=-1)
        out = jnp.einsum('bhqk,bkhd->bqhd', attn, v).reshape(B, S, E)
        attention = out @ w_out + b_out
        x = layernorm(attention + query, g1, beta1)
        ff = jax.nn.relu(x @ w_ff1 + b_ff1) @ w_ff2 + b_ff2
        return layernorm(ff + x, g2, beta2)

    def _L1_xattn_ref(enc_out, dec_out, Wq, Wk, Wv, Wo, gamma, beta):
        import jax, jax.numpy as jnp
        import numpy as np
        EMB_DIM = 256
        H = 16
        HEAD_DIM = EMB_DIM // H
        B = 2
        S = 512
        LN_EPS = 1e-05
        d = Wq.shape[-1]
        q = jnp.einsum('bse,hed->bhsd', dec_out, Wq)
        k = jnp.einsum('bte,hed->bhtd', enc_out, Wk)
        v = jnp.einsum('bte,hed->bhtd', enc_out, Wv)
        scores = jnp.einsum('bhsd,bhtd->bhst', q, k) / jnp.sqrt(jnp.asarray(d, q.dtype))
        att = jax.nn.softmax(scores, axis=-1)
        ctx = jnp.einsum('bhst,bhtd->bhsd', att, v)
        b, h, s, hd = ctx.shape
        ctx = ctx.transpose(0, 2, 1, 3).reshape(b, s, h * hd)
        transformed = ctx @ Wo
        x = dec_out + transformed
        mu = jnp.mean(x, axis=-1, keepdims=True)
        var = jnp.mean(jnp.square(x - mu), axis=-1, keepdims=True)
        return (x - mu) * jax.lax.rsqrt(var + LN_EPS) * gamma + beta

    def _L2_xattn_ref(x, encoder_output, sa_wq, sa_bq, sa_wk, sa_bk, sa_wv, sa_bv, sa_wo, sa_bo, ca_wq, ca_bq, ca_wk, ca_bk, ca_wv, ca_bv, ca_wo, ca_bo, ln1_g, ln1_b, ln2_g, ln2_b, ln3_g, ln3_b, router_w, router_b, e_w1, e_b1, e_w2, e_b2):
        import jax, jax.numpy as jnp
        import numpy as np
        B, S, SE, D, H, FF, E, K = (2, 512, 512, 256, 16, 1024, 8, 2)
        HD = D // H

        def _layernorm(x, g, b):
            m = x.mean(-1, keepdims=True)
            v = ((x - m) ** 2).mean(-1, keepdims=True)
            return (x - m) / jnp.sqrt(v + 1e-05) * g + b

        def _attn(q_in, k_in, v_in, wq, bq, wk, bk, wv, bv, wo, bo, causal):
            Bq, Sq, Dm = q_in.shape
            Sk = k_in.shape[1]
            Q = (q_in @ wq + bq).reshape(Bq, Sq, H, HD)
            Kp = (k_in @ wk + bk).reshape(Bq, Sk, H, HD)
            V = (v_in @ wv + bv).reshape(Bq, Sk, H, HD)
            scores = jnp.einsum('bqhd,bkhd->bhqk', Q, Kp) / jnp.sqrt(jnp.float32(HD))
            if causal:
                mask = jnp.tril(jnp.ones((Sq, Sk), bool))
                scores = jnp.where(mask, scores, -jnp.inf)
            a = jax.nn.softmax(scores, axis=-1)
            o = jnp.einsum('bhqk,bkhd->bqhd', a, V).reshape(Bq, Sq, Dm)
            return o @ wo + bo

        def _moe(x, rw, rb, w1, b1, w2, b2):
            T = x.shape[0] * x.shape[1]
            xf = x.reshape(T, D)
            router_weights = jax.nn.softmax(xf @ rw + rb, axis=-1)
            topw, topi = jax.lax.top_k(router_weights, K)
            topw = jax.nn.softmax(topw, axis=-1)
            combine = jnp.zeros((T, E), xf.dtype).at[jnp.arange(T)[:, None], topi].add(topw)
            h = jax.nn.gelu(jnp.einsum('td,edf->etf', xf, w1) + b1[:, None, :], approximate=False)
            eo = jnp.einsum('etf,efd->etd', h, w2) + b2[:, None, :]
            out = jnp.einsum('etd,te->td', eo, combine)
            return out.reshape(x.shape)
        x = _layernorm(x + _attn(x, x, x, sa_wq, sa_bq, sa_wk, sa_bk, sa_wv, sa_bv, sa_wo, sa_bo, True), ln1_g, ln1_b)
        x = _layernorm(x + _attn(x, encoder_output, encoder_output, ca_wq, ca_bq, ca_wk, ca_bk, ca_wv, ca_bv, ca_wo, ca_bo, False), ln2_g, ln2_b)
        x = _layernorm(x + _moe(x, router_w, router_b, e_w1, e_b1, e_w2, e_b2), ln3_g, ln3_b)
        return x

    def _L3_xattn_ref(query, key, value, Wq, bq, Wk, bk, Wv, bv, Wo, bo, Wg, bg, rms_w):
        import jax, jax.numpy as jnp
        import numpy as np
        D_MODEL = 256
        N_HEADS = 16
        N_KV_HEADS = 1
        HEAD_DIM = D_MODEL // N_HEADS
        WINDOW = 128
        EPS = 1e-06
        NEG = -1000000000.0

        def _window_mask(S):
            i = jnp.arange(S)[:, None]
            j = jnp.arange(S)[None, :]
            half = WINDOW // 2
            return (j >= i - half) & (j < i + half + 1)
        B, S, D = query.shape
        q = (query @ Wq + bq).reshape(B, S, N_HEADS, HEAD_DIM).transpose(0, 2, 1, 3)
        k = (key @ Wk + bk).reshape(B, S, N_KV_HEADS, HEAD_DIM).transpose(0, 2, 1, 3)
        v = (value @ Wv + bv).reshape(B, S, N_KV_HEADS, HEAD_DIM).transpose(0, 2, 1, 3)
        scale = 1.0 / jnp.sqrt(jnp.float32(HEAD_DIM))
        scores = jnp.matmul(q, jnp.swapaxes(k, -1, -2)) * scale
        keep = _window_mask(S)
        scores = jnp.where(keep[None, None], scores, NEG)
        probs = jax.nn.softmax(scores, axis=-1)
        attn = jnp.matmul(probs, v)
        attn = attn.transpose(0, 2, 1, 3).reshape(B, S, D)
        attn = attn @ Wo + bo
        gate = jax.nn.silu(jnp.concatenate([attn, query], axis=-1) @ Wg + bg)
        out = attn * gate + query * (1.0 - gate)
        x_hat = out * jax.lax.rsqrt(jnp.mean(out * out, axis=-1, keepdims=True) + EPS) * rms_w
        return x_hat - jnp.mean(x_hat, axis=1, keepdims=True)
    x = _L0_xattn_ref(ctx_1024, ctx_1024, x, mask_Bx1x1xS2_if1, L0_xattn_wv, L0_xattn_wk, L0_xattn_wq, L0_xattn_w_out, L0_xattn_b_out, L0_xattn_g1, L0_xattn_beta1, L0_xattn_w_ff1, L0_xattn_b_ff1, L0_xattn_w_ff2, L0_xattn_b_ff2, L0_xattn_g2, L0_xattn_beta2)
    x = _L1_xattn_ref(ctx_1024, x, L1_xattn_Wq, L1_xattn_Wk, L1_xattn_Wv, L1_xattn_Wo, L1_xattn_gamma, L1_xattn_beta)
    x = _L2_xattn_ref(x, ctx_1024, L2_xattn_sa_wq, L2_xattn_sa_bq, L2_xattn_sa_wk, L2_xattn_sa_bk, L2_xattn_sa_wv, L2_xattn_sa_bv, L2_xattn_sa_wo, L2_xattn_sa_bo, L2_xattn_ca_wq, L2_xattn_ca_bq, L2_xattn_ca_wk, L2_xattn_ca_bk, L2_xattn_ca_wv, L2_xattn_ca_bv, L2_xattn_ca_wo, L2_xattn_ca_bo, L2_xattn_ln1_g, L2_xattn_ln1_b, L2_xattn_ln2_g, L2_xattn_ln2_b, L2_xattn_ln3_g, L2_xattn_ln3_b, L2_xattn_router_w, L2_xattn_router_b, L2_xattn_e_w1, L2_xattn_e_b1, L2_xattn_e_w2, L2_xattn_e_b2)
    x = _L3_xattn_ref(x, ctx_1024, ctx_1024, L3_xattn_Wq, L3_xattn_bq, L3_xattn_Wk, L3_xattn_bk, L3_xattn_Wv, L3_xattn_bv, L3_xattn_Wo, L3_xattn_bo, L3_xattn_Wg, L3_xattn_bg, L3_xattn_rms_w)
    return x

_drawn_inputs = setup_inputs


def setup_inputs(seed=0):
    import zlib

    import numpy as np

    out = dict(_drawn_inputs(seed))
    spreads = {'L0_xattn_b_out': (0.0, 0.1),
     'L0_xattn_g1': (1.0, 0.2),
     'L0_xattn_beta1': (0.0, 0.1),
     'L0_xattn_b_ff1': (0.0, 0.1),
     'L0_xattn_b_ff2': (0.0, 0.1),
     'L0_xattn_g2': (1.0, 0.2),
     'L0_xattn_beta2': (0.0, 0.1),
     'L1_xattn_gamma': (1.0, 0.2),
     'L1_xattn_beta': (0.0, 0.1),
     'L2_xattn_sa_bq': (0.0, 0.8),
     'L2_xattn_sa_bk': (0.0, 0.8),
     'L2_xattn_sa_bv': (0.0, 0.337),
     'L2_xattn_sa_bo': (0.0, 0.1),
     'L2_xattn_ca_bq': (0.0, 0.8),
     'L2_xattn_ca_bk': (0.0, 0.8),
     'L2_xattn_ca_bv': (0.0, 0.357),
     'L2_xattn_ca_bo': (0.0, 0.1),
     'L2_xattn_ln1_g': (1.0, 0.2),
     'L2_xattn_ln1_b': (0.0, 0.1),
     'L2_xattn_ln2_g': (1.0, 0.2),
     'L2_xattn_ln2_b': (0.0, 0.1),
     'L2_xattn_ln3_g': (1.0, 0.2),
     'L2_xattn_ln3_b': (0.0, 0.326),
     'L2_xattn_router_b': (0.0, 0.1),
     'L2_xattn_e_b1': (0.0, 0.37),
     'L2_xattn_e_b2': (0.0, 0.1),
     'L3_xattn_bq': (0.0, 0.8),
     'L3_xattn_bk': (0.0, 0.8),
     'L3_xattn_bv': (0.0, 0.8),
     'L3_xattn_bo': (0.0, 0.35),
     'L3_xattn_bg': (0.0, 0.1),
     'L3_xattn_rms_w': (1.0, 0.2)}
    factors = {'L0_xattn_wv': 4.678,
     'L0_xattn_wk': 8.0,
     'L0_xattn_wq': 8.0,
     'L0_xattn_w_out': 4.632,
     'L2_xattn_sa_wq': 8.0,
     'L2_xattn_sa_wk': 8.0,
     'L2_xattn_ca_wq': 8.0,
     'L2_xattn_ca_wk': 8.0,
     'L3_xattn_Wq': 8.0,
     'L3_xattn_Wk': 8.0,
     'L3_xattn_Wv': 4.306,
     'L3_xattn_Wo': 3.934}
    for name, (base, spread) in spreads.items():
        noise = np.random.default_rng([zlib.crc32(name.encode()), seed]).standard_normal(out[name].shape)
        drawn = base * np.exp(spread * noise) if base else spread * noise
        out[name] = jnp.asarray(drawn.astype(out[name].dtype))
    for name, factor in factors.items():
        out[name] = (out[name] * factor).astype(out[name].dtype)
    return out
```

```python
from contextlib import ExitStack

import concourse.bass as bass
from concourse import mybir
import numpy as np

F32 = mybir.dt.float32
BF16 = mybir.dt.bfloat16
I32 = mybir.dt.int32
U32 = mybir.dt.uint32
ALU = mybir.AluOpType
ACT = mybir.ActivationFunctionType
AX_X = mybir.AxisListType.X

P = 128
B = 32
D = 256
KC = D // P
H = 16
HD = D // H
HPC = H // KC
FF = 1024
FC = FF // P
E = 8
TOPK = 2
NS = 4
LAYERS = 4
TPI = LAYERS * NS
ITERS = B // NS
NT = LAYERS * B
SPAN = B * P + P
TILES = (B * P * TOPK + E * (P - 1)) // P
UNUSED = TILES - B * P * TOPK // P
W1_EARLY = E - 2
DUMMY = E * SPAN
NEG = -float(2 ** 66)
LN_EPS = 1e-5
RMS_EPS = 1e-6
WINDOW_HALF = 64

C_ID, C_TRI, C_HMASK, C_ECOL, C_IOTA, C_EBASE, C_TILE, C_END, C_CAUSAL, C_WIN, C_ALL = np.cumsum(
    [0, P, P, HPC, H, E, E, TILES, 0, P, P]).tolist()

COL_NAMES = ["L0_xattn_g1", "L0_xattn_beta1", "L0_xattn_g2", "L0_xattn_beta2", "L1_xattn_gamma", "L1_xattn_beta",
                 "L2_xattn_ln1_g", "L2_xattn_ln1_b", "L2_xattn_ln2_g", "L2_xattn_ln2_b", "L2_xattn_ln3_g",
                 "L2_xattn_ln3_b", "L2_xattn_sa_bq", "L2_xattn_sa_bk", "L2_xattn_ca_bq", "L2_xattn_ca_bk",
                 "L3_xattn_bq"]
COLS = len(COL_NAMES) * KC + FC + 1 + E * FC


def constants():
    c = np.zeros((P, C_ALL), np.float32)
    i, j = np.arange(P)[:, None], np.arange(P)[None, :]
    c[:, C_ID:C_TRI] = i == j
    c[:, C_CAUSAL:C_WIN] = np.where(j <= i, 0.0, NEG)
    c[:, C_WIN:C_ALL] = np.where((j >= i - WINDOW_HALF) & (j < i + WINDOW_HALF + 1), 0.0, NEG)
    c[:, C_TRI:C_HMASK] = i < j
    c[:, C_HMASK:C_ECOL] = np.arange(P)[:, None] // HD == np.arange(HPC)[None, :]
    c[:, C_ECOL:C_IOTA] = (i == np.arange(H)[None, :]) | (i == H + np.arange(H)[None, :])
    c[:, C_IOTA:C_EBASE] = np.arange(E)
    c[:, C_EBASE:C_TILE] = np.arange(E) * SPAN
    c[:, C_TILE:C_END] = np.arange(TILES)
    return c


def build(nc, a, out):
    with ExitStack() as ctx:
        program(nc, a, out, ctx)


def program(nc, a, out, ctx):
    def sb(name, shape, dt=F32):
        return ctx.enter_context(nc.sbuf_tensor(name, [P] + shape, dt))

    def psum(name, shape, dt=F32):
        return ctx.enter_context(nc.psum_tensor(name, [P] + shape, dt))

    def sem(name):
        return ctx.enter_context(nc.semaphore(name))

    def wait(eng, s, value):
        if isinstance(value, int) and value <= 0:
            return
        eng.wait_ge(s, value)

    def wait_apart(eng, sem_, value):
        wait(eng, sem_, value)
        if not isinstance(value, int):
            eng.sem_inc(waits_met, 1)

    x2_dram = nc.dram_tensor("x2_scratch", [B, P, D], F32).ap()
    sorted_x = nc.dram_tensor("sorted_x", [DUMMY + UNUSED * P, D], F32).ap()
    sorted_y = nc.dram_tensor("sorted_y", [TILES * P, D], F32).ap()

    ps_s = psum("ps_scores", [4, 512])
    ps_xv = psum("ps_xv", [512])
    ps_qk = psum("ps_qk", [512])
    ps_o = psum("ps_o", [4, P])
    ps_w = psum("ps_w", [512])

    w1 = sb("w1_experts", [E, KC, FF])
    arena = sb("arena", [16384])
    work = sb("work", [6144])

    class Carver:
        def __init__(self, t):
            self.t, self.pos = t, 0

        def __call__(self, shape, dt=F32):
            n = int(np.prod(shape))
            words = n if dt == F32 else (n + 1) // 2
            v = self.t[:, self.pos:self.pos + words]
            self.pos += words
            assert self.pos <= self.t.shape[1]
            if dt != F32:
                v = v.bitcast(dt)
            if len(shape) > 1:
                names = "abcd"[:len(shape)]
                v = v.rearrange(f"p ({' '.join(names)}) -> p {' '.join(names)}",
                                **{k: s for k, s in zip(names, shape)})
            return v

    cv = Carver(arena)
    bd = [cv([P]) for _ in range(3)]
    w_l0o = cv([KC, D])
    w_ff1, w_ff2 = cv([KC, FF]), cv([FC, D])
    w_attn = {l: [cv([KC, D]) for _ in range(4)] for l in (1, 2, 3)}
    row_names = ["L0_xattn_b_out", "L0_xattn_g1", "L0_xattn_beta1", "L0_xattn_b_ff2", "L0_xattn_g2",
                 "L0_xattn_beta2", "L1_xattn_gamma", "L1_xattn_beta", "L2_xattn_sa_bo", "L2_xattn_ln1_g",
                 "L2_xattn_ln1_b", "L2_xattn_ca_bo", "L2_xattn_ln2_g", "L2_xattn_ln2_b",
                 "L2_xattn_sa_bv", "L2_xattn_ca_bv"]
    rows = {}
    hT = cv([FC, P])
    n_l0_rows = 0
    for n in row_names[:3]:
        rows[n] = cv([D])
    assert cv.pos <= 16384
    rest_rows = row_names[3:]
    left = (16384 - cv.pos) // D
    for n in rest_rows[:left]:
        rows[n] = cv([D])
    for n in rest_rows[left:]:
        rows[n] = sb("row_" + n, [D])

    cv = Carver(work)
    qbd = [cv([KC, HPC, P]) for _ in range(2)]
    pt = cv([H, P])
    cv = Carver(work)
    xg = [cv([D]) for _ in range(2)]
    xgT = [cv([KC, P]) for _ in range(2)]
    hs = cv([FF])
    gT = cv([FC, P])
    ys = [cv([D]) for _ in range(2)]
    b2 = cv([E, D])
    w2 = arena[:, :].rearrange("p (e j n) -> p e (j n)", e=E, j=FC)
    w1f = w1[:].rearrange("p e c n -> p (e c n)")
    w2f = arena[:, :]
    cv = Carver(arena)
    yg = [[cv([D]) for _ in range(TOPK)] for _ in range(2)]
    x2l = [cv([D]) for _ in range(2)]
    at = [cv([D]) for _ in range(NS)]
    atT = cv([KC, P])
    gu, ge, gd, gq = cv([D]), cv([D]), cv([D]), cv([D])
    go, xh = cv([D]), [cv([D]) for _ in range(2)]
    fin = [cv([D]) for _ in range(2)]

    qT, kT = sb("qT", [KC, P]), [sb(f"kT{i}", [KC, P]) for i in range(2)]
    xT_all = sb("xT", [NS, KC, P])
    xT = [xT_all[:, i] for i in range(NS)]
    fxT = sb("fxT", [KC, P])
    oT, rs = sb("oT", [KC, P]), sb("rs", [KC, P])
    vz = [sb(f"vz{i}", [H // 2, 2, 2, HD]) for i in range(2)]
    xin = [sb(f"xin{i}", [D]) for i in range(2)]
    cin = [sb(f"cin{i}", [D]) for i in range(2)]
    cT = [sb(f"cT{i}", [KC, P]) for i in range(NS)]
    xn = [sb(f"xn{i}", [D]) for i in range(NS)]
    xr = [sb(f"xr{i}", [D]) for i in range(NS)]
    yb = [sb(f"yb{i}", [D]) for i in range(2)]
    nm = sb("nm", [H])
    mb = sb("mb", [P], BF16)
    mT = sb("mT", [P], BF16)

    consts = sb("consts", [C_END])
    ident = consts[:, C_ID:C_TRI]
    tri = consts[:, C_TRI:C_HMASK]
    hmask = consts[:, C_HMASK:C_ECOL]
    iota8 = consts[:, C_IOTA:C_EBASE]
    tile_iota = consts[:, C_TILE:C_END]
    ident_b, causal_b, win_b = sb("ident_b", [P], BF16), sb("causal_b", [P], BF16), sb("win_b", [P], BF16)
    ecol_b = sb("ecol_b", [H], BF16)
    one_b = sb("one_b", [1], BF16)
    one_f = sb("one_f", [1])
    mean_w = sb("mean_w", [1])
    neghalf = sb("neghalf", [1])
    onz = sb("onz", [2, 2, HD])
    kmask = [sb(f"kmask{i}", [P], BF16) for i in range(2)]
    kmi = [sb(f"kmi{i}", [P], I32) for i in range(2)]
    mask_cols = sb("mask_cols", [B], I32)
    kmcol = [sb(f"kmcol{i}", [1]) for i in range(2)]

    col_names = COL_NAMES
    cols_all = sb("cols_all", [COLS])
    n_c = len(COL_NAMES) * KC
    cols_t = cols_all[:, 0:n_c].rearrange("p (n c) -> p n c", c=KC)
    bff1, bk3 = cols_all[:, n_c:n_c + FC], cols_all[:, n_c + FC:n_c + FC + 1]
    b1T = cols_all[:, n_c + FC + 1:COLS]
    col = {n: cols_t[:, i, :] for i, n in enumerate(col_names)}
    b1s = [sb(f"b1s{i}", [FC]) for i in range(2)]

    w3q, w3o, w3g = sb("w3q", [KC, D]), sb("w3o", [KC, D]), sb("w3g", [2 * KC, D])
    w3kv_raw = sb("w3kv_raw", [2, KC, HD])
    w3k = sb("w3k", [KC, HPC, HD])
    row3 = {n: sb("row_" + n, [D]) for n in
            ("L3_xattn_bo", "L3_xattn_bg", "L3_xattn_rms_w", "L2_xattn_ln3_g", "L2_xattn_ln3_b")}
    bv3 = sb("bv3", [HD])
    rw, rb = sb("rw", [KC, E]), sb("rb", [E])
    lg, ex, pr, mx8, p8 = (sb(n, [E]) for n in ("lg", "ex", "pr", "mx8", "p8"))
    ix8 = sb("ix8", [E], U32)
    ixf = sb("ixf", [TOPK])
    oh = [sb(f"oh{i}", [TOPK, E]) for i in range(2)]
    ohm = [sb(f"ohm{i}", [E]) for i in range(2)]
    rsm = sb("rsm", [8])
    rk, junk, base = sb("rk", [E]), sb("junk", [E]), sb("base", [E])
    posf = sb("posf", [TOPK])
    posu = [sb(f"posu{i}", [TOPK], U32) for i in range(NS)]
    pos_all = sb("pos_all", [B * TOPK])
    shift = sb("shift", [E])
    w_all = sb("w_all", [B * TOPK])
    wsel = [sb(f"wsel{i}", [TOPK]) for i in range(2)]
    pidx = [[sb(f"pidx{i}{k}", [1], U32) for k in range(TOPK)] for i in range(2)]
    st6 = [sb(f"st6_{i}", [6]) for i in range(3)]
    mv = [sb(f"mv{i}", [2]) for i in range(3)]
    ve = [sb(f"ve{i}", [1]) for i in range(4)]
    rstd = [sb(f"rstd{i}", [1]) for i in range(4)]
    ssq = sb("ssq", [1])
    tt = sb("tt", [8, E])
    tti = sb("tti", [2, E], I32)
    tb = xT_all[:].rearrange("p a b c -> p (a b c)")[:, 0:5 * TILES].rearrange("p (a b) -> p a b", a=5)
    tbi = sb("tbi", [3, TILES], I32)
    tails = sb("tails", [E], I32)
    zeros = sb("zeros", [D])

    ld_const = sem("ld_const")
    ld_bd = sem("ld_bd")
    ld_bd_pool = sem("ld_bd_pool")
    ld_l0 = sem("ld_l0")
    ld_l1 = sem("ld_l1")
    ld_sa = sem("ld_sa")
    ld_ca = sem("ld_ca")
    ld_rows = sem("ld_rows")
    ld_cols = sem("ld_cols")
    ld_l3 = sem("ld_l3")
    ld_router = sem("ld_router")
    ld_w1 = sem("ld_w1")
    ld_experts = sem("ld_experts")
    ld_b2 = sem("ld_b2")
    waits_met = sem("waits_met")
    consts_ready = sem("consts_ready")
    bd_zero = sem("bd_zero")
    rows_ready = sem("rows_ready")
    mask_ready = sem("mask_ready")
    xt_psum = sem("xt_psum")
    xt_sb = sem("xt_sb")
    ctxt_sb = sem("ctxt_sb")
    qk_psum = sem("qk_psum")
    qk_sb = sem("qk_sb")
    v_psum = sem("v_psum")
    vz_ready = sem("vz_ready")
    qbd_ready = sem("qbd_ready")
    scores_ready = sem("scores_ready")
    maxima_part = sem("maxima_part")
    maxima_ready = sem("maxima_ready")
    mt_psum = sem("mt_psum")
    mt_sb = sem("mt_sb")
    st_ready = sem("st_ready")
    probs_ready = sem("probs_ready")
    av_ready = sem("av_ready")
    recip_ready = sem("recip_ready")
    ot_ready = sem("ot_ready")
    wo_ready = sem("wo_ready")
    ln_step = sem("ln_step")
    rstd_ready = sem("rstd_ready")
    xr_part = sem("xr_part")
    xr_ready = sem("xr_ready")
    xinit_ready = sem("xinit_ready")
    fxt_psum = sem("fxt_psum")
    fxt_sb = sem("fxt_sb")
    ff_up = sem("ff_up")
    ff_relu_a = sem("ff_relu_a")
    ff_relu_b = sem("ff_relu_b")
    ff_down = sem("ff_down")
    ffln_step = sem("ffln_step")
    ffrstd_ready = sem("ffrstd_ready")
    ffxr_part = sem("ffxr_part")
    ffxr_ready = sem("ffxr_ready")
    rt_logits = sem("rt_logits")
    rt_step = sem("rt_step")
    rt_exp = sem("rt_exp")
    rt_w_step = sem("rt_w_step")
    rt_rank = sem("rt_rank")
    rt2_step = sem("rt2_step")
    zero_filled = sem("zero_filled")
    tail_zeroed = sem("tail_zeroed")
    table_step = sem("table_step")
    b_xt_psum = sem("b_xt_psum")
    b_xt_sb = sem("b_xt_sb")
    b_b1 = sem("b_b1")
    b_up = sem("b_up")
    b_h_a = sem("b_h_a")
    b_h_b = sem("b_h_b")
    b_tr = sem("b_tr")
    b_gelu = sem("b_gelu")
    b_down = sem("b_down")
    b_y = sem("b_y")
    c_idx = sem("c_idx")
    c_ln = sem("c_ln")
    c_rstd = sem("c_rstd")
    c_xr_part = sem("c_xr_part")
    c_xr = sem("c_xr")
    c_at = sem("c_at")
    c_att_psum = sem("c_att_psum")
    c_att_sb = sem("c_att_sb")
    c_gate = sem("c_gate")
    c_gstep = sem("c_gstep")
    c_exp = sem("c_exp")
    c_rms = sem("c_rms")
    c_mean = sem("c_mean")
    c_fin = sem("c_fin")
    x_loaded = [sem(f"x_loaded{i}") for i in range(2)]
    ctx_loaded = [sem(f"ctx_loaded{i}") for i in range(2)]
    mask_loaded = [sem(f"mask_loaded{i}") for i in range(2)]
    x2_stored = [sem(f"x2_stored{i}") for i in range(NS)]
    scattered = [sem(f"scattered{i}") for i in range(NS)]
    b_loaded = [sem(f"b_loaded{i}") for i in range(2)]
    b_stored = [sem(f"b_stored{i}") for i in range(2)]
    c_loaded = [sem(f"c_loaded{i}") for i in range(2)]
    c_gathered = [sem(f"c_gathered{i}") for i in range(2)]
    c_out = [sem(f"c_out{i}") for i in range(2)]

    LAYER = [
        dict(scale=1.0 / 16.0, mask="keys", bq=None, bk=None, bv=None),
        dict(scale=0.25, mask=None, bq=None, bk=None, bv=None),
        dict(scale=0.25, mask=causal_b, bq="L2_xattn_sa_bq", bk="L2_xattn_sa_bk", bv="L2_xattn_sa_bv"),
        dict(scale=0.25, mask=None, bq="L2_xattn_ca_bq", bk="L2_xattn_ca_bk", bv="L2_xattn_ca_bv"),
        dict(scale=0.25, mask=win_b, bq="L3_xattn_bq", bk=None, bv=None),
    ]
    XT_GAIN = {1: ("L0_xattn_g2", "L0_xattn_beta2"), 2: ("L1_xattn_gamma", "L1_xattn_beta"),
               3: ("L2_xattn_ln1_g", "L2_xattn_ln1_b"), 4: ("L2_xattn_ln3_g", "L2_xattn_ln3_b")}
    XR_GAIN = {0: ("L0_xattn_g1", "L0_xattn_beta1"), 1: ("L1_xattn_gamma", "L1_xattn_beta"),
               2: ("L2_xattn_ln1_g", "L2_xattn_ln1_b"), 3: ("L2_xattn_ln2_g", "L2_xattn_ln2_b")}

    def slots(run, eng):
        def iteration(i, first, last):
            for tau in range(TPI + (3 if last else 0)):
                run(i, tau, i * TPI + tau, first, last)
        iteration(0, True, False)
        with eng.Fori(1, ITERS - 1) as i:
            iteration(i, False, False)
        iteration(ITERS - 1, False, True)

    def parts(i, tau, first, last):
        has = lambda d: not (first and tau + d < 0) and not (last and tau + d >= TPI)
        def at_(d):
            w = (tau + d) % TPI
            j = i + (tau + d) // TPI
            return dict(l=w // NS, s=w % NS, j=j, h=2 * j + (w % NS) // 2, t=i * TPI + tau + d, p=(tau + d) % 2, ok=has(d), d=d)
        return at_

    def cslots(run, eng):
        def iteration(j, first, last):
            for st in range(NS + (4 if last else 0)):
                run(j, st, j * NS + st, first, last)
        iteration(0, True, False)
        with eng.Fori(1, ITERS - 1) as j:
            iteration(j, False, False)
        iteration(ITERS - 1, False, True)

    def cparts(j, st, first, last):
        def at_(d):
            ok = not (first and st + d < 0) and not (last and st + d >= NS)
            jj = j + (st + d) // NS
            return dict(l=4, s=(st + d) % NS, j=jj, h=2 * jj + (st + d) % NS // 2, b=j * NS + st + d, t=NT + j * NS + st + d, p=(st + d) % 2, ok=ok)
        return at_

    def pairs(body, eng):
        body(0)
        with eng.Fori(1, (TILES - 1) // 2) as j:
            body(j)

    RT = 12

    def r_par(n):
        return n["s"] % 2

    def load_block(eng, m, n, h, done):
        eng.dma_start(bd[m][HD * h:HD * (h + 1), HD * h:HD * (h + 1)], a["L0_xattn_" + n]).then_inc(done, 16)

    block = ctx.enter_context(nc.Block())

    @block.sync
    def _(sp):
        sp.dma_start(consts[:], a["consts"][:, 0:C_END]).then_inc(ld_const, 16)
        sp.dma_start(pt[:, 0:2, :], a["consts"][:, C_CAUSAL:C_ALL].rearrange("p (a b) -> p a b", a=2)).then_inc(ld_const, 16)

        def load_x(i, st):
            u = b = i * NS + st
            wait_apart(sp, xt_psum, (i * TPI + st - 2 + 1) if st >= 2 else (i - 1) * TPI + st + 2 + 1)
            wait_apart(sp, xinit_ready, u - 1)
            wait_apart(sp, mask_ready, 3 * (u - 1))
            sp.dma_start(xin[st % 2][:], a["x"][bass.ds(b, 1)].rearrange("o s d -> s (o d)")).then_inc(x_loaded[st % 2], 16)
            sp.dma_start(cin[st % 2][:], a["ctx"][bass.ds(b, 1)].rearrange("o s d -> s (o d)")).then_inc(ctx_loaded[st % 2], 16)
            sp.dma_start(kmi[st % 2][0:1, :], a["mask"][bass.ds(b, 1)]).then_inc(mask_loaded[st % 2], 16)

        sp.dma_start(mask_cols[:], a["mask_cols"]).then_inc(ld_cols, 16)
        sp.dma_start(cols_all[:], a["cols"]).then_inc(ld_cols, 16)
        load_x(0, 0)
        kcp = lambda n: a[n].rearrange("(c p) n -> p c n", p=P)
        for n in row_names:
            sp.dma_start(rows[n], a[n].rearrange("(o d) -> o d", o=1).partition_broadcast(P)).then_inc(ld_rows, 16)
        load_x(0, 1)
        sp.dma_start(w_l0o, kcp("L0_xattn_w_out")).then_inc(ld_l0, 16)
        sp.dma_start(w_ff1, kcp("L0_xattn_w_ff1")).then_inc(ld_l0, 16)
        sp.dma_start(w_ff2, kcp("L0_xattn_w_ff2")).then_inc(ld_l0, 16)

        def late_loads(tau):
            if tau == 0:
                for j, n in enumerate(("Wq", "Wk", "Wv")):
                    for c in range(KC):
                        sp.dma_start(w_attn[1][j][:, c, :].rearrange("p (h d) -> p h d", h=H),
                                     a["L1_xattn_" + n].rearrange("h (c p) d -> p c h d", p=P)[:, c]).then_inc(ld_l1, 16)
                sp.dma_start(w_attn[1][3], kcp("L1_xattn_Wo")).then_inc(ld_l1, 16)
            if tau == 2:
                for l, pre, ld in ((2, "L2_xattn_sa_", ld_sa), (3, "L2_xattn_ca_", ld_ca)):
                    for j, n in enumerate(("wq", "wk", "wv", "wo")):
                        sp.dma_start(w_attn[l][j], kcp(pre + n)).then_inc(ld, 16)
                sp.dma_start(rw[:], kcp("L2_xattn_router_w")).then_inc(ld_router, 16)
                sp.dma_start(rb[:], a["L2_xattn_router_b"].rearrange("(o d) -> o d", o=1).partition_broadcast(P)).then_inc(ld_router, 16)
            if tau == 4:
                sp.dma_start(w3q[:], kcp("L3_xattn_Wq")).then_inc(ld_l3, 16)
                sp.dma_start(w3kv_raw[:, 0], kcp("L3_xattn_Wk")).then_inc(ld_l3, 16)
                sp.dma_start(w3kv_raw[:, 1], kcp("L3_xattn_Wv")).then_inc(ld_l3, 16)
                sp.dma_start(w3o[:], kcp("L3_xattn_Wo")).then_inc(ld_l3, 16)
                sp.dma_start(w3g[:], kcp("L3_xattn_Wg")).then_inc(ld_l3, 16)
                for n in row3:
                    sp.dma_start(row3[n][:], a[n].rearrange("(o d) -> o d", o=1).partition_broadcast(P)).then_inc(ld_l3, 16)
                sp.dma_start(bv3[:], a["L3_xattn_bv"].rearrange("(o d) -> o d", o=1).partition_broadcast(P)).then_inc(ld_l3, 16)
            if tau == 5:
                sp.wait_ge(consts_ready, 1)
                for k in range(UNUSED):
                    sp.dma_start(sorted_x[DUMMY + k * P:DUMMY + (k + 1) * P, :], zeros[:]).then_inc(zero_filled, 16)
            e = tau - 6
            if 0 <= e < W1_EARLY:
                sp.dma_start(w1[:, e], a["L2_xattn_e_w1"][e].rearrange("(c p) n -> p c n", p=P)).then_inc(ld_w1, 16)

        def run(i, tau, t, first, last):
            at_ = parts(i, tau, first, last)
            n = at_(2)
            if n["ok"] and n["l"] == 0 and not (first and tau + 2 == 0):
                load_x(n["j"], n["s"])
            if first:
                late_loads(tau)
            q = at_(-2)
            if q["ok"] and q["l"] == 3:
                b = q["j"] * NS + q["s"]
                wait_apart(sp, xr_ready, q["t"] + 1)
                sp.dma_start(x2_dram[bass.ds(b, 1)].rearrange("o s d -> s (o d)"), xr[q["s"]][:]).then_inc(x2_stored[q["s"]], 16)
        slots(run, sp)

        sp.wait_ge(av_ready, NT)
        sp.dma_start(b2, a["L2_xattn_e_b2"].rearrange("(o e) d -> o (e d)", o=1).partition_broadcast(P)
                     .rearrange("p o (e d) -> p (o e) d", e=E)).then_inc(ld_b2, 16)
        sp.wait_ge(table_step, TABLE_TAILS)
        for e in range(E):
            r = sp.value_load(tails[0:1, e:e + 1], min_val=0, max_val=DUMMY - P)
            sp.dma_start(sorted_x[bass.ds(r, P), :], zeros[:]).then_inc(tail_zeroed, 16)
        sp.wait_ge(tail_zeroed, 16 * E)
        sp.wait_ge(zero_filled, 16 * UNUSED)
        for st in range(NS):
            sp.wait_ge(scattered[st], 32 * ITERS)
        sp.wait_ge(table_step, TABLE_ALL)

        def load_tile(k, par):
            r = sp.value_load(tbi[0:1, 0, bass.ds(k, 1)], min_val=0, max_val=DUMMY + (UNUSED - 1) * P)
            sp.dma_start(xg[par], sorted_x[bass.ds(r, P), :]).then_inc(b_loaded[par], 16)

        def store_tile(k, par):
            wait_apart(sp, b_y, k + 1)
            sp.dma_start(sorted_y[bass.ds(k * P, P), :], ys[par]).then_inc(b_stored[par], 16)

        load_tile(0, 0)
        load_tile(1, 1)

        def tile_pair(j):
            wait_apart(sp, b_xt_psum, 2 * j + 1)
            load_tile(2 * j + 2, 0)
            store_tile(2 * j, 0)
            wait_apart(sp, b_xt_psum, 2 * j + 2)
            r = sp.value_load(tbi[0:1, 2, bass.ds(2 * j, 1)], min_val=0, max_val=DUMMY + (UNUSED - 1) * P)
            sp.dma_start(xg[1], sorted_x[bass.ds(r, P), :]).then_inc(b_loaded[1], 16)
            store_tile(2 * j + 1, 1)
        pairs(tile_pair, sp)
        store_tile(TILES - 1, 0)

        for par in range(2):
            sp.wait_ge(b_stored[par], 16 * ((TILES + 1 - par) // 2))
        for st in range(NS):
            sp.wait_ge(x2_stored[st], 16 * ITERS)

        def load_c(b, par):
            wait_apart(sp, c_ln, 6 * (b - 2) + 1)
            wait_apart(sp, xt_psum, NT + b - 1)
            sp.dma_start(x2l[par], x2_dram[bass.ds(b, 1)].rearrange("o s d -> s (o d)")).then_inc(c_loaded[par], 16)
            sp.dma_start(cin[par][:], a["ctx"][bass.ds(b, 1)].rearrange("o s d -> s (o d)")).then_inc(ctx_loaded[par], 16)

        def store_c(b, par):
            wait_apart(sp, c_fin, b + 1)
            sp.dma_start(out[bass.ds(b, 1)].rearrange("o s d -> s (o d)"), fin[par]).then_inc(c_out[par], 16)

        load_c(0, 0)
        load_c(1, 1)
        load_c(2, 0)

        def run_c(j, st, b, first, last):
            c = cparts(j, st, first, last)
            if c(3)["ok"]:
                load_c(c(3)["b"], c(3)["p"])
            if c(-4)["ok"]:
                store_c(c(-4)["b"], c(-4)["p"])
        cslots(run_c, sp)
        for par in range(2):
            sp.wait_ge(c_out[par], 16 * B // 2)

    @block.tensor
    def _(pe):
        mm = nc.tensor.matmul

        def transposes(ps, src, done):
            for c in range(KC):
                last = nc.tensor.transpose(ps[:, P * c:P * (c + 1)], src[:, P * c:P * (c + 1)], ident)
            if done is not None:
                last.then_inc(done, 1)

        def xt(n):
            t, l = n["t"], n["l"]
            wait(pe, vz_ready, t)
            if l == 0:
                u = n["j"] * NS + n["s"]
                wait(pe, ff_relu_b, n["j"] * NS)
                wait(pe, x_loaded[n["s"] % 2], 16 * (n["h"] + 1))
                wait(pe, ctx_loaded[n["s"] % 2], 16 * (n["h"] + 1))
                for c in range(KC):
                    nc.tensor.transpose(ps_xv[:, D + P * c:D + P * (c + 1)], cin[n["s"] % 2][:, P * c:P * (c + 1)], ident)
                transposes(ps_xv, xin[n["s"] % 2], xt_psum)
            elif l == 4:
                wait(pe, ctx_loaded[n["p"]], 16 * (B // 2 + n["h"] + 1))
                wait(pe, c_ln, 6 * (n["b"] + 1))
                wait(pe, c_att_sb, n["b"] - 3)
                for c in range(KC):
                    nc.tensor.transpose(ps_xv[:, D + P * c:D + P * (c + 1)], cin[n["p"]][:, P * c:P * (c + 1)], ident)
                transposes(ps_xv, xn[n["s"]], xt_psum)
            else:
                f = n["j"] * NS + n["s"]
                if l == 1:
                    wait(pe, ffln_step, 5 * (f + 1))
                    wait(pe, ff_relu_b, f + 1)
                else:
                    wait(pe, ln_step, 5 * (t - NS + 1))
                wait(pe, fxt_sb, xv_uses(n))
                transposes(ps_xv, xn[n["s"]], xt_psum)

        def xv_uses(n):
            j, l = n["j"], n["l"]
            if l == 1:
                return j * 2 * NS + n["s"] + 1 if n["s"] < NS else 0
            return j * 2 * NS + NS

        def project_v(n, first_l):
            t, l = n["t"], n["l"]
            if first_l:
                if l == 0:
                    pe.wait_ge(ld_bd, 16 * (HPC + HPC // 2))
                    pe.wait_ge(ld_bd_pool, 16 * (HPC + HPC // 2))
                elif l == 1:
                    pe.wait_ge(ld_l1, 16 * 7)
                elif l == 2:
                    pe.wait_ge(ld_sa, 16 * 4)
                elif l == 3:
                    pe.wait_ge(ld_ca, 16 * 4)
            kv = xT[n["s"]] if l == 2 else cT[n["s"]]
            wait(pe, xt_sb, t + 1)
            if l == 0:
                wait(pe, ctxt_sb, n["j"] * NS + n["s"] + 1)
                for c in range(KC):
                    last = mm(ps_xv[:, D + P * c:D + P * (c + 1)], kv[:, c, :], bd[2], start=True, stop=True)
            elif l == 4:
                wait(pe, ctxt_sb, B + n["b"] + 1)
                for c in range(KC):
                    last = mm(ps_xv[:, D:D + HD], kv[:, c, :], w3kv_raw[:, 1, c, :], start=c == 0, stop=c == KC - 1)
            else:
                for c in range(KC):
                    last = mm(ps_xv[:, D:2 * D], kv[:, c, :], w_attn[l][2][:, c, :], start=c == 0, stop=c == KC - 1)
            last.then_inc(v_psum, 1)

        def project_qk(n):
            t, l = n["t"], n["l"]
            src = xT[n["s"]]
            kv = src if l == 2 else cT[n["s"]]
            wait(pe, mt_sb, t)
            if l == 0:
                for m, (w, x_) in enumerate(((bd[0], src), (bd[1], kv))):
                    for c in range(KC):
                        last = mm(ps_qk[:, D * m + P * c:D * m + P * (c + 1)], w, x_[:, c, :], start=True, stop=True)
            else:
                wq = w3q if l == 4 else w_attn[l][0]
                for o in range(KC):
                    for c in range(KC):
                        mm(ps_qk[:, P * o:P * (o + 1)], wq[:, c, P * o:P * (o + 1)], src[:, c, :], start=c == 0, stop=c == KC - 1)
                if l == 4:
                    for c in range(KC):
                        last = mm(ps_qk[:, D:D + P], w3k[:, c].rearrange("p r d -> p (r d)"), kv[:, c, :], start=c == 0, stop=c == KC - 1)
                else:
                    for o in range(KC):
                        for c in range(KC):
                            last = mm(ps_qk[:, D + P * o:D + P * (o + 1)], w_attn[l][1][:, c, P * o:P * (o + 1)],
                                      kv[:, c, :], start=c == 0, stop=c == KC - 1)
            last.then_inc(qk_psum, 1)

        def scores(n):
            t, l, p = n["t"], n["l"], n["p"]
            mask = LAYER[l]["mask"]
            wait(pe, qk_sb, t + 1)
            wait(pe, qbd_ready, t + 1)
            if l == 0:
                wait(pe, mask_ready, 3 * (n["j"] * NS + n["s"] + 1))
            for g in range(4):
                c = g // 2
                if g % 2 == 0:
                    wait(pe, probs_ready, 4 * (t - 1) + g + 2)
                if mask == "keys":
                    mm(ps_s[:, g, :].rearrange("p (h k) -> p h k", h=4), one_b[:].to_broadcast([P, P]),
                       kmask[n["s"] % 2][:].unsqueeze(1).to_broadcast([P, 4, P]), start=True, stop=False)
                elif mask is not None:
                    mm(ps_s[:, g, :].rearrange("p (h k) -> p h k", h=4), ident_b[:],
                       mask[:].unsqueeze(1).to_broadcast([P, 4, P]), start=True, stop=False)
                k_ = kT[p][:, 0 if l == 4 else c, :].bitcast(BF16).rearrange("p (k two) -> p two k", two=2)[:, 1, :]
                for h in range(4):
                    q_ = qbd[p][:, c, (g % 2) * 4 + h, :].bitcast(BF16).rearrange("p (k two) -> p two k", two=2)[:, 1, :]
                    last = mm(ps_s[:, g, P * h:P * (h + 1)], q_, k_, start=mask is None, stop=mask is None or h == 3)
                if g % 2 == 1:
                    last.then_inc(scores_ready, 1)

        def scores_t(n, groups=range(4)):
            t, l, p = n["t"], n["l"], n["p"]
            mask = LAYER[l]["mask"]
            wait(pe, mt_sb, t + 1)
            for g in groups:
                c = g // 2
                mm(ps_s[:, g, :], kT[p][:, 0 if l == 4 else c, :],
                   qbd[p][:, c, (g % 2) * 4:(g % 2) * 4 + 4, :].rearrange("p h q -> p (h q)"), start=True, stop=False)
                if mask is not None and mask != "keys":
                    mm(ps_s[:, g, :].rearrange("p (h q) -> p h q", h=4), mask[:],
                       ident_b[:].unsqueeze(1).to_broadcast([P, 4, P]), start=False, stop=False)
                for h in range(4):
                    last = mm(ps_s[:, g, P * h:P * (h + 1)], ecol_b[:, 4 * g + h:4 * g + h + 1].to_broadcast([P, P]),
                              mT[:], start=False, stop=h == 3)
                last.then_inc(st_ready, 1)

        def maxima_t(n):
            t, l = n["t"], n["l"]
            wait(pe, maxima_ready, t + 1)
            wait(pe, qk_sb, t + 1)
            if l != 4 and n.get("ffwait") is not None:
                wait(pe, ff_relu_a, n["ffwait"])
            nc.tensor.transpose(ps_qk[:].bitcast(BF16)[:, 0:P], mb[:], ident_b[:]).then_inc(mt_psum, 1)

        def av(n):
            t, l, p = n["t"], n["l"], n["p"]
            wait(pe, probs_ready, 4 * (t + 1))
            wait(pe, vz_ready, t + 1)
            wait(pe, ot_ready, t)
            for kind in range(2):
                for c in range(KC):
                    for par in range(2):
                        for q in range(4):
                            h = c * HPC + 2 * q + par
                            w = vz[p][:, h // 2, par].rearrange("p a d -> p (a d)") if kind == 0 else onz[:, par].rearrange("p a d -> p (a d)")
                            last = mm(ps_o[32 * q:32 * q + 32, 2 * kind + c, :], w, pt[:, h, :],
                                      start=par == 0, stop=par == 1, tile_position=(0, 32 * q))
            last.then_inc(av_ready, 1)

        def wo(n, first_l, w_free):
            t, l = n["t"], n["l"]
            if first_l and l == 0:
                pe.wait_ge(ld_l0, 16 * 3)
            w = w_l0o if l == 0 else w3o if l == 4 else w_attn[l][3]
            wait(pe, ot_ready, t + 1)
            w_free()
            for c in range(KC):
                last = mm(ps_w[:, 0:D], oT[:, c, :], w[:, c, :], start=c == 0, stop=c == KC - 1)
            last.then_inc(wo_ready, 1)

        def fxt(n, ahead):
            t = n["t"]
            wait(pe, ln_step, 5 * (t + 1))
            if ahead:
                wait(pe, vz_ready, t + 4)
            transposes(ps_xv, xn[n["s"]], fxt_psum)

        def ff_hidden(n, u):
            t = n["t"]
            wait(pe, fxt_sb, u + 1)
            wait(pe, qk_sb, t + 4)
            for half, bank, done in ((0, ps_qk, 1), (1, ps_xv, 1)):
                for j in range(4):
                    for c in range(KC):
                        last = mm(bank[:, P * j:P * (j + 1)], w_ff1[:, c, P * (4 * half + j):P * (4 * half + j + 1)],
                                  fxT[:, c, :], start=c == 0, stop=c == KC - 1)
                last.then_inc(ff_up, 1)

        def ff_output(n):
            f = n["j"] * NS + n["s"]
            wait(pe, ln_step, 5 * (n["t"] + 1) + 1)
            for j in range(FC):
                if j == 0:
                    wait(pe, ff_relu_a, f + 1)
                if j == 4:
                    wait(pe, ff_relu_b, f + 1)
                last = mm(ps_w[:, 0:D], hT[:, j, :], w_ff2[:, j, :], start=j == 0, stop=j == FC - 1)
            last.then_inc(ff_down, 1)

        def router(n, u, tail):
            t = n["t"]
            wait(pe, fxt_sb, u + 1)
            wait(pe, rt2_step, 6 * (n["j"] * NS + n["s"] - 1) + 5)
            if not tail:
                wait(pe, ln_step, 5 * (t + 1) + 1)
            for c in range(KC):
                last = mm(ps_w[:, 0:E], fxT[:, c, :], rw[:, c, :], start=c == 0, stop=c == KC - 1)
            last.then_inc(rt_logits, 1)

        def rank(n, behind):
            r = n["j"] * NS + n["s"]
            wait(pe, rt_step, RT * (r + 1))
            wait(pe, ln_step, 5 * behind + 1)
            mm(ps_w[:, D:D + E], tri, ohm[r_par(n)][:], start=True, stop=True)
            mm(ps_w[:, D + E:D + 2 * E], one_f[:].to_broadcast([P, P]), ohm[r_par(n)][:], start=True, stop=True).then_inc(rt_rank, 1)

        def run(i, tau, t, first, last):
            at_ = parts(i, tau, first, last)
            now, prev, ff, rk_, nxt, old = at_(0), at_(-1), at_(-2), at_(-3), at_(1), at_(-4)
            u_of = lambda n: n["j"] * 2 * NS + (0 if n["l"] == 0 else NS) + n["s"]
            ff_behind = rk_["ok"] and rk_["l"] == 0
            if first and tau == 0:
                pe.wait_ge(ld_const, 32)
                pe.wait_ge(consts_ready, 1)
                xt(now)
                project_v(now, True)
                project_qk(now)
            if now["ok"]:
                scores(now)
            if ff_behind:
                if rk_["s"] == 0:
                    wait(pe, rt2_step, 6 * NS * rk_["j"])
                ff_output(rk_)
                now["ffwait"] = rk_["j"] * NS + rk_["s"] + 1
                maxima_t(now)
                av(prev)
                xt(nxt)
                scores_t(now, range(1))
                project_v(nxt, first and nxt["s"] == 0 and nxt["l"] > 0)
                project_qk(nxt)
                scores_t(now, range(1, 4))
            else:
                if rk_["ok"] and rk_["l"] == 3:
                    if first and rk_["s"] == 0:
                        pe.wait_ge(ld_router, 16 * 2)
                    router(rk_, u_of(rk_), tail=not ff["ok"])
                if nxt["ok"]:
                    xt(nxt)
                if prev["ok"]:
                    av(prev)
                if now["ok"]:
                    maxima_t(now)
                if nxt["ok"]:
                    project_v(nxt, first and nxt["s"] == 0 and nxt["l"] > 0)
                    project_qk(nxt)
                if now["ok"]:
                    scores_t(now)
            if ff["ok"] and ff["l"] in (0, 3):
                fxt(ff, nxt["ok"])
            if prev["ok"]:
                def w_free():
                    wait(pe, ln_step, 5 * (prev["t"] - 1) + 1)
                    if ff_behind:
                        wait(pe, ffln_step, 5 * (rk_["j"] * NS + rk_["s"]) + 1)
                    if rk_["ok"] and rk_["l"] == 3:
                        wait(pe, rt_step, RT * (rk_["j"] * NS + rk_["s"]) + 1)
                    if old["ok"] and old["l"] == 3:
                        wait(pe, rt2_step, 6 * (old["j"] * NS + old["s"]) + 5)
                wo(prev, first and tau - 1 == 0, w_free)
            if ff["ok"] and ff["l"] == 0:
                ff_hidden(ff, u_of(ff))
            if rk_["ok"] and rk_["l"] == 3:
                rank(rk_, prev["t"] if prev["ok"] else NT - 1)
        slots(run, pe)

        pe.wait_ge(ld_w1, 16 * W1_EARLY)
        pe.wait_ge(rt2_step, 6 * B)
        pe.wait_ge(table_step, TABLE_ALL)

        def tile_transposes(k, par, use):
            wait(pe, b_loaded[par], 16 * (use + 1))
            wait(pe, b_xt_sb, k)
            transposes(ps_xv, xg[par], b_xt_psum)

        def up(k, par):
            e = pe.value_load(tbi[0:1, 1, bass.ds(k, 1)], min_val=0, max_val=E - 1)
            wait(pe, ld_experts, e * 48 + 16)
            wait(pe, b_xt_sb, k + 1)
            wait(pe, b_h_a, k)
            wait(pe, b_h_b, k)
            for half in range(2):
                for c in range(KC):
                    last = mm(ps_s[:, half, :], xgT[par][:, c, :],
                              w1f[:, bass.ds(e * (KC * FF) + (c * FF + 512 * half), 512)], start=c == 0, stop=c == KC - 1)
                last.then_inc(b_up, 1)
            return e

        def down(k):
            e = pe.value_load(tbi[0:1, 1, bass.ds(k, 1)], min_val=0, max_val=E - 1)
            wait(pe, ld_experts, e * 48 + 16)
            wait(pe, b_gelu, k + 1)
            wait(pe, b_y, k)
            for j in range(FC):
                last = mm(ps_w[:, 0:D], gT[:, j, :], w2f[:, bass.ds(e * (FC * D) + j * D, D)], start=j == 0, stop=j == FC - 1)
            last.then_inc(b_down, 1)

        def hidden_transposes(k):
            wait(pe, b_gelu, k)
            wait(pe, b_h_a, k + 1)
            for j in range(4):
                nc.tensor.transpose(ps_s[:, 2, P * j:P * (j + 1)], hs[:, P * j:P * (j + 1)], ident)
            wait(pe, b_h_b, k + 1)
            for j in range(4):
                last = nc.tensor.transpose(ps_s[:, 3, P * j:P * (j + 1)], hs[:, P * (4 + j):P * (5 + j)], ident)
            last.then_inc(b_tr, 1)

        tile_transposes(0, 0, 0)
        up(0, 0)
        hidden_transposes(0)
        tile_transposes(1, 1, 0)

        def tile_pair(j):
            for d in (1, 2):
                k = 2 * j + d
                up(k, d % 2)
                down(k - 1)
                tile_transposes(k + 1, (d + 1) % 2, j + 1)
                hidden_transposes(k)
        pairs(tile_pair, pe)
        down(TILES - 1)

        def gate(n):
            b = n["b"]
            wait(pe, c_at, b + 1)
            wait(pe, xt_sb, min_t(n, 3))
            wait(pe, vz_ready, min_t(n, 3))
            wait(pe, c_xr, b + 1)
            transposes(ps_xv, at[n["s"]], c_att_psum)
            wait(pe, c_att_sb, b + 1)
            wait(pe, c_at, min_b(n, 2))
            wait(pe, c_fin, b - 1)
            for c in range(KC):
                mm(ps_w[:, 0:D], atT[:, c, :], w3g[:, c, :], start=c == 0, stop=False)
            for c in range(KC):
                last = mm(ps_w[:, 0:D], xT[n["s"]][:, c, :], w3g[:, KC + c, :], start=False, stop=c == KC - 1)
            last.then_inc(c_gate, 1)

        def min_t(n, d):
            return n["t"] + d + 1 if n["ahead"] >= d else n["t"] + n["ahead"] + 1

        def min_b(n, d):
            return n["b"] + d if n["ahead"] >= d - 1 else n["b"] + n["ahead"] + 1

        def mean(n):
            b = n["b"]
            wait(pe, c_rms, 5 * (b + 1))
            wait(pe, c_gstep, 9 * (b + 1) + 1 if n["ahead"] else 9 * b + 1)
            mm(ps_w[:, D:2 * D], mean_w[:].to_broadcast([P, P]), xh[n["p"]], start=True, stop=True).then_inc(c_mean, 1)

        pe.wait_ge(ld_l3, 16 * 11)

        def run_c(j, st, b, first, last):
            c = cparts(j, st, first, last)
            now, prev, g_, m_, nxt = c(0), c(-1), c(-2), c(-4), c(1)
            m_["ahead"] = not (last and st == NS + 3)
            g_["ahead"] = 99 if not last else (NS - 1) - (st - 2)
            if first and st == 0:
                pe.wait_ge(b_y, TILES)
                xt(now)
                project_v(now, False)
                project_qk(now)
            if now["ok"]:
                scores(now)
            if nxt["ok"]:
                xt(nxt)
            if prev["ok"]:
                av(prev)
            if now["ok"]:
                maxima_t(now)
            if nxt["ok"]:
                project_v(nxt, False)
                project_qk(nxt)
            if now["ok"]:
                scores_t(now)
            if m_["ok"]:
                mean(m_)
            if prev["ok"]:
                wo(prev, False, lambda: wait(pe, c_gstep, 9 * (prev["b"] - 2) + 1))
            if g_["ok"]:
                gate(g_)
        cslots(run_c, pe)

    @block.scalar
    def _(act):
        act.wait_ge(bd_zero, 1)
        for h in range(HPC):
            load_block(act, 1, "wk", h, ld_bd)
        for h in range(HPC // 2):
            load_block(act, 0, "wq", h, ld_bd)

        def xt_evac(n):
            t, l = n["t"], n["l"]
            wait(act, xt_psum, t + 1)
            src = ps_xv[:, 0:D].rearrange("p (c q) -> p c q", c=KC)
            if l in (0, 4):
                nc.scalar.copy(cT[n["s"]][:], ps_xv[:, D:2 * D].rearrange("p (c q) -> p c q", c=KC)).then_inc(ctxt_sb, 1)
            if l == 0:
                nc.scalar.copy(xT[n["s"]], src).then_inc(xt_sb, 1)
                return
            g, b_ = XT_GAIN[l]
            for c in range(KC):
                last = nc.scalar.activation(xT[n["s"]][:, c, :], src[:, c, :], ACT.Identity, bias=col[b_][:, c:c + 1], scale=col[g][:, c:c + 1])
            last.then_inc(xt_sb, 1)

        def qk_evac(n):
            t, l, p = n["t"], n["l"], n["p"]
            wait(act, qk_psum, t + 1)
            wait(act, qbd_ready, t)
            L = LAYER[l]
            srcs = ps_qk[:].rearrange("p (m c q) -> p m c q", m=2, c=KC)
            for m, dst, bias in ((0, qT, L["bq"]), (1, kT[p], L["bk"])):
                if l == 4 and m == 1:
                    last = nc.scalar.activation(dst[:, 0, :], srcs[:, 1, 0], ACT.Identity, bias=bk3[:])
                elif bias is None:
                    last = nc.scalar.copy(dst[:], srcs[:, m])
                else:
                    for c in range(KC):
                        last = nc.scalar.activation(dst[:, c, :], srcs[:, m, c], ACT.Identity, bias=col[bias][:, c:c + 1])
            last.then_inc(qk_sb, 1)

        def mt_evac(n):
            wait(act, mt_psum, n["t"] + 1)
            nc.scalar.copy(mT[:], ps_qk[:].bitcast(BF16)[:, 0:P]).then_inc(mt_sb, 1)

        def exps(n, groups=range(4)):
            t, l = n["t"], n["l"]
            for g in groups:
                wait(act, st_ready, 4 * t + g + 1)
                bias = kmcol[n["s"] % 2][:] if l == 0 else 0.0
                nc.scalar.activation(pt[:, 4 * g:4 * g + 4, :].rearrange("p h q -> p (h q)"), ps_s[:, g, :], ACT.Exp,
                                     bias=bias, scale=LAYER[l]["scale"]).then_inc(probs_ready, 1)

        def fxt_evac(n, u):
            wait(act, fxt_psum, u + 1)
            g, b_ = XR_GAIN[n["l"]]
            for c in range(KC):
                last = nc.scalar.activation(fxT[:, c, :], ps_xv[:, P * c:P * (c + 1)], ACT.Identity, bias=col[b_][:, c:c + 1], scale=col[g][:, c:c + 1])
            last.then_inc(fxt_sb, 1)

        def relu_a(n):
            f = n["j"] * NS + n["s"]
            wait(act, ff_up, 2 * f + 1)
            for j in range(4):
                last = nc.scalar.activation(hT[:, j, :], ps_qk[:, P * j:P * (j + 1)], ACT.Relu, bias=bff1[:, j:j + 1])
            last.then_inc(ff_relu_a, 1)

        def router_exps(n):
            r = n["j"] * NS + n["s"]
            wait(act, rt_step, RT * r + 3)
            nc.scalar.activation(ex[:], lg[:], ACT.Exp, bias=rsm[:, 0:1], accum_out=rsm[:, 1:2]).then_inc(rt_exp, 1)

        def router_weight(n):
            r = n["j"] * NS + n["s"]
            wait(act, rt_step, RT * r + 7)
            nc.scalar.activation(rsm[:, 4:5], rsm[:, 3:4], ACT.Exp).then_inc(rt_exp, 1)

        def run(i, tau, t, first, last):
            at_ = parts(i, tau, first, last)
            now, ff, rk_, nxt = at_(0), at_(-2), at_(-3), at_(1)
            u_of = lambda n: n["j"] * 2 * NS + (0 if n["l"] == 0 else NS) + n["s"]
            if first and tau == 0:
                xt_evac(now)
                act.wait_ge(ld_cols, 32)
                qk_evac(now)
            if now["ok"] and now["l"] == 0:
                wait(act, mask_ready, 3 * (now["j"] * NS + now["s"] + 1))
            if rk_["ok"] and rk_["l"] == 0:
                mt_evac(now)
                xt_evac(nxt)
                exps(now, range(1))
                qk_evac(nxt)
                exps(now, range(1, 4))
            else:
                if nxt["ok"]:
                    xt_evac(nxt)
                if now["ok"]:
                    mt_evac(now)
                if nxt["ok"]:
                    qk_evac(nxt)
                routing = rk_["ok"] and rk_["l"] == 3
                if now["ok"]:
                    exps(now, range(1))
                if routing:
                    router_exps(rk_)
                if now["ok"]:
                    exps(now, range(1, 3))
                if routing:
                    router_weight(rk_)
                if now["ok"]:
                    exps(now, range(3, 4))
            if ff["ok"] and ff["l"] in (0, 3):
                fxt_evac(ff, u_of(ff))
                if ff["l"] == 0:
                    relu_a(ff)
        slots(run, act)

        def tile(k, par):
            wait(act, b_up, 2 * k + 1)
            wait(act, b_tr, k)
            nc.scalar.copy(hs[:, 0:512], ps_s[:, 0, :]).then_inc(b_h_a, 1)
            wait(act, b_tr, k + 1)
            wait(act, b_b1, k + 1)
            wait(act, b_down, k)
            for j in range(FC):
                last = nc.scalar.activation(gT[:, j, :], ps_s[:, 2 + j // 4, P * (j % 4):P * (j % 4 + 1)], ACT.Gelu,
                                            bias=b1s[par][:, j:j + 1])
            last.then_inc(b_gelu, 1)

        tile(0, 0)

        def tile_pair(j):
            for d in (1, 2):
                tile(2 * j + d, d % 2)
        pairs(tile_pair, act)

        def run_c(j, st, b, first, last):
            c = cparts(j, st, first, last)
            now, g_, h_, nxt = c(0), c(-2), c(-3), c(1)
            if first and st == 0:
                xt_evac(now)
                qk_evac(now)
            if nxt["ok"]:
                xt_evac(nxt)
            if now["ok"]:
                mt_evac(now)
            if nxt["ok"]:
                qk_evac(nxt)
            if h_["ok"]:
                wait(act, c_gstep, 9 * h_["b"] + 1)
                nc.scalar.activation(ge, gu, ACT.Exp, scale=-1.0).then_inc(c_exp, 1)
            if now["ok"]:
                exps(now)
            if g_["ok"]:
                wait(act, c_att_psum, g_["b"] + 1)
                nc.scalar.copy(atT, ps_xv[:, 0:D].rearrange("p (c q) -> p c q", c=KC)).then_inc(c_att_sb, 1)
        cslots(run_c, act)

    @block.vector
    def _(dve):
        V = nc.vector

        V.memset(bd[0], 0.0)
        V.memset(bd[1], 0.0)
        V.memset(bd[2], 0.0).then_inc(bd_zero, 1)
        V.memset(one_b[:], 1.0)
        V.memset(one_f[:], 1.0)
        V.memset(mean_w[:], 1.0 / P)
        V.memset(neghalf[:], -0.5)
        V.memset(zeros[:], 0.0)
        V.memset(mb[:], 0.0)
        for i in range(2):
            V.memset(vz[i][:], 0.0)
            V.memset(kmask[i][:], 0.0)
        V.memset(onz[:, 0, 1, :], 0.0)
        V.memset(onz[:, 1, 0, :], 0.0)
        V.memset(onz[:, 0, 0, :], 1.0)
        V.memset(onz[:, 1, 1, :], 1.0)
        dve.wait_ge(ld_const, 32)
        V.tensor_copy(ident_b[:], ident)
        V.tensor_copy(causal_b[:], pt[:, 0, :])
        V.tensor_copy(win_b[:], pt[:, 1, :])
        V.tensor_copy(base[:], consts[:, C_EBASE:C_TILE])
        V.tensor_copy(ecol_b[:], consts[:, C_ECOL:C_IOTA]).then_inc(consts_ready, 1)
        dve.wait_ge(consts_ready, 1)

        def vz_evac(n):
            t, l, p = n["t"], n["l"], n["p"]
            wait(dve, v_psum, t + 1)
            if l == 4:
                src = ps_xv[:, D:D + HD]
                for par in range(2):
                    last = V.tensor_tensor(vz[p][:, :, par, par, :], src.unsqueeze(1).to_broadcast([P, H // 2, HD]),
                                           bv3[:].unsqueeze(1).to_broadcast([P, H // 2, HD]), ALU.add)
            else:
                src = ps_xv[:, D:2 * D].rearrange("p (h two d) -> p h two d", two=2, d=HD)
                bv = LAYER[l]["bv"]
                for par in range(2):
                    if bv is None:
                        last = V.tensor_copy(vz[p][:, :, par, par, :], src[:, :, par, :])
                    else:
                        last = V.tensor_tensor(vz[p][:, :, par, par, :], src[:, :, par, :],
                                               rows[bv].rearrange("p (h two d) -> p h two d", two=2, d=HD)[:, :, par, :], ALU.add)
            last.then_inc(vz_ready, 1)

        def mask_prep(n):
            b = n["j"] * NS + n["s"]
            par = n["s"] % 2
            wait(dve, mask_loaded[par], 16 * (n["h"] + 1))
            wait(dve, probs_ready, 4 * (n["t"] - 2 + 1) if n["s"] >= 2 else 4 * (n["t"] - TPI + 2 + 1))
            V.tensor_scalar(kmask[par][0:1, :], kmi[par][0:1, :], 0.0, NEG, ALU.is_equal, ALU.mult).then_inc(mask_ready, 1)
            V.tensor_scalar(kmcol[par][:], mask_cols[:, bass.ds(b, 1)], 0.0, NEG * LAYER[0]["scale"], ALU.is_equal, ALU.mult).then_inc(mask_ready, 2)

        def maxima(n):
            t = n["t"]
            for half in range(2):
                wait(dve, scores_ready, 2 * t + half + 1)
                V.tensor_reduce(nm[:, 8 * half:8 * half + 8],
                                ps_s[:, 2 * half:2 * half + 2, :].rearrange("p g (h k) -> p (g h) k", h=4),
                                AX_X, ALU.max, negate=True).then_inc(maxima_part, 1)
            dve.wait_ge(maxima_part, 4 * t + 2)
            V.tensor_copy(mb[:, 0:H], nm[:]).then_inc(maxima_part, 1)
            dve.wait_ge(maxima_part, 4 * t + 3)
            V.tensor_tensor(mb[:, H:2 * H], nm[:], mb[:, 0:H], ALU.subtract).then_inc(maxima_part, 1)
            dve.wait_ge(maxima_part, 4 * t + 4)
            V.tensor_copy(mb[:, 2 * H:2 * H + 1], zeros[:, 0:1]).then_inc(maxima_ready, 1)

        def normalise(n):
            t = n["t"]
            wait(dve, av_ready, t + 1)
            V.reciprocal(rs[:], ps_o[:, 2:4, :]).then_inc(recip_ready, 1)
            dve.wait_ge(recip_ready, t + 1)
            V.tensor_tensor(oT[:], ps_o[:, 0:2, :], rs[:], ALU.mult).then_inc(ot_ready, 1)

        def norm_stats(kind, y, step, n_):
            wait_apart(dve, step, 5 * n_ + 1)
            V.bn_stats(st6[kind][:], y).then_inc(step, 1)
            wait_apart(dve, step, 5 * n_ + 2)
            V.bn_aggr(mv[kind][:], st6[kind][:]).then_inc(step, 1)
            dve.wait_ge(step, 5 * n_ + 3)
            V.tensor_scalar_add(ve[kind][:], mv[kind][:, 1:2], LN_EPS).then_inc(step, 1)

        def norm_apply(kind, dst, y, step, rs_sem, n_):
            wait(dve, rs_sem, n_ + 1)
            V.tensor_scalar(dst, y, mv[kind][:, 0:1], rstd[kind][:], ALU.subtract, ALU.mult).then_inc(step, 1)

        def relu_b(n):
            f = n["j"] * NS + n["s"]
            wait(dve, ff_up, 2 * f + 2)
            for j in range(4):
                last = V.tensor_scalar(hT[:, 4 + j, :], ps_xv[:, P * j:P * (j + 1)], bff1[:, 4 + j:5 + j], 0.0, ALU.add, ALU.max)
            last.then_inc(ff_relu_b, 1)

        def router(n):
            r = n["j"] * NS + n["s"]
            q = r_par(n)
            k = [0]

            def link(ins, to_next=True):
                ins.then_inc(rt_step, 1)
                k[0] += 1
                wait_apart(dve, rt_step, RT * r + k[0])
            wait(dve, rt_logits, r + 1)
            link(V.tensor_tensor(lg[:], ps_w[:, 0:E], rb[:], ALU.add))
            link(V.max(mx8[:], lg[:]))
            link(V.tensor_scalar_mul(rsm[:, 0:1], mx8[:, 0:1], -1.0))
            wait(dve, rt_exp, 2 * r + 1)
            link(V.reciprocal(rsm[:, 2:3], rsm[:, 1:2]))
            link(V.tensor_scalar_mul(pr[:], ex[:], rsm[:, 2:3]))
            link(V.max(p8[:], pr[:]))
            link(V.tensor_tensor(rsm[:, 3:4], p8[:, 1:2], p8[:, 0:1], ALU.subtract))
            link(V.max_index(ix8[:], p8[:], pr[:]))
            link(V.tensor_copy(ixf[:], ix8[:, 0:TOPK]))
            for k_ in range(TOPK):
                ins = V.tensor_scalar(oh[q][:, k_, :], iota8, ixf[:, k_:k_ + 1], None, ALU.is_equal)
                link(ins)
            link(V.tensor_tensor(ohm[q][:], oh[q][:, 0, :], oh[q][:, 1, :], ALU.add))
            assert k[0] == RT
            wait(dve, rt_exp, 2 * r + 2)
            V.tensor_scalar_add(rsm[:, 5:6], rsm[:, 4:5], 1.0).then_inc(rt_w_step, 1)
            dve.wait_ge(rt_w_step, 3 * r + 1)
            V.reciprocal(rsm[:, 6:7], rsm[:, 5:6]).then_inc(rt_w_step, 1)
            dve.wait_ge(rt_w_step, 3 * r + 2)
            V.tensor_copy(w_all[:, bass.ds(r * TOPK, 1)], rsm[:, 6:7])
            V.tensor_tensor(w_all[:, bass.ds(r * TOPK + 1, 1)], rsm[:, 4:5], rsm[:, 6:7], ALU.mult).then_inc(rt_w_step, 1)

        def positions(n):
            r = n["j"] * NS + n["s"]
            q = r_par(n)
            wait(dve, rt_rank, r + 1)
            V.tensor_tensor(rk[:], ps_w[:, D:D + E], base[:], ALU.add).then_inc(rt2_step, 1)
            dve.wait_ge(rt2_step, 6 * r + 1)
            for k_ in range(TOPK):
                V.scalar_tensor_tensor(junk[:], oh[q][:, k_, :], 1.0, rk[:], ALU.mult, ALU.mult,
                                       accum_out=posf[:, k_:k_ + 1]).then_inc(rt2_step, 1)
                dve.wait_ge(rt2_step, 6 * r + 2 + k_)
            wait(dve, xinit_ready, r + 1)
            V.tensor_copy(posu[n["s"]][:], posf[:]).then_inc(rt2_step, 1)
            V.tensor_tensor(base[:], base[:], ps_w[:, D + E:D + 2 * E], ALU.add).then_inc(rt2_step, 1)
            V.tensor_copy(pos_all[:, bass.ds(r * TOPK, TOPK)], posf[:]).then_inc(rt2_step, 1)

        def run(i, tau, t, first, last):
            at_ = parts(i, tau, first, last)
            now, prev, ff, rk_, nxt = at_(0), at_(-1), at_(-2), at_(-3), at_(1)
            if first and tau == 0:
                vz_evac(now)
                dve.wait_ge(ld_cols, 32)
                mask_prep(now)
                dve.wait_ge(ld_rows, 16 * len(row_names))
                for dst, add in (("L0_xattn_beta1", "L0_xattn_b_ff2"), ("L1_xattn_beta", "L2_xattn_sa_bo"), ("L2_xattn_ln1_b", "L2_xattn_ca_bo")):
                    last_ = V.tensor_tensor(rows[dst], rows[dst], rows[add], ALU.add)
                last_.then_inc(rows_ready, 1)
            routing = rk_["ok"] and rk_["l"] == 3
            if now["ok"]:
                maxima(now)
            if ff["ok"]:
                norm_stats(0, yb[0][:], ln_step, ff["t"])
            if rk_["ok"] and rk_["l"] == 0:
                f = rk_["j"] * NS + rk_["s"]
                wait(dve, ff_down, f + 1)
                wait(dve, xr_ready, rk_["t"] + 1)
                V.tensor_tensor(yb[1][:], ps_w[:, 0:D], xr[rk_["s"]][:], ALU.add).then_inc(ffln_step, 1)
                norm_stats(1, yb[1][:], ffln_step, f)
                norm_apply(1, xn[rk_["s"]][:], yb[1][:], ffln_step, ffrstd_ready, f)
            if prev["ok"]:
                normalise(prev)
            if ff["ok"]:
                norm_apply(0, xn[ff["s"]][:], yb[0][:], ln_step, rstd_ready, ff["t"])
            if nxt["ok"]:
                if nxt["l"] == 0:
                    mask_prep(nxt)
                vz_evac(nxt)
            if routing:
                if first and rk_["s"] == 0:
                    dve.wait_ge(ld_router, 16 * 2)
                router(rk_)
            if prev["ok"]:
                wait(dve, wo_ready, prev["t"] + 1)
                residual_ready(prev)
                wait(dve, ln_step, 5 * prev["t"])
                V.tensor_tensor(yb[0][:], ps_w[:, 0:D], xr[prev["s"]][:], ALU.add).then_inc(ln_step, 1)
            if routing:
                positions(rk_)
            if ff["ok"] and ff["l"] == 0:
                relu_b(ff)

        def residual_ready(n):
            l, j = n["l"], n["j"]
            f = j * NS + n["s"]
            if l == 0:
                wait(dve, xinit_ready, f + 1)
            elif l == 1:
                wait(dve, ffxr_ready, f + 1)
            else:
                wait(dve, xr_ready, n["t"] - NS + 1)
        slots(run, dve)

        step = [0]

        def tlink(ins):
            ins.then_inc(table_step, 1)
            step[0] += 1
            dve.wait_ge(table_step, step[0])
        dve.wait_ge(rt2_step, 6 * B)
        tlink(V.tensor_copy(tails[:], base[:]))
        assert step[0] == TABLE_TAILS
        cnt, incl, excl, n_t = tt[:, 0], tt[:, 1], tt[:, 2], tt[:, 3]
        tlink(V.tensor_tensor(cnt, base[:], consts[:, C_EBASE:C_TILE], ALU.subtract))
        tlink(V.tensor_scalar_add(tti[:, 0], cnt, float(P - 1)))
        tlink(V.tensor_scalar(tti[:, 1], tti[:, 0], 7, None, ALU.arith_shift_right))
        tlink(V.tensor_copy(n_t, tti[:, 1]))
        tlink(V.tensor_scalar(tt[:, 4], n_t, 0.0, 1.0, ALU.mult, ALU.add))
        tlink(V.tensor_tensor_scan(incl, tt[:, 4], n_t, 0.0, ALU.mult, ALU.add))
        eid, ex_, row_, addr = tb[:, 0], tb[:, 1], tb[:, 2], tb[:, 3]
        tlink(V.memset(tb[:, 0:2], 0.0))
        for e in range(E):
            tlink(V.tensor_scalar(tb[:, 4], tile_iota, incl[:, e:e + 1], None, ALU.is_ge))
            tlink(V.tensor_tensor(eid, eid, tb[:, 4], ALU.add))
            tlink(V.scalar_tensor_tensor(ex_, tb[:, 4], n_t[:, e:e + 1], ex_, ALU.mult, ALU.add))
        tlink(V.tensor_tensor(row_, tile_iota, ex_, ALU.subtract))
        tlink(V.tensor_scalar_mul(row_, row_, float(P)))
        tlink(V.scalar_tensor_tensor(addr, eid, float(SPAN), row_, ALU.mult, ALU.add))
        tlink(V.tensor_copy(tbi[:, 0], addr))
        tlink(V.tensor_scalar_min(tbi[:, 1], eid, float(E - 1)))
        tlink(V.tensor_copy(tbi[:, 2, TILES - 3:TILES], tbi[:, 0, TILES - 1:TILES].to_broadcast([P, 3])))
        tlink(V.tensor_copy(tbi[:, 2, 0:TILES - 3], tbi[:, 0, 3:TILES]))
        assert step[0] == TABLE_ALL
        tlink(V.tensor_scalar(shift[:], n_t, float(P), -float(SPAN), ALU.mult, ALU.add))
        pos_in = yb[1][:, 0:B * TOPK]
        moved = yb[1][:, P:P + B * TOPK]
        tlink(V.tensor_copy(pos_in, pos_all[:]))
        for e in range(1, E):
            tlink(V.tensor_scalar(moved, pos_in, float(e * SPAN), shift[:, e - 1:e], ALU.is_ge, ALU.mult))
            tlink(V.tensor_tensor(pos_all[:], pos_all[:], moved, ALU.add))

        dve.wait_ge(ld_b2, 16)

        def tile_evac(k, par):
            wait(dve, b_xt_psum, k + 1)
            V.tensor_copy(xgT[par], ps_xv[:, 0:D].rearrange("p (c q) -> p c q", c=KC)).then_inc(b_xt_sb, 1)

        def tile_h(k, par):
            e = dve.value_load(tbi[0:1, 1, bass.ds(k, 1)], min_val=0, max_val=E - 1)
            V.tensor_copy(b1s[par][:], b1T[:, bass.ds(e * FC, FC)]).then_inc(b_b1, 1)
            wait(dve, b_up, 2 * k + 2)
            wait(dve, b_tr, k)
            V.tensor_copy(hs[:, 512:1024], ps_s[:, 1, :]).then_inc(b_h_b, 1)

        def tile_y(k, par, use):
            e = dve.value_load(tbi[0:1, 1, bass.ds(k, 1)], min_val=0, max_val=E - 1)
            wait(dve, b_down, k + 1)
            wait(dve, b_stored[par], 16 * use)
            V.tensor_tensor(ys[par], ps_w[:, 0:D], b2.rearrange("p e d -> p (e d)")[:, bass.ds(e * D, D)], ALU.add).then_inc(b_y, 1)

        tile_evac(0, 0)
        tile_h(0, 0)
        tile_evac(1, 1)

        def tile_pair(j):
            for d in (1, 2):
                k = 2 * j + d
                tile_h(k, d % 2)
                tile_y(k - 1, (d - 1) % 2, j)
                tile_evac(k + 1, (d + 1) % 2)
        pairs(tile_pair, dve)
        tile_y(TILES - 1, 0, (TILES - 1) // 2)

        dve.wait_ge(ld_l3, 16 * 11)
        V.tensor_copy(w3k[:], w3kv_raw[:, 0].unsqueeze(2).to_broadcast([P, KC, HPC, HD])).then_inc(b_y, 1)

        def index_prep(n):
            b = n["b"]
            wait(dve, c_gathered[n["p"]], 32 * n["h"])
            for k_ in range(TOPK):
                last = V.tensor_copy(pidx[n["p"]][k_][:], pos_all[:, bass.ds(b * TOPK + k_, 1)])
            last.then_inc(c_idx, 1)

        def combine(n):
            b, p = n["b"], n["p"]
            wait(dve, c_gathered[p], 32 * (n["h"] + 1))
            wait(dve, c_loaded[p], 16 * (n["h"] + 1))
            V.tensor_copy(wsel[p][:], w_all[:, bass.ds(b * TOPK, TOPK)])
            V.tensor_copy(rsm[:, 0:1], zeros[:, 0:1]).then_inc(rt_w_step, 1)
            dve.wait_ge(rt_w_step, 3 * B + b + 1)
            V.scalar_tensor_tensor(gq, yg[p][0], wsel[p][:, 0:1], x2l[p], ALU.mult, ALU.add).then_inc(c_ln, 1)
            dve.wait_ge(c_ln, 6 * b + 1)
            V.scalar_tensor_tensor(yb[0][:], yg[p][1], wsel[p][:, 1:2], gq, ALU.mult, ALU.add).then_inc(c_ln, 1)
            wait_apart(dve, c_ln, 6 * b + 2)
            V.bn_stats(st6[2][:], yb[0][:]).then_inc(c_ln, 1)
            wait_apart(dve, c_ln, 6 * b + 3)
            V.bn_aggr(mv[2][:], st6[2][:]).then_inc(c_ln, 1)
            dve.wait_ge(c_ln, 6 * b + 4)
            V.tensor_scalar_add(ve[2][:], mv[2][:, 1:2], LN_EPS).then_inc(c_ln, 1)

        def combine_apply(n):
            b = n["b"]
            wait(dve, c_rstd, b + 1)
            wait(dve, c_xr, b - NS + 1)
            V.tensor_scalar(xn[n["s"]][:], yb[0][:], mv[2][:, 0:1], rstd[2][:], ALU.subtract, ALU.mult).then_inc(c_ln, 1)

        def gate_link(n, k, ins):
            ins.then_inc(c_gstep, 1)
            dve.wait_ge(c_gstep, 9 * n["b"] + k)

        def gate_open(n):
            wait(dve, c_gate, n["b"] + 1)
            gate_link(n, 1, V.tensor_tensor(gu, ps_w[:, 0:D], row3["L3_xattn_bg"][:], ALU.add))
            gate_link(n, 2, V.tensor_tensor(gd, at[n["s"]], xr[n["s"]][:], ALU.subtract))

        def gate_apply(n):
            wait(dve, c_exp, n["b"] + 1)
            gate_link(n, 3, V.tensor_scalar_add(ge, ge, 1.0))
            gate_link(n, 4, V.reciprocal(gq, ge))
            gate_link(n, 5, V.tensor_tensor(gu, gu, gq, ALU.mult))
            gate_link(n, 6, V.tensor_tensor(gd, gd, gu, ALU.mult))
            gate_link(n, 7, V.tensor_tensor(go, gd, xr[n["s"]][:], ALU.add))
            gate_link(n, 8, V.scalar_tensor_tensor(gd, go, 1.0 / D, go, ALU.mult, ALU.mult, accum_out=ssq[:]))
            gate_link(n, 9, V.tensor_scalar_add(ve[3][:], ssq[:], RMS_EPS))

        def rms_apply(n):
            b = n["b"]
            wait(dve, c_rms, 5 * b + 4)
            wait(dve, c_mean, b - 1)
            V.scalar_tensor_tensor(xh[n["p"]], go, rstd[3][:], row3["L3_xattn_rms_w"][:], ALU.mult, ALU.mult).then_inc(c_rms, 1)

        def finish(n):
            b = n["b"]
            wait(dve, c_mean, b + 1)
            wait(dve, c_out[n["p"]], 16 * n["h"])
            V.tensor_tensor(fin[n["p"]], xh[n["p"]], ps_w[:, D:2 * D], ALU.subtract).then_inc(c_fin, 1)

        def run_c(j, st, b, first, last):
            c = cparts(j, st, first, last)
            now, prev, g_, m_, nxt, nn = c(0), c(-1), c(-3), c(-4), c(1), c(2)
            if first and st == 0:
                for q in (now, nxt):
                    index_prep(q)
                    combine(q)
                    combine_apply(q)
                index_prep(nn)
                vz_evac(now)
            if now["ok"]:
                maxima(now)
            if prev["ok"]:
                normalise(prev)
            if g_["ok"]:
                gate_open(g_)
            if nxt["ok"]:
                vz_evac(nxt)
            if c(3)["ok"]:
                index_prep(c(3))
            if g_["ok"]:
                gate_apply(g_)
            if prev["ok"]:
                wait(dve, wo_ready, prev["t"] + 1)
            if m_["ok"]:
                finish(m_)
            if prev["ok"]:
                V.tensor_tensor(at[prev["s"]], ps_w[:, 0:D], row3["L3_xattn_bo"][:], ALU.add).then_inc(c_at, 1)
            if nn["ok"]:
                combine(nn)
            if g_["ok"]:
                rms_apply(g_)
            if nn["ok"]:
                combine_apply(nn)
        cslots(run_c, dve)

    @block.gpsimd
    def _(pool):
        G = nc.gpsimd

        pool.wait_ge(bd_zero, 1)
        for h in range(HPC):
            load_block(pool, 2, "wv", h, ld_bd_pool)
        for h in range(HPC // 2, HPC):
            load_block(pool, 0, "wq", h, ld_bd_pool)

        def expand(n):
            t, p = n["t"], n["p"]
            wait(pool, qk_sb, t + 1)
            for c in range(KC):
                last = G.tensor_tensor(qbd[p][:, c], qT[:, c, :].unsqueeze(1).to_broadcast([P, HPC, P]),
                                       hmask.unsqueeze(2).to_broadcast([P, HPC, P]), ALU.mult)
            last.then_inc(qbd_ready, 1)

        def x_init(n):
            f = n["j"] * NS + n["s"]
            wait(pool, x_loaded[n["s"] % 2], 16 * (n["h"] + 1))
            wait(pool, x2_stored[n["s"]], 16 * n["j"])
            wait(pool, scattered[n["s"]], 32 * n["j"])
            G.tensor_tensor(xr[n["s"]][:], xin[n["s"] % 2][:], rows["L0_xattn_b_out"], ALU.add).then_inc(xinit_ready, 1)

        def root(kind, step, value, done):
            wait(pool, step, value)
            G.tensor_tensor(rstd[kind][:], ve[kind][:], neghalf[:], ALU.pow).then_inc(done, 1)

        def residual(n, g, b_, step, value, part, done, count):
            wait(pool, step, value)
            G.tensor_tensor(xr[n["s"]][:], xn[n["s"]][:], g, ALU.mult).then_inc(part, 1)
            wait(pool, part, count + 1)
            G.tensor_tensor(xr[n["s"]][:], xr[n["s"]][:], b_, ALU.add).then_inc(done, 1)

        def scatter(n):
            r = n["j"] * NS + n["s"]
            wait_apart(pool, rt2_step, 6 * r + 6)
            wait_apart(pool, xr_ready, n["t"] + 1)
            for k_ in range(TOPK):
                G.indirect_dma_start(sorted_x, bass.IndirectOffsetOnAxis(posu[n["s"]][:, k_:k_ + 1], 0),
                                     xr[n["s"]][:], None).then_inc(scattered[n["s"]], 16)

        def run(i, tau, t, first, last):
            at_ = parts(i, tau, first, last)
            prev, ff, rk_, nxt, now = at_(-1), at_(-2), at_(-3), at_(1), at_(0)
            if first and tau == 0:
                pool.wait_ge(ld_const, 32)
                pool.wait_ge(consts_ready, 1)
                expand(now)
                pool.wait_ge(rows_ready, 1)
                x_init(now)
            if ff["ok"]:
                root(0, ln_step, 5 * ff["t"] + 4, rstd_ready)
            if now["ok"] and now["l"] == 0 and not (first and tau == 0):
                x_init(now)
            ff_behind = rk_["ok"] and rk_["l"] == 0
            f = rk_["j"] * NS + rk_["s"]
            if ff_behind:
                root(1, ffln_step, 5 * f + 4, ffrstd_ready)
            if nxt["ok"]:
                expand(nxt)
            if ff["ok"]:
                g, b_ = XR_GAIN[ff["l"]]
                residual(ff, rows[g], rows[b_], ln_step, 5 * ff["t"] + 5, xr_part, xr_ready, ff["t"])
            if ff_behind:
                residual(rk_, rows["L0_xattn_g2"], rows["L0_xattn_beta2"], ffln_step, 5 * f + 5, ffxr_part, ffxr_ready, f)
            if rk_["ok"] and rk_["l"] == 3:
                scatter(rk_)
        slots(run, pool)

        pool.wait_ge(rt_rank, B)
        pool.wait_ge(rt2_step, 6 * B)
        pool.wait_ge(xr_ready, NT)

        def load_w2(e, j0, j1):
            pool.dma_start(arena[:, :].rearrange("p (e j n) -> p e j n", e=E, j=FC)[:, e, j0:j1],
                           a["L2_xattn_e_w2"][e].rearrange("(j p) n -> p j n", p=P)[:, j0:j1]).then_inc(ld_experts, 16)
        load_w2(0, 0, FC)
        pool.wait_ge(ld_experts, 16)
        for e in range(W1_EARLY, E):
            pool.dma_start(w1[:, e], a["L2_xattn_e_w1"][e].rearrange("(c p) n -> p c n", p=P)).then_inc(ld_experts, 16)
        load_w2(1, 0, FC)
        pool.wait_ge(ld_experts, 16 + 48)
        for e in range(2, E):
            for j0, j1 in ((0, 3), (3, 6), (6, FC)):
                load_w2(e, j0, j1)
            pool.wait_ge(ld_experts, 16 + 48 * e)

        def gather(n):
            b, p = n["b"], n["p"]
            wait_apart(pool, c_idx, b + 1)
            wait_apart(pool, c_ln, 6 * (b - 2) + 2)
            for k_ in range(TOPK):
                G.indirect_dma_start(yg[p][k_], None, sorted_y,
                                     bass.IndirectOffsetOnAxis(pidx[p][k_][:], 0)).then_inc(c_gathered[p], 16)

        def c_root(n):
            root(2, c_ln, 6 * n["b"] + 5, c_rstd)

        def c_residual(n):
            wait(pool, c_gstep, 9 * (n["b"] - NS) + 7)
            residual(n, row3["L2_xattn_ln3_g"][:], row3["L2_xattn_ln3_b"][:], c_ln, 6 * n["b"] + 6, c_xr_part, c_xr, n["b"])

        for par in range(2):
            pool.wait_ge(b_stored[par], 16 * ((TILES + 1 - par) // 2))
        pool.wait_ge(ld_l3, 16 * 11)

        def run_c(j, st, b, first, last):
            c = cparts(j, st, first, last)
            now, g_, nxt, nn = c(0), c(-3), c(1), c(2)
            if first and st == 0:
                for q in (now, nxt):
                    gather(q)
                    c_root(q)
                gather(nn)
                expand(now)
            if nxt["ok"]:
                expand(nxt)
            if c(3)["ok"]:
                gather(c(3))
            if g_["ok"]:
                wait(pool, c_gstep, 9 * g_["b"] + 9)
                G.tensor_tensor(rstd[3][:], ve[3][:], neghalf[:], ALU.pow).then_inc(c_rms, 4)
            if nn["ok"]:
                c_root(nn)
            if now["ok"]:
                c_residual(now)
        cslots(run_c, pool)


TABLE_TAILS = 1
TABLE_ALL = TABLE_TAILS + 6 + 1 + 3 * E + 7


_NAMES = ["L0_xattn_wv", "L0_xattn_wk", "L0_xattn_wq", "L0_xattn_w_out", "L0_xattn_b_out", "L0_xattn_g1",
          "L0_xattn_beta1", "L0_xattn_w_ff1", "L0_xattn_b_ff1", "L0_xattn_w_ff2", "L0_xattn_b_ff2", "L0_xattn_g2",
          "L0_xattn_beta2", "L1_xattn_Wq", "L1_xattn_Wk", "L1_xattn_Wv", "L1_xattn_Wo", "L1_xattn_gamma",
          "L1_xattn_beta", "L2_xattn_sa_wq", "L2_xattn_sa_bq", "L2_xattn_sa_wk", "L2_xattn_sa_bk", "L2_xattn_sa_wv",
          "L2_xattn_sa_bv", "L2_xattn_sa_wo", "L2_xattn_sa_bo", "L2_xattn_ca_wq", "L2_xattn_ca_bq", "L2_xattn_ca_wk",
          "L2_xattn_ca_bk", "L2_xattn_ca_wv", "L2_xattn_ca_bv", "L2_xattn_ca_wo", "L2_xattn_ca_bo", "L2_xattn_ln1_g",
          "L2_xattn_ln1_b", "L2_xattn_ln2_g", "L2_xattn_ln2_b", "L2_xattn_ln3_g", "L2_xattn_ln3_b",
          "L2_xattn_router_w", "L2_xattn_router_b", "L2_xattn_e_w1", "L2_xattn_e_b1", "L2_xattn_e_w2",
          "L2_xattn_e_b2", "L3_xattn_Wq", "L3_xattn_bq", "L3_xattn_Wk", "L3_xattn_bk", "L3_xattn_Wv", "L3_xattn_bv",
          "L3_xattn_Wo", "L3_xattn_bo", "L3_xattn_Wg", "L3_xattn_bg", "L3_xattn_rms_w"]


def kernel(**inputs):
    import numpy as _np
    import concourse.bacc as _bacc
    from concourse import mybir as _mybir
    from concourse.bass_utils import run_bass_kernel_spmd as _run

    nc = _bacc.Bacc("TRN2", target_bir_lowering=False, num_devices=1)
    given = {"x": inputs["x"], "ctx": inputs["ctx_1024"], "mask": _np.asarray(inputs["mask_Bx1x1xS2_if1"]).reshape(B, P),
             "consts": constants()}
    given["mask_cols"] = _np.ascontiguousarray(given["mask"].T)
    chunks = lambda v: _np.asarray(v).reshape(-1, P).T
    given["cols"] = _np.concatenate(
        [chunks(inputs[n]) for n in COL_NAMES] + [chunks(inputs["L0_xattn_b_ff1"])]
        + [_np.tile(_np.asarray(inputs["L3_xattn_bk"]), HPC).reshape(P, 1)]
        + [_np.asarray(inputs["L2_xattn_e_b1"]).reshape(E * FC, P).T], axis=1)
    given.update({n: inputs[n] for n in _NAMES})
    arrays, args = {}, {}
    for name, v in given.items():
        v = _np.ascontiguousarray(v)
        arrays[f"in_{name}"] = v
        args[name] = nc.dram_tensor(f"in_{name}", v.shape, _mybir.dt.from_np(v.dtype), kind="ExternalInput").ap()
    out = nc.dram_tensor("out_0", (B, P, D), F32, kind="ExternalOutput").ap()
    build(nc, args, out)
    r = _run(nc, [arrays], core_ids=[0])
    return r.results[0]["out_0"]
```

```python
from contextlib import ExitStack

import concourse.bass as bass
from concourse import mybir
import numpy as np

F32 = mybir.dt.float32
F32R = mybir.dt.float32r
BF16 = mybir.dt.bfloat16
I32 = mybir.dt.int32
U32 = mybir.dt.uint32
ALU = mybir.AluOpType
ACT = mybir.ActivationFunctionType
AX_X = mybir.AxisListType.X

P = 128
B = 32
D = 256
KC = D // P
H = 16
HD = D // H
HPC = H // KC
FF = 1024
FC = FF // P
E = 8
TOPK = 2
NS = 4
LAYERS = 4
TPI = LAYERS * NS
ITERS = B // NS
NT = LAYERS * B
SPAN = B * P + P
TILES = (B * P * TOPK + E * (P - 1)) // P
UNUSED = TILES - B * P * TOPK // P
W1_EARLY = E - 2
DUMMY = E * SPAN
NEG = -float(2 ** 66)
LN_EPS = 1e-5
RMS_EPS = 1e-6
WINDOW_HALF = 64

C_ID, C_TRI, C_HMASK, C_ECOL, C_IOTA, C_EBASE, C_TILE, C_END, C_CAUSAL, C_WIN, C_ALL = np.cumsum(
    [0, P, P, HPC, H, E, E, TILES, 0, P, P]).tolist()

COL_NAMES = ["L0_xattn_g1", "L0_xattn_beta1", "L0_xattn_g2", "L0_xattn_beta2", "L1_xattn_gamma", "L1_xattn_beta",
                 "L2_xattn_ln1_g", "L2_xattn_ln1_b", "L2_xattn_ln2_g", "L2_xattn_ln2_b", "L2_xattn_ln3_g",
                 "L2_xattn_ln3_b", "L2_xattn_sa_bq", "L2_xattn_sa_bk", "L2_xattn_ca_bq", "L2_xattn_ca_bk",
                 "L3_xattn_bq"]
COLS = len(COL_NAMES) * KC + FC + 1 + E * FC


def constants():
    c = np.zeros((P, C_ALL), np.float32)
    i, j = np.arange(P)[:, None], np.arange(P)[None, :]
    c[:, C_ID:C_TRI] = i == j
    c[:, C_CAUSAL:C_WIN] = np.where(j <= i, 0.0, NEG)
    c[:, C_WIN:C_ALL] = np.where((j >= i - WINDOW_HALF) & (j < i + WINDOW_HALF + 1), 0.0, NEG)
    c[:, C_TRI:C_HMASK] = i < j
    c[:, C_HMASK:C_ECOL] = np.arange(P)[:, None] // HD == np.arange(HPC)[None, :]
    c[:, C_ECOL:C_IOTA] = (i == np.arange(H)[None, :]) | (i == H + np.arange(H)[None, :])
    c[:, C_IOTA:C_EBASE] = np.arange(E)
    c[:, C_EBASE:C_TILE] = np.arange(E) * SPAN
    c[:, C_TILE:C_END] = np.arange(TILES)
    return c


def build(nc, a, out):
    with ExitStack() as ctx:
        program(nc, a, out, ctx)


def program(nc, a, out, ctx):
    def sb(name, shape, dt=F32):
        return ctx.enter_context(nc.sbuf_tensor(name, [P] + shape, dt))

    def psum(name, shape, dt=F32):
        return ctx.enter_context(nc.psum_tensor(name, [P] + shape, dt))

    def sem(name):
        return ctx.enter_context(nc.semaphore(name))

    def wait(eng, s, value):
        if isinstance(value, int) and value <= 0:
            return
        eng.wait_ge(s, value)

    def wait_apart(eng, sem_, value):
        wait(eng, sem_, value)
        if not isinstance(value, int):
            eng.sem_inc(waits_met, 1)

    x2_dram = nc.dram_tensor("x2_scratch", [B, P, D], F32).ap()
    sorted_x = nc.dram_tensor("sorted_x", [DUMMY + UNUSED * P, D], F32).ap()
    sorted_y = nc.dram_tensor("sorted_y", [TILES * P, D], F32).ap()

    ps_s = psum("ps_scores", [4, 512])
    ps_xv = psum("ps_xv", [512])
    ps_qk = psum("ps_qk", [512])
    ps_o = psum("ps_o", [4, P])
    ps_w = psum("ps_w", [512])

    with nc.sbuf_tensor("w1_experts", [P, E, KC, FF], F32) as w1:
        pass
    sb("w1_early", [W1_EARLY, KC, FF])
    lower = sb("lower", [4096])
    arena = sb("arena", [16384])
    with nc.sbuf_tensor("tiles", [P, 6144], F32) as tiles:
        pass
    qbd_all = sb("qbd_all", [4096])
    pt_all = sb("pt_all", [2048])

    class Carver:
        def __init__(self, t):
            self.t, self.pos = t, 0

        def __call__(self, shape, dt=F32):
            n = int(np.prod(shape))
            words = n if dt == F32 else (n + 1) // 2
            v = self.t[:, self.pos:self.pos + words]
            self.pos += words
            assert self.pos <= self.t.shape[1]
            if dt != F32:
                v = v.bitcast(dt)
            if len(shape) > 1:
                names = "abcd"[:len(shape)]
                v = v.rearrange(f"p ({' '.join(names)}) -> p {' '.join(names)}",
                                **{k: s for k, s in zip(names, shape)})
            return v

    cv = Carver(arena)
    bd = [cv([P]) for _ in range(3)]
    w_l0o = cv([KC, D])
    w_ff1, w_ff2 = cv([KC, FF]), cv([FC, D])
    w_attn = {l: [cv([KC, D]) for _ in range(4)] for l in (1, 2, 3)}
    row_names = ["L0_xattn_b_out", "L0_xattn_g1", "L0_xattn_beta1", "L0_xattn_b_ff2", "L0_xattn_g2",
                 "L0_xattn_beta2", "L1_xattn_gamma", "L1_xattn_beta", "L2_xattn_sa_bo", "L2_xattn_ln1_g",
                 "L2_xattn_ln1_b", "L2_xattn_ca_bo", "L2_xattn_ln2_g", "L2_xattn_ln2_b",
                 "L2_xattn_sa_bv", "L2_xattn_ca_bv"]
    rows = {}
    hT = cv([FC, P])
    left = (arena.shape[1] - cv.pos) // D
    for n in row_names[:left]:
        rows[n] = cv([D])
    for n in row_names[left:]:
        rows[n] = sb("row_" + n, [D])

    cv = Carver(qbd_all)
    qbd = [cv([KC, HPC, P]) for _ in range(2)]
    pt = Carver(pt_all)([H, P])
    cv = Carver(lower)
    qbd_lo = cv([KC, HPC, P])
    qT_lo, kT_lo = cv([KC, P]), [cv([KC, P]) for _ in range(2)]
    cv = Carver(tiles)
    xg = [cv([D]) for _ in range(2)]
    xgT = [cv([KC, P]) for _ in range(2)]
    gT = cv([FC, P])
    ys = [cv([D]) for _ in range(2)]
    b2 = cv([E, D])
    w1f = w1[:].rearrange("p e c n -> p (e c n)")
    w2f = arena[:, :]
    cv = Carver(arena)
    yg = [[cv([D]) for _ in range(TOPK)] for _ in range(2)]
    x2l = [cv([D]) for _ in range(2)]
    at = [cv([D]) for _ in range(NS)]
    atT = cv([KC, P])
    gu, ge, gd, gq = cv([D]), cv([D]), cv([D]), cv([D])
    go, xh = cv([D]), [cv([D]) for _ in range(2)]
    fin = [cv([D]) for _ in range(2)]

    with nc.sbuf_tensor("w1_now", [P, 2, KC, FF], F32) as w1_now:
        pass
    qT, kT = sb("qT", [KC, P]), [sb(f"kT{i}", [KC, P]) for i in range(2)]
    fxT = sb("fxT", [KC, P])
    oT, rs = sb("oT", [KC, P]), sb("rs", [KC, P])
    xin = [sb(f"xin{i}", [D]) for i in range(2)]
    cin = [sb(f"cin{i}", [D]) for i in range(2)]
    cT = [sb(f"cT{i}", [KC, P]) for i in range(NS)]
    xn = [sb(f"xn{i}", [D]) for i in range(NS)]
    xT_all = sb("xT", [NS, KC, P])
    xT = [xT_all[:, i] for i in range(NS)]
    vz = [sb(f"vz{i}", [H // 2, 2, 2, HD]) for i in range(2)]
    xr = [sb(f"xr{i}", [D]) for i in range(NS)]
    yb = [sb(f"yb{i}", [D]) for i in range(2)]
    nm = sb("nm", [H])
    mb = sb("mb", [P], BF16)
    mT = sb("mT", [P], BF16)

    consts = sb("consts", [C_END])
    ident = consts[:, C_ID:C_TRI]
    tri = consts[:, C_TRI:C_HMASK]
    hmask = consts[:, C_HMASK:C_ECOL]
    iota8 = consts[:, C_IOTA:C_EBASE]
    tile_iota = consts[:, C_TILE:C_END]
    ident_b, causal_b, win_b = sb("ident_b", [P], BF16), sb("causal_b", [P], BF16), sb("win_b", [P], BF16)
    ecol_b = sb("ecol_b", [H], BF16)
    one_b = sb("one_b", [1], BF16)
    one_f = sb("one_f", [1])
    mean_w = sb("mean_w", [1])
    neghalf = sb("neghalf", [1])
    onz = sb("onz", [2, 2, HD])
    kmask = [sb(f"kmask{i}", [P], BF16) for i in range(2)]
    kmi = [sb(f"kmi{i}", [P], I32) for i in range(2)]
    mask_cols = sb("mask_cols", [B], I32)
    kmcol = [sb(f"kmcol{i}", [1]) for i in range(2)]

    col_names = COL_NAMES
    cols_all = sb("cols_all", [COLS])
    n_c = len(COL_NAMES) * KC
    cols_t = cols_all[:, 0:n_c].rearrange("p (n c) -> p n c", c=KC)
    bff1, bk3 = cols_all[:, n_c:n_c + FC], cols_all[:, n_c + FC:n_c + FC + 1]
    b1T = cols_all[:, n_c + FC + 1:COLS]
    col = {n: cols_t[:, i, :] for i, n in enumerate(col_names)}
    b1s = [sb(f"b1s{i}", [FC]) for i in range(2)]

    w3q, w3o, w3g = sb("w3q", [KC, D]), sb("w3o", [KC, D]), sb("w3g", [2 * KC, D])
    w3kv_raw = sb("w3kv_raw", [2, KC, HD])
    w3k = sb("w3k", [KC, HPC, HD])
    row3 = {n: sb("row_" + n, [D]) for n in
            ("L3_xattn_bo", "L3_xattn_bg", "L3_xattn_rms_w", "L2_xattn_ln3_g", "L2_xattn_ln3_b")}
    bv3 = sb("bv3", [HD])
    rw, rb = sb("rw", [KC, E]), sb("rb", [E])
    lg, ex, pr, mx8, p8 = (sb(n, [E]) for n in ("lg", "ex", "pr", "mx8", "p8"))
    ix8 = sb("ix8", [E], U32)
    ixf = sb("ixf", [TOPK])
    oh = [sb(f"oh{i}", [TOPK, E]) for i in range(2)]
    ohm = [sb(f"ohm{i}", [E]) for i in range(2)]
    rsm = sb("rsm", [8])
    rk, junk, base = sb("rk", [E]), sb("junk", [E]), sb("base", [E])
    posf = sb("posf", [TOPK])
    posu = [sb(f"posu{i}", [TOPK], U32) for i in range(NS)]
    pos_all = sb("pos_all", [B * TOPK])
    shift = sb("shift", [E])
    w_all = sb("w_all", [B * TOPK])
    wsel = [sb(f"wsel{i}", [TOPK]) for i in range(2)]
    pidx = [[sb(f"pidx{i}{k}", [1], U32) for k in range(TOPK)] for i in range(2)]
    st6 = [sb(f"st6_{i}", [6]) for i in range(3)]
    mv = [sb(f"mv{i}", [2]) for i in range(3)]
    ve = [sb(f"ve{i}", [1]) for i in range(4)]
    rstd = [sb(f"rstd{i}", [1]) for i in range(4)]
    ssq = sb("ssq", [1])
    tt = sb("tt", [8, E])
    tti = sb("tti", [2, E], I32)
    tb = xT_all[:].rearrange("p a b c -> p (a b c)")[:, 0:5 * TILES].rearrange("p (a b) -> p a b", a=5)
    tbi = sb("tbi", [3, TILES + 1], I32)
    tails = sb("tails", [E], I32)
    zeros = sb("zeros", [D])

    ld_const = sem("ld_const")
    ld_bd = sem("ld_bd")
    ld_bd_pool = sem("ld_bd_pool")
    ld_l0 = sem("ld_l0")
    ld_l1 = sem("ld_l1")
    ld_sa = sem("ld_sa")
    ld_ca = sem("ld_ca")
    ld_rows = sem("ld_rows")
    ld_cols = sem("ld_cols")
    ld_l3 = sem("ld_l3")
    ld_router = sem("ld_router")
    ld_w1 = sem("ld_w1")
    ld_experts = sem("ld_experts")
    ld_b2 = sem("ld_b2")
    waits_met = sem("waits_met")
    consts_ready = sem("consts_ready")
    bd_zero = sem("bd_zero")
    rows_ready = sem("rows_ready")
    mask_ready = sem("mask_ready")
    xt_psum = sem("xt_psum")
    xt_sb = sem("xt_sb")
    ctxt_sb = sem("ctxt_sb")
    qk_psum = sem("qk_psum")
    qk_sb = sem("qk_sb")
    v_psum = sem("v_psum")
    vz_ready = sem("vz_ready")
    qbd_ready = sem("qbd_ready")
    qbd_half_ready = sem("qbd_half_ready")
    qbd_act_ready = sem("qbd_act_ready")
    c_ctx_psum = sem("c_ctx_psum")
    qk_lo_ready = sem("qk_lo_ready")
    qbd_lo_ready = sem("qbd_lo_ready")
    scores_ready = sem("scores_ready")
    maxima_part = sem("maxima_part")
    maxima_ready = sem("maxima_ready")
    mt_psum = sem("mt_psum")
    mt_sb = sem("mt_sb")
    st_ready = sem("st_ready")
    probs_ready = sem("probs_ready")
    av_ready = sem("av_ready")
    recip_ready = sem("recip_ready")
    ot_ready = sem("ot_ready")
    wo_ready = sem("wo_ready")
    ln_step = sem("ln_step")
    rstd_ready = sem("rstd_ready")
    xr_part = sem("xr_part")
    xr_ready = sem("xr_ready")
    xinit_ready = sem("xinit_ready")
    fxt_psum = sem("fxt_psum")
    fxt_sb = sem("fxt_sb")
    ff_up = sem("ff_up")
    ff_relu_a = sem("ff_relu_a")
    ff_relu_b = sem("ff_relu_b")
    ff_down = sem("ff_down")
    ffln_step = sem("ffln_step")
    ffrstd_ready = sem("ffrstd_ready")
    ffxr_part = sem("ffxr_part")
    ffxr_ready = sem("ffxr_ready")
    rt_logits = sem("rt_logits")
    rt_step = sem("rt_step")
    rt_exp = sem("rt_exp")
    rt_w_step = sem("rt_w_step")
    rt_rank = sem("rt_rank")
    rt2_step = sem("rt2_step")
    zero_filled = sem("zero_filled")
    tail_zeroed = sem("tail_zeroed")
    table_step = sem("table_step")
    b_xt_psum = sem("b_xt_psum")
    b_xt_sb = sem("b_xt_sb")
    b_b1 = sem("b_b1")
    b_up = sem("b_up")
    w1_copied = sem("w1_copied")
    b_gelu = sem("b_gelu")
    b_down = sem("b_down")
    b_y = sem("b_y")
    c_idx = sem("c_idx")
    c_ln = sem("c_ln")
    c_rstd = sem("c_rstd")
    c_xr_part = sem("c_xr_part")
    c_xr = sem("c_xr")
    c_at = sem("c_at")
    c_att_psum = sem("c_att_psum")
    c_att_sb = sem("c_att_sb")
    c_gate = sem("c_gate")
    c_gstep = sem("c_gstep")
    c_exp = sem("c_exp")
    c_rms = sem("c_rms")
    c_mean = sem("c_mean")
    c_fin = sem("c_fin")
    x_loaded = [sem(f"x_loaded{i}") for i in range(2)]
    ctx_loaded = [sem(f"ctx_loaded{i}") for i in range(2)]
    mask_loaded = [sem(f"mask_loaded{i}") for i in range(2)]
    x2_stored = [sem(f"x2_stored{i}") for i in range(NS)]
    scattered = [sem(f"scattered{i}") for i in range(NS)]
    b_loaded = [sem(f"b_loaded{i}") for i in range(2)]
    b_stored = [sem(f"b_stored{i}") for i in range(2)]
    c_loaded = [sem(f"c_loaded{i}") for i in range(2)]
    c_gathered = [sem(f"c_gathered{i}") for i in range(2)]
    c_out = [sem(f"c_out{i}") for i in range(2)]

    LAYER = [
        dict(scale=1.0 / 16.0, mask="keys", bq=None, bk=None, bv=None),
        dict(scale=0.25, mask=None, bq=None, bk=None, bv=None),
        dict(scale=0.25, mask=causal_b, bq="L2_xattn_sa_bq", bk="L2_xattn_sa_bk", bv="L2_xattn_sa_bv"),
        dict(scale=0.25, mask=None, bq="L2_xattn_ca_bq", bk="L2_xattn_ca_bk", bv="L2_xattn_ca_bv"),
        dict(scale=0.25, mask=win_b, bq="L3_xattn_bq", bk=None, bv=None),
    ]
    XT_GAIN = {1: ("L0_xattn_g2", "L0_xattn_beta2"), 2: ("L1_xattn_gamma", "L1_xattn_beta"),
               3: ("L2_xattn_ln1_g", "L2_xattn_ln1_b"), 4: ("L2_xattn_ln3_g", "L2_xattn_ln3_b")}
    XR_GAIN = {0: ("L0_xattn_g1", "L0_xattn_beta1"), 1: ("L1_xattn_gamma", "L1_xattn_beta"),
               2: ("L2_xattn_ln1_g", "L2_xattn_ln1_b"), 3: ("L2_xattn_ln2_g", "L2_xattn_ln2_b")}

    def slots(run, eng):
        def iteration(i, first, last):
            for tau in range(TPI + (4 if last else 0)):
                run(i, tau, i * TPI + tau, first, last)
        iteration(0, True, False)
        with eng.Fori(1, ITERS - 1) as i:
            iteration(i, False, False)
        iteration(ITERS - 1, False, True)

    def parts(i, tau, first, last):
        has = lambda d: not (first and tau + d < 0) and not (last and tau + d >= TPI)
        def at_(d):
            w = (tau + d) % TPI
            j = i + (tau + d) // TPI
            return dict(l=w // NS, s=w % NS, j=j, h=2 * j + (w % NS) // 2, t=i * TPI + tau + d, p=(tau + d) % 2, ok=has(d), d=d)
        return at_

    def cslots(run, eng):
        def iteration(j, first, last):
            for st in range(NS + (4 if last else 0)):
                run(j, st, j * NS + st, first, last)
        iteration(0, True, False)
        with eng.Fori(1, ITERS - 1) as j:
            iteration(j, False, False)
        iteration(ITERS - 1, False, True)

    def cparts(j, st, first, last):
        def at_(d):
            ok = not (first and st + d < 0) and not (last and st + d >= NS)
            jj = j + (st + d) // NS
            return dict(l=4, s=(st + d) % NS, j=jj, h=2 * jj + (st + d) % NS // 2, b=j * NS + st + d, t=NT + j * NS + st + d, p=(st + d) % 2, ok=ok)
        return at_

    def pairs(body, eng):
        body(0)
        with eng.Fori(1, (TILES - 1) // 2) as j:
            body(j)

    def halves(n):
        if n["l"] == 4:
            return 3 * B
        return n["j"] * 3 * NS + ((n["l"] - 1) * NS + n["s"] if n["l"] > 0 else 0)

    def act_halves(n):
        if n["l"] == 4:
            return B + n["b"]
        return n["j"] * NS + (n["s"] if n["l"] == 0 else NS)

    RT = 12

    def r_par(n):
        return n["s"] % 2


    def load_block(eng, m, n, h, done):
        eng.dma_start(bd[m][HD * h:HD * (h + 1), HD * h:HD * (h + 1)], a["L0_xattn_" + n]).then_inc(done, 16)

    block = ctx.enter_context(nc.Block())

    @block.sync
    def _(sp):
        sp.dma_start(consts[:], a["consts"][:, 0:C_END]).then_inc(ld_const, 16)
        sp.dma_start(pt[:, 0:2, :], a["consts"][:, C_CAUSAL:C_ALL].rearrange("p (a b) -> p a b", a=2)).then_inc(ld_const, 16)

        def load_x(i, st):
            u = b = i * NS + st
            wait_apart(sp, xt_psum, (i * TPI + st - 2 + 1) if st >= 2 else (i - 1) * TPI + st + 2 + 1)
            wait_apart(sp, xinit_ready, u - 1)
            wait_apart(sp, mask_ready, 3 * (u - 1))
            sp.dma_start(xin[st % 2][:], a["x"][bass.ds(b, 1)].rearrange("o s d -> s (o d)")).then_inc(x_loaded[st % 2], 16)
            sp.dma_start(cin[st % 2][:], a["ctx"][bass.ds(b, 1)].rearrange("o s d -> s (o d)")).then_inc(ctx_loaded[st % 2], 16)
            sp.dma_start(kmi[st % 2][0:1, :], a["mask"][bass.ds(b, 1)]).then_inc(mask_loaded[st % 2], 16)

        sp.dma_start(mask_cols[:], a["mask_cols"]).then_inc(ld_cols, 16)
        sp.dma_start(cols_all[:], a["cols"]).then_inc(ld_cols, 16)
        load_x(0, 0)
        kcp = lambda n: a[n].rearrange("(c p) n -> p c n", p=P)
        for n in row_names:
            sp.dma_start(rows[n], a[n].rearrange("(o d) -> o d", o=1).partition_broadcast(P)).then_inc(ld_rows, 16)
        load_x(0, 1)
        sp.dma_start(w_l0o, kcp("L0_xattn_w_out")).then_inc(ld_l0, 16)
        sp.dma_start(w_ff1, kcp("L0_xattn_w_ff1")).then_inc(ld_l0, 16)
        sp.dma_start(w_ff2, kcp("L0_xattn_w_ff2")).then_inc(ld_l0, 16)

        def late_loads(tau):
            if tau == 0:
                for j, n in enumerate(("Wq", "Wk", "Wv")):
                    for c in range(KC):
                        sp.dma_start(w_attn[1][j][:, c, :].rearrange("p (h d) -> p h d", h=H),
                                     a["L1_xattn_" + n].rearrange("h (c p) d -> p c h d", p=P)[:, c]).then_inc(ld_l1, 16)
                sp.dma_start(w_attn[1][3], kcp("L1_xattn_Wo")).then_inc(ld_l1, 16)
            if tau == 2:
                for l, pre, ld in ((2, "L2_xattn_sa_", ld_sa), (3, "L2_xattn_ca_", ld_ca)):
                    for j, n in enumerate(("wq", "wk", "wv", "wo")):
                        sp.dma_start(w_attn[l][j], kcp(pre + n)).then_inc(ld, 16)
                sp.dma_start(rw[:], kcp("L2_xattn_router_w")).then_inc(ld_router, 16)
                sp.dma_start(rb[:], a["L2_xattn_router_b"].rearrange("(o d) -> o d", o=1).partition_broadcast(P)).then_inc(ld_router, 16)
            if tau == 4:
                sp.dma_start(w3q[:], kcp("L3_xattn_Wq")).then_inc(ld_l3, 16)
                sp.dma_start(w3kv_raw[:, 0], kcp("L3_xattn_Wk")).then_inc(ld_l3, 16)
                sp.dma_start(w3kv_raw[:, 1], kcp("L3_xattn_Wv")).then_inc(ld_l3, 16)
                sp.dma_start(w3o[:], kcp("L3_xattn_Wo")).then_inc(ld_l3, 16)
                sp.dma_start(w3g[:], kcp("L3_xattn_Wg")).then_inc(ld_l3, 16)
                for n in row3:
                    sp.dma_start(row3[n][:], a[n].rearrange("(o d) -> o d", o=1).partition_broadcast(P)).then_inc(ld_l3, 16)
                sp.dma_start(bv3[:], a["L3_xattn_bv"].rearrange("(o d) -> o d", o=1).partition_broadcast(P)).then_inc(ld_l3, 16)
            if tau == 5:
                sp.wait_ge(consts_ready, 1)
                for k in range(UNUSED):
                    sp.dma_start(sorted_x[DUMMY + k * P:DUMMY + (k + 1) * P, :], zeros[:]).then_inc(zero_filled, 16)
            e = tau - 6
            if 0 <= e < W1_EARLY:
                sp.dma_start(w1[:, e], a["L2_xattn_e_w1"][e].rearrange("(c p) n -> p c n", p=P)).then_inc(ld_w1, 16)

        def run(i, tau, t, first, last):
            at_ = parts(i, tau, first, last)
            n = at_(2)
            if n["ok"] and n["l"] == 0 and not (first and tau + 2 == 0):
                load_x(n["j"], n["s"])
            if first:
                late_loads(tau)
            q = at_(-2)
            if q["ok"] and q["l"] == 3:
                b = q["j"] * NS + q["s"]
                wait_apart(sp, xr_ready, q["t"] + 1)
                sp.dma_start(x2_dram[bass.ds(b, 1)].rearrange("o s d -> s (o d)"), xr[q["s"]][:]).then_inc(x2_stored[q["s"]], 16)
        slots(run, sp)

        sp.wait_ge(av_ready, NT)
        sp.dma_start(b2, a["L2_xattn_e_b2"].rearrange("(o e) d -> o (e d)", o=1).partition_broadcast(P)
                     .rearrange("p o (e d) -> p (o e) d", e=E)).then_inc(ld_b2, 16)
        sp.wait_ge(table_step, TABLE_TAILS)
        for e in range(E):
            r = sp.value_load(tails[0:1, e:e + 1], min_val=0, max_val=DUMMY - P)
            sp.dma_start(sorted_x[bass.ds(r, P), :], zeros[:]).then_inc(tail_zeroed, 16)
        sp.wait_ge(tail_zeroed, 16 * E)
        sp.wait_ge(zero_filled, 16 * UNUSED)
        for st in range(NS):
            sp.wait_ge(scattered[st], 32 * ITERS)
        sp.wait_ge(table_step, TABLE_ALL)

        def load_tile(k, par):
            r = sp.value_load(tbi[0:1, 0, bass.ds(k, 1)], min_val=0, max_val=DUMMY + (UNUSED - 1) * P)
            sp.dma_start(xg[par], sorted_x[bass.ds(r, P), :]).then_inc(b_loaded[par], 16)

        def store_tile(k, par):
            wait_apart(sp, b_y, k + 1)
            sp.dma_start(sorted_y[bass.ds(k * P, P), :], ys[par]).then_inc(b_stored[par], 16)

        load_tile(0, 0)
        load_tile(1, 1)

        def tile_pair(j, first):
            wait_apart(sp, b_xt_psum, 2 * j + 1)
            load_tile(2 * j + 2, 0)
            if not first:
                store_tile(2 * j - 2, 0)
            wait_apart(sp, b_xt_psum, 2 * j + 2)
            r = sp.value_load(tbi[0:1, 2, bass.ds(2 * j, 1)], min_val=0, max_val=DUMMY + (UNUSED - 1) * P)
            sp.dma_start(xg[1], sorted_x[bass.ds(r, P), :]).then_inc(b_loaded[1], 16)
            if not first:
                store_tile(2 * j - 1, 1)
        tile_pair(0, True)
        with sp.Fori(1, (TILES - 1) // 2) as j:
            tile_pair(j, False)
        for k in range(TILES - 3, TILES):
            store_tile(k, k % 2)

        for par in range(2):
            sp.wait_ge(b_stored[par], 16 * ((TILES + 1 - par) // 2))
        for st in range(NS):
            sp.wait_ge(x2_stored[st], 16 * ITERS)

        def load_c(b, par):
            wait_apart(sp, c_ln, 6 * (b - 2) + 1)
            wait_apart(sp, xt_psum, NT + b - 1)
            sp.dma_start(x2l[par], x2_dram[bass.ds(b, 1)].rearrange("o s d -> s (o d)")).then_inc(c_loaded[par], 16)
            sp.dma_start(cin[par][:], a["ctx"][bass.ds(b, 1)].rearrange("o s d -> s (o d)")).then_inc(ctx_loaded[par], 16)

        def store_c(b, par):
            wait_apart(sp, c_fin, b + 1)
            sp.dma_start(out[bass.ds(b, 1)].rearrange("o s d -> s (o d)"), fin[par]).then_inc(c_out[par], 16)

        load_c(0, 0)
        load_c(1, 1)
        load_c(2, 0)

        def run_c(j, st, b, first, last):
            c = cparts(j, st, first, last)
            if c(3)["ok"]:
                load_c(c(3)["b"], c(3)["p"])
            if c(-4)["ok"]:
                store_c(c(-4)["b"], c(-4)["p"])
        cslots(run_c, sp)
        for par in range(2):
            sp.wait_ge(c_out[par], 16 * B // 2)

    @block.tensor
    def _(pe):
        mm = nc.tensor.matmul

        def transposes(ps, src, done):
            for c in range(KC):
                last = nc.tensor.transpose(ps[:, P * c:P * (c + 1)], src[:, P * c:P * (c + 1)], ident)
            if done is not None:
                last.then_inc(done, 1)

        def xt(n):
            t, l = n["t"], n["l"]
            wait(pe, vz_ready, t)
            if l == 0:
                u = n["j"] * NS + n["s"]
                wait(pe, ff_relu_b, n["j"] * NS)
                wait(pe, x_loaded[n["s"] % 2], 16 * (n["h"] + 1))
                wait(pe, ctx_loaded[n["s"] % 2], 16 * (n["h"] + 1))
                for c in range(KC):
                    nc.tensor.transpose(ps_xv[:, D + P * c:D + P * (c + 1)], cin[n["s"] % 2][:, P * c:P * (c + 1)], ident)
                transposes(ps_xv, xin[n["s"] % 2], xt_psum)
            elif l == 4:
                wait(pe, c_ln, 6 * (n["b"] + 1))
                wait(pe, ctxt_sb, B + n["b"] + 1)
                transposes(ps_xv, xn[n["s"]], xt_psum)
            else:
                f = n["j"] * NS + n["s"]
                if l == 1:
                    wait(pe, ffln_step, 5 * (f + 1))
                    wait(pe, ff_relu_b, f + 1)
                else:
                    wait(pe, ln_step, 5 * (t - NS + 1))
                wait(pe, fxt_sb, xv_uses(n))
                transposes(ps_xv, xn[n["s"]], xt_psum)

        def ctxt(n):
            wait(pe, vz_ready, n["t"])
            wait(pe, ctx_loaded[n["p"]], 16 * (B // 2 + n["h"] + 1))
            wait(pe, c_att_sb, n["b"] - 3)
            transposes(ps_xv[:, D:2 * D], cin[n["p"]], c_ctx_psum)

        def xv_uses(n):
            j, l = n["j"], n["l"]
            if l == 1:
                return j * 2 * NS + n["s"] + 1 if n["s"] < NS else 0
            return j * 2 * NS + NS

        def project_v(n, first_l):
            t, l = n["t"], n["l"]
            if first_l:
                if l == 0:
                    pe.wait_ge(ld_bd, 16 * (HPC + HPC // 2))
                    pe.wait_ge(ld_bd_pool, 16 * (HPC + HPC // 2))
                elif l == 1:
                    pe.wait_ge(ld_l1, 16 * 7)
                elif l == 2:
                    pe.wait_ge(ld_sa, 16 * 4)
                elif l == 3:
                    pe.wait_ge(ld_ca, 16 * 4)
            kv = xT[n["s"]] if l == 2 else cT[n["s"]]
            wait(pe, xt_sb, t + 1)
            if l == 0:
                wait(pe, ctxt_sb, n["j"] * NS + n["s"] + 1)
                for c in range(KC):
                    last = mm(ps_xv[:, D + P * c:D + P * (c + 1)], kv[:, c, :], bd[2], start=True, stop=True)
            elif l == 4:
                wait(pe, ctxt_sb, B + n["b"] + 1)
                for c in range(KC):
                    last = mm(ps_xv[:, D:D + HD], kv[:, c, :], w3kv_raw[:, 1, c, :], start=c == 0, stop=c == KC - 1)
            else:
                for c in range(KC):
                    last = mm(ps_xv[:, D:2 * D], kv[:, c, :], w_attn[l][2][:, c, :], start=c == 0, stop=c == KC - 1)
            last.then_inc(v_psum, 1)

        def project_qk(n):
            t, l = n["t"], n["l"]
            src = xT[n["s"]]
            kv = src if l == 2 else cT[n["s"]]
            wait(pe, mt_sb, t)
            if l == 0:
                for m, (w, x_) in enumerate(((bd[0], src), (bd[1], kv))):
                    for c in range(KC):
                        last = mm(ps_qk[:, D * m + P * c:D * m + P * (c + 1)], w, x_[:, c, :], start=True, stop=True)
            else:
                wq = w3q if l == 4 else w_attn[l][0]
                for o in range(KC):
                    for c in range(KC):
                        mm(ps_qk[:, P * o:P * (o + 1)], wq[:, c, P * o:P * (o + 1)], src[:, c, :], start=c == 0, stop=c == KC - 1)
                if l == 4:
                    for c in range(KC):
                        last = mm(ps_qk[:, D:D + P], w3k[:, c].rearrange("p r d -> p (r d)"), kv[:, c, :], start=c == 0, stop=c == KC - 1)
                else:
                    for o in range(KC):
                        for c in range(KC):
                            last = mm(ps_qk[:, D + P * o:D + P * (o + 1)], w_attn[l][1][:, c, P * o:P * (o + 1)],
                                      kv[:, c, :], start=c == 0, stop=c == KC - 1)
            last.then_inc(qk_psum, 1)

        def scores(n):
            t, l, p = n["t"], n["l"], n["p"]
            mask = LAYER[l]["mask"]
            wait(pe, qk_sb, t + 1)
            wait(pe, qbd_ready, t + 1)
            if l in (1, 2, 3):
                wait(pe, qbd_half_ready, halves(n) + 1)
            else:
                wait(pe, qbd_act_ready, act_halves(n) + 1)
            if l == 0:
                wait(pe, mask_ready, 3 * (n["j"] * NS + n["s"] + 1))
            for g in range(4):
                c = g // 2
                if g % 2 == 0:
                    wait(pe, probs_ready, 4 * (t - 1) + g + 2)
                if mask == "keys":
                    mm(ps_s[:, g, :].rearrange("p (h k) -> p h k", h=4), one_b[:].to_broadcast([P, P]),
                       kmask[n["s"] % 2][:].unsqueeze(1).to_broadcast([P, 4, P]), start=True, stop=False)
                elif mask is not None:
                    mm(ps_s[:, g, :].rearrange("p (h k) -> p h k", h=4), ident_b[:],
                       mask[:].unsqueeze(1).to_broadcast([P, 4, P]), start=True, stop=False)
                k_ = kT[p][:, 0 if l == 4 else c, :].bitcast(BF16).rearrange("p (k two) -> p two k", two=2)[:, 1, :]
                for h in range(4):
                    q_ = qbd[p][:, c, (g % 2) * 4 + h, :].bitcast(BF16).rearrange("p (k two) -> p two k", two=2)[:, 1, :]
                    last = mm(ps_s[:, g, P * h:P * (h + 1)], q_, k_, start=mask is None, stop=mask is None or h == 3)
                if g % 2 == 1:
                    last.then_inc(scores_ready, 1)

        def scores_t(n, groups=range(4)):
            t, l, p = n["t"], n["l"], n["p"]
            mask = LAYER[l]["mask"]
            wait(pe, mt_sb, t + 1)
            wait(pe, qk_lo_ready, t + 1)
            wait(pe, qbd_lo_ready, t + 1)
            for g in groups:
                c = g // 2
                kc = 0 if l == 4 else c
                four = lambda q_: q_[:, c, (g % 2) * 4:(g % 2) * 4 + 4, :].rearrange("p h q -> p (h q)").bitcast(F32R)
                for k_, q_ in ((kT[p], qbd[p]), (kT[p], qbd_lo), (kT_lo[p], qbd[p])):
                    mm(ps_s[:, g, :], k_[:, kc, :].bitcast(F32R), four(q_), start=q_ is qbd[p] and k_ is kT[p], stop=False)
                if mask is not None and mask != "keys":
                    mm(ps_s[:, g, :].rearrange("p (h q) -> p h q", h=4), mask[:],
                       ident_b[:].unsqueeze(1).to_broadcast([P, 4, P]), start=False, stop=False)
                for h in range(4):
                    last = mm(ps_s[:, g, P * h:P * (h + 1)], ecol_b[:, 4 * g + h:4 * g + h + 1].to_broadcast([P, P]),
                              mT[:], start=False, stop=h == 3)
                last.then_inc(st_ready, 1)

        def maxima_t(n):
            t, l = n["t"], n["l"]
            wait(pe, maxima_ready, t + 1)
            wait(pe, qk_lo_ready, t + 1)
            if l != 4 and n.get("ffwait") is not None:
                wait(pe, ff_relu_a, n["ffwait"])
            nc.tensor.transpose(ps_qk[:].bitcast(BF16)[:, 0:P], mb[:], ident_b[:]).then_inc(mt_psum, 1)

        def av(n):
            t, l, p = n["t"], n["l"], n["p"]
            wait(pe, probs_ready, 4 * (t + 1))
            wait(pe, vz_ready, t + 1)
            wait(pe, ot_ready, t)
            for kind in range(2):
                for c in range(KC):
                    for par in range(2):
                        for q in range(4):
                            h = c * HPC + 2 * q + par
                            w = vz[p][:, h // 2, par].rearrange("p a d -> p (a d)") if kind == 0 else onz[:, par].rearrange("p a d -> p (a d)")
                            last = mm(ps_o[32 * q:32 * q + 32, 2 * kind + c, :], w, pt[:, h, :],
                                      start=par == 0, stop=par == 1, tile_position=(0, 32 * q))
            last.then_inc(av_ready, 1)

        def wo(n, first_l, w_free):
            t, l = n["t"], n["l"]
            if first_l and l == 0:
                pe.wait_ge(ld_l0, 16 * 3)
            w = w_l0o if l == 0 else w3o if l == 4 else w_attn[l][3]
            wait(pe, ot_ready, t + 1)
            w_free()
            for c in range(KC):
                last = mm(ps_w[:, 0:D], oT[:, c, :], w[:, c, :], start=c == 0, stop=c == KC - 1)
            last.then_inc(wo_ready, 1)

        def fxt(n, ahead):
            t = n["t"]
            wait(pe, ln_step, 5 * (t + 1))
            if ahead:
                wait(pe, vz_ready, t + 4)
            transposes(ps_xv, xn[n["s"]], fxt_psum)

        def ff_hidden(n, u):
            t = n["t"]
            wait(pe, fxt_sb, u + 1)
            wait(pe, qk_lo_ready, t + 4)
            for half, bank, done in ((0, ps_qk, 1), (1, ps_xv, 1)):
                for j in range(4):
                    for c in range(KC):
                        last = mm(bank[:, P * j:P * (j + 1)], w_ff1[:, c, P * (4 * half + j):P * (4 * half + j + 1)],
                                  fxT[:, c, :], start=c == 0, stop=c == KC - 1)
                last.then_inc(ff_up, 1)

        def ff_output(n):
            f = n["j"] * NS + n["s"]
            wait(pe, ln_step, 5 * (n["t"] + 1) + 1)
            for j in range(FC):
                if j == 0:
                    wait(pe, ff_relu_a, f + 1)
                if j == 4:
                    wait(pe, ff_relu_b, f + 1)
                last = mm(ps_w[:, 0:D], hT[:, j, :], w_ff2[:, j, :], start=j == 0, stop=j == FC - 1)
            last.then_inc(ff_down, 1)

        def router(n, u, tail):
            t = n["t"]
            wait(pe, fxt_sb, u + 1)
            if isinstance(n["j"], int):
                wait(pe, rt2_step, 6 * (n["j"] * NS + n["s"] - 2) + 5)
            if not tail:
                wait(pe, ln_step, 5 * (t + 1) + 1)
            for c in range(KC):
                last = mm(ps_w[:, 0:E], fxT[:, c, :], rw[:, c, :], start=c == 0, stop=c == KC - 1)
            last.then_inc(rt_logits, 1)

        def rank(n, behind):
            r = n["j"] * NS + n["s"]
            wait(pe, rt_step, RT * (r + 1))
            wait(pe, ln_step, 5 * behind + 1)
            mm(ps_w[:, D:D + E], tri, ohm[r_par(n)][:], start=True, stop=True)
            mm(ps_w[:, D + E:D + 2 * E], one_f[:].to_broadcast([P, P]), ohm[r_par(n)][:], start=True, stop=True).then_inc(rt_rank, 1)

        def run(i, tau, t, first, last):
            at_ = parts(i, tau, first, last)
            now, prev, ff, rk_, nxt, old = at_(0), at_(-1), at_(-2), at_(-3), at_(1), at_(-4)
            u_of = lambda n: n["j"] * 2 * NS + (0 if n["l"] == 0 else NS) + n["s"]
            ff_behind = rk_["ok"] and rk_["l"] == 0

            def last_scores(g0):
                if now["ok"]:
                    scores_t(now, range(g0, 3))
                if ff["ok"] and ff["l"] in (0, 3):
                    fxt(ff, nxt["ok"])
                if now["ok"]:
                    scores_t(now, range(3, 4))

            if first and tau == 0:
                pe.wait_ge(ld_const, 32)
                pe.wait_ge(consts_ready, 1)
                xt(now)
                project_v(now, True)
                project_qk(now)
            if now["ok"]:
                scores(now)
            if rk_["ok"] and rk_["l"] == 3:
                if first and rk_["s"] == 0:
                    pe.wait_ge(ld_router, 16 * 2)
                router(rk_, u_of(rk_), tail=not ff["ok"])
            if old["ok"] and old["l"] == 3:
                rank(old, ff["t"] if ff["ok"] else NT - 1)
            if ff_behind:
                if rk_["s"] == 0:
                    wait(pe, rt2_step, 6 * NS * rk_["j"])
                ff_output(rk_)
                now["ffwait"] = rk_["j"] * NS + rk_["s"] + 1
                maxima_t(now)
                av(prev)
                xt(nxt)
                scores_t(now, range(1))
                project_v(nxt, first and nxt["s"] == 0 and nxt["l"] > 0)
                project_qk(nxt)
                last_scores(1)
            else:
                if nxt["ok"]:
                    xt(nxt)
                if prev["ok"]:
                    av(prev)
                if now["ok"]:
                    maxima_t(now)
                if nxt["ok"]:
                    project_v(nxt, first and nxt["s"] == 0 and nxt["l"] > 0)
                    project_qk(nxt)
                last_scores(0)
            if prev["ok"]:
                def w_free():
                    wait(pe, ln_step, 5 * (prev["t"] - 1) + 1)
                    if ff_behind:
                        wait(pe, ffln_step, 5 * (rk_["j"] * NS + rk_["s"]) + 1)
                    if rk_["ok"] and rk_["l"] == 3:
                        wait(pe, rt_step, RT * (rk_["j"] * NS + rk_["s"]) + 1)
                    if old["ok"] and old["l"] == 3:
                        wait(pe, rt2_step, 6 * (old["j"] * NS + old["s"]) + 5)
                wo(prev, first and tau - 1 == 0, w_free)
            if ff["ok"] and ff["l"] == 0:
                ff_hidden(ff, u_of(ff))
        slots(run, pe)

        pe.wait_ge(rt2_step, 6 * B)
        pe.wait_ge(table_step, TABLE_ALL)

        def tile_transposes(k, par, use):
            wait(pe, b_loaded[par], 16 * (use + 1))
            wait(pe, b_xt_sb, k)
            transposes(ps_xv, xg[par], b_xt_psum)

        def up(k, par):
            wait(pe, w1_copied, k + 1)
            wait(pe, b_xt_sb, k + 1)
            wait(pe, b_gelu, k - 1)
            for j in range(FC):
                for c in range(KC):
                    last = mm(ps_s[:, 2 * par + j // 4, P * (j % 4):P * (j % 4 + 1)],
                              w1_now[:, par, c, P * j:P * (j + 1)], xgT[par][:, c, :], start=c == 0, stop=c == KC - 1)
            last.then_inc(b_up, 1)

        def down(k):
            e = pe.value_load(tbi[0:1, 1, bass.ds(k, 1)], min_val=0, max_val=E - 1)
            wait(pe, ld_experts, e * 48 + 16)
            wait(pe, b_gelu, k + 1)
            wait(pe, b_y, k)
            for j in range(FC):
                last = mm(ps_w[:, 0:D], gT[:, j, :], w2f[:, bass.ds(e * (FC * D) + j * D, D)], start=j == 0, stop=j == FC - 1)
            last.then_inc(b_down, 1)

        tile_transposes(0, 0, 0)
        up(0, 0)
        tile_transposes(1, 1, 0)

        def tile_pair(j):
            for d in (1, 2):
                k = 2 * j + d
                up(k, d % 2)
                tile_transposes(k + 1, (d + 1) % 2, j + 1)
                down(k - 1)
        pairs(tile_pair, pe)
        down(TILES - 1)

        def gate_transposes(n):
            b = n["b"]
            wait(pe, c_at, b + 1)
            wait(pe, xt_sb, min_t(n, 3))
            wait(pe, vz_ready, min_t(n, 3))
            wait(pe, c_xr, b + 1)
            transposes(ps_xv, at[n["s"]], c_att_psum)

        def gate(n):
            b = n["b"]
            wait(pe, c_att_sb, b + 1)
            wait(pe, c_at, min_b(n, 2))
            wait(pe, c_fin, b - 1)
            for c in range(KC):
                mm(ps_w[:, 0:D], atT[:, c, :], w3g[:, c, :], start=c == 0, stop=False)
            for c in range(KC):
                last = mm(ps_w[:, 0:D], xT[n["s"]][:, c, :], w3g[:, KC + c, :], start=False, stop=c == KC - 1)
            last.then_inc(c_gate, 1)

        def min_t(n, d):
            return n["t"] + d + 1 if n["ahead"] >= d else n["t"] + n["ahead"] + 1

        def min_b(n, d):
            return n["b"] + d if n["ahead"] >= d - 1 else n["b"] + n["ahead"] + 1

        def mean(n):
            b = n["b"]
            wait(pe, c_rms, 5 * (b + 1))
            wait(pe, c_gstep, 9 * (b + 1) + 1 if n["ahead"] else 9 * b + 1)
            mm(ps_w[:, D:2 * D], mean_w[:].to_broadcast([P, P]), xh[n["p"]], start=True, stop=True).then_inc(c_mean, 1)

        pe.wait_ge(ld_l3, 16 * 11)

        def run_c(j, st, b, first, last):
            c = cparts(j, st, first, last)
            now, prev, g_, m_, nxt = c(0), c(-1), c(-2), c(-4), c(1)
            m_["ahead"] = not (last and st == NS + 3)
            h_ = c(-3)
            g_["ahead"] = 99 if not last else (NS - 1) - (st - 2)
            h_["ahead"] = 99 if not last else (NS - 1) - (st - 3)
            if first and st == 0:
                pe.wait_ge(b_y, TILES)
                ctxt(now)
                xt(now)
                project_v(now, False)
                project_qk(now)
            if now["ok"]:
                scores(now)
            if h_["ok"]:
                gate(h_)
            if nxt["ok"]:
                ctxt(nxt)
            if prev["ok"]:
                av(prev)
            if now["ok"]:
                maxima_t(now)
            if nxt["ok"]:
                xt(nxt)
            if now["ok"]:
                scores_t(now, range(1))
            if nxt["ok"]:
                project_v(nxt, False)
                project_qk(nxt)
            if now["ok"]:
                scores_t(now, range(1, 4))
            if m_["ok"]:
                mean(m_)
            if prev["ok"]:
                wo(prev, False, lambda: wait(pe, c_gstep, 9 * (prev["b"] - 2) + 1))
            if g_["ok"]:
                gate_transposes(g_)
        cslots(run_c, pe)

    @block.scalar
    def _(act):
        act.wait_ge(bd_zero, 1)
        for h in range(HPC):
            load_block(act, 1, "wk", h, ld_bd)
        for h in range(HPC // 2):
            load_block(act, 0, "wq", h, ld_bd)

        def xt_evac(n):
            t, l = n["t"], n["l"]
            wait(act, xt_psum, t + 1)
            src = ps_xv[:, 0:D].rearrange("p (c q) -> p c q", c=KC)
            if l == 0:
                nc.scalar.copy(cT[n["s"]][:], ps_xv[:, D:2 * D].rearrange("p (c q) -> p c q", c=KC)).then_inc(ctxt_sb, 1)
            if l == 0:
                nc.scalar.copy(xT[n["s"]], src).then_inc(xt_sb, 1)
                return
            g, b_ = XT_GAIN[l]
            for c in range(KC):
                last = nc.scalar.activation(xT[n["s"]][:, c, :], src[:, c, :], ACT.Identity, bias=col[b_][:, c:c + 1], scale=col[g][:, c:c + 1])
            last.then_inc(xt_sb, 1)

        def ctxt_evac(n):
            wait(act, c_ctx_psum, n["b"] + 1)
            nc.scalar.copy(cT[n["s"]][:], ps_xv[:, D:2 * D].rearrange("p (c q) -> p c q", c=KC)).then_inc(ctxt_sb, 1)

        def qk_evac(n):
            t, l, p = n["t"], n["l"], n["p"]
            wait(act, qk_psum, t + 1)
            wait(act, qbd_ready, t)
            wait(act, qbd_half_ready, halves(n))
            wait(act, qbd_act_ready, act_halves(n))
            wait(act, qk_lo_ready, t)
            L = LAYER[l]
            srcs = ps_qk[:].rearrange("p (m c q) -> p m c q", m=2, c=KC)
            for m, dst, bias in ((0, qT, L["bq"]), (1, kT[p], L["bk"])):
                if l == 4 and m == 1:
                    last = nc.scalar.activation(dst[:, 0, :].bitcast(F32R), srcs[:, 1, 0], ACT.Identity, bias=bk3[:])
                elif bias is None:
                    last = nc.scalar.copy(dst[:].bitcast(F32R), srcs[:, m])
                else:
                    for c in range(KC):
                        last = nc.scalar.activation(dst[:, c, :].bitcast(F32R), srcs[:, m, c], ACT.Identity, bias=col[bias][:, c:c + 1])
            last.then_inc(qk_sb, 1)
            if l in (0, 4):
                wait(act, qk_sb, t + 1)
                for h in range(HPC):
                    last = nc.scalar.activation(qbd[p][:, 1, h, :].bitcast(F32R), qT[:, 1, :], ACT.Identity,
                                                bias=0.0, scale=hmask[:, h:h + 1])
                last.then_inc(qbd_act_ready, 1)

        def mt_evac(n):
            wait(act, mt_psum, n["t"] + 1)
            nc.scalar.copy(mT[:], ps_qk[:].bitcast(BF16)[:, 0:P]).then_inc(mt_sb, 1)

        def exps(n, groups=range(4)):
            t, l = n["t"], n["l"]
            for g in groups:
                wait(act, st_ready, 4 * t + g + 1)
                bias = kmcol[n["s"] % 2][:] if l == 0 else 0.0
                nc.scalar.activation(pt[:, 4 * g:4 * g + 4, :].rearrange("p h q -> p (h q)"), ps_s[:, g, :], ACT.Exp,
                                     bias=bias, scale=LAYER[l]["scale"]).then_inc(probs_ready, 1)

        def fxt_evac(n, u):
            wait(act, fxt_psum, u + 1)
            g, b_ = XR_GAIN[n["l"]]
            for c in range(KC):
                last = nc.scalar.activation(fxT[:, c, :], ps_xv[:, P * c:P * (c + 1)], ACT.Identity, bias=col[b_][:, c:c + 1], scale=col[g][:, c:c + 1])
            last.then_inc(fxt_sb, 1)

        def relu_a(n):
            f = n["j"] * NS + n["s"]
            wait(act, ff_up, 2 * f + 1)
            for j in range(4):
                last = nc.scalar.activation(hT[:, j, :], ps_qk[:, P * j:P * (j + 1)], ACT.Relu, bias=bff1[:, j:j + 1])
            last.then_inc(ff_relu_a, 1)

        def router_exps(n):
            r = n["j"] * NS + n["s"]
            wait(act, rt_step, RT * r + 3)
            nc.scalar.activation(ex[:], lg[:], ACT.Exp, bias=rsm[:, 0:1], accum_out=rsm[:, 1:2]).then_inc(rt_exp, 1)

        def router_weight(n):
            r = n["j"] * NS + n["s"]
            wait(act, rt_step, RT * r + 7)
            nc.scalar.activation(rsm[:, 4:5], rsm[:, 3:4], ACT.Exp).then_inc(rt_exp, 1)

        def run(i, tau, t, first, last):
            at_ = parts(i, tau, first, last)
            now, ff, rk_, nxt = at_(0), at_(-2), at_(-3), at_(1)
            u_of = lambda n: n["j"] * 2 * NS + (0 if n["l"] == 0 else NS) + n["s"]
            if first and tau == 0:
                xt_evac(now)
                act.wait_ge(ld_cols, 32)
                qk_evac(now)
            if now["ok"] and now["l"] == 0:
                wait(act, mask_ready, 3 * (now["j"] * NS + now["s"] + 1))
            ff_now = ff["ok"] and ff["l"] == 0
            routing = rk_["ok"] and rk_["l"] == 3
            if rk_["ok"] and rk_["l"] == 0:
                mt_evac(now)
                xt_evac(nxt)
                exps(now, range(1))
                qk_evac(nxt)
                exps(now, range(1, 4) if not ff_now else range(1, 3))
            else:
                if nxt["ok"]:
                    xt_evac(nxt)
                if now["ok"]:
                    mt_evac(now)
                if routing:
                    router_exps(rk_)
                if nxt["ok"]:
                    qk_evac(nxt)
                if now["ok"]:
                    exps(now, range(1))
                if routing:
                    router_weight(rk_)
                if now["ok"]:
                    exps(now, range(1, 4) if not ff_now else range(1, 3))
            if ff["ok"] and ff["l"] in (0, 3):
                fxt_evac(ff, u_of(ff))
            if ff_now:
                exps(now, range(3, 4))
                relu_a(ff)
        slots(run, act)

        def copy_weights(k, par):
            e = act.value_load(tbi[0:1, 1, bass.ds(k, 1)], min_val=0, max_val=E - 1)
            wait(act, ld_experts, e * 48 + 16)
            wait(act, b_up, k - 1)
            nc.scalar.copy(w1_now[:, par].rearrange("p c n -> p (c n)"),
                           w1f[:, bass.ds(e * (KC * FF), KC * FF)]).then_inc(w1_copied, 1)

        def hidden(k, par):
            wait(act, b_up, k + 1)
            wait(act, b_b1, k + 1)
            wait(act, b_down, k)
            for j in range(FC):
                last = nc.scalar.activation(gT[:, j, :], ps_s[:, 2 * par + j // 4, P * (j % 4):P * (j % 4 + 1)], ACT.Gelu,
                                            bias=b1s[par][:, j:j + 1])
            last.then_inc(b_gelu, 1)

        act.wait_ge(table_step, TABLE_ALL)
        act.wait_ge(rt_rank, B)
        act.wait_ge(xr_ready, NT)
        act.wait_ge(ld_w1, 16 * W1_EARLY)
        copy_weights(0, 0)
        copy_weights(1, 1)
        hidden(0, 0)

        def tile_pair(j):
            for d in (1, 2):
                k = 2 * j + d
                copy_weights(k + 1, (d + 1) % 2)
                hidden(k, d % 2)
        pairs(tile_pair, act)

        def run_c(j, st, b, first, last):
            c = cparts(j, st, first, last)
            now, g_, h_, nxt = c(0), c(-2), c(-3), c(1)
            if first and st == 0:
                ctxt_evac(now)
                xt_evac(now)
                qk_evac(now)
            if nxt["ok"]:
                ctxt_evac(nxt)
            if now["ok"]:
                mt_evac(now)
            if nxt["ok"]:
                xt_evac(nxt)
            if h_["ok"]:
                wait(act, c_gstep, 9 * h_["b"] + 1)
                nc.scalar.activation(ge, gu, ACT.Exp, scale=-1.0).then_inc(c_exp, 1)
            if now["ok"]:
                exps(now, range(1))
            if nxt["ok"]:
                qk_evac(nxt)
            if now["ok"]:
                exps(now, range(1, 4))
            if g_["ok"]:
                wait(act, c_att_psum, g_["b"] + 1)
                nc.scalar.copy(atT, ps_xv[:, 0:D].rearrange("p (c q) -> p c q", c=KC)).then_inc(c_att_sb, 1)
        cslots(run_c, act)

    @block.vector
    def _(dve):
        V = nc.vector

        V.memset(bd[0], 0.0)
        V.memset(bd[1], 0.0)
        V.memset(bd[2], 0.0).then_inc(bd_zero, 1)
        V.memset(one_b[:], 1.0)
        V.memset(one_f[:], 1.0)
        V.memset(mean_w[:], 1.0 / P)
        V.memset(neghalf[:], -0.5)
        V.memset(zeros[:], 0.0)
        V.memset(mb[:], 0.0)
        for i in range(2):
            V.memset(vz[i][:], 0.0)
            V.memset(kmask[i][:], 0.0)
        V.memset(onz[:, 0, 1, :], 0.0)
        V.memset(onz[:, 1, 0, :], 0.0)
        V.memset(onz[:, 0, 0, :], 1.0)
        V.memset(onz[:, 1, 1, :], 1.0)
        dve.wait_ge(ld_const, 32)
        V.tensor_copy(ident_b[:], ident)
        V.tensor_copy(causal_b[:], pt[:, 0, :])
        V.tensor_copy(win_b[:], pt[:, 1, :])
        V.tensor_copy(base[:], consts[:, C_EBASE:C_TILE])
        V.tensor_copy(ecol_b[:], consts[:, C_ECOL:C_IOTA]).then_inc(consts_ready, 1)
        dve.wait_ge(consts_ready, 1)

        def vz_evac(n):
            t, l, p = n["t"], n["l"], n["p"]
            wait(dve, v_psum, t + 1)
            if l == 4:
                src = ps_xv[:, D:D + HD]
                for par in range(2):
                    last = V.tensor_tensor(vz[p][:, :, par, par, :], src.unsqueeze(1).to_broadcast([P, H // 2, HD]),
                                           bv3[:].unsqueeze(1).to_broadcast([P, H // 2, HD]), ALU.add)
            else:
                src = ps_xv[:, D:2 * D].rearrange("p (h two d) -> p h two d", two=2, d=HD)
                bv = LAYER[l]["bv"]
                for par in range(2):
                    if bv is None:
                        last = V.tensor_copy(vz[p][:, :, par, par, :], src[:, :, par, :])
                    else:
                        last = V.tensor_tensor(vz[p][:, :, par, par, :], src[:, :, par, :],
                                               rows[bv].rearrange("p (h two d) -> p h two d", two=2, d=HD)[:, :, par, :], ALU.add)
            last.then_inc(vz_ready, 1)

        def qk_lo(n):
            t, l, p = n["t"], n["l"], n["p"]
            wait(dve, qk_sb, t + 1)
            wait(dve, qbd_lo_ready, t)
            L = LAYER[l]
            srcs = ps_qk[:].rearrange("p (m c q) -> p m c q", m=2, c=KC)
            for m, hi, lo, bias in ((0, qT, qT_lo, L["bq"]), (1, kT[p], kT_lo[p], L["bk"])):
                if l == 4 and m == 1:
                    last = V.scalar_tensor_tensor(lo[:, 0, :].bitcast(F32R), srcs[:, 1, 0], bk3[:], hi[:, 0, :], ALU.add, ALU.subtract)
                elif bias is None:
                    last = V.tensor_tensor(lo[:].bitcast(F32R), srcs[:, m], hi[:], ALU.subtract)
                else:
                    for c in range(KC):
                        last = V.scalar_tensor_tensor(lo[:, c, :].bitcast(F32R), srcs[:, m, c], col[bias][:, c:c + 1], hi[:, c, :],
                                                      ALU.add, ALU.subtract)
            last.then_inc(qk_lo_ready, 1)

        def expand_half(n):
            wait(dve, qk_sb, n["t"] + 1)
            V.tensor_tensor(qbd[n["p"]][:, 1].bitcast(F32R), qT[:, 1, :].unsqueeze(1).to_broadcast([P, HPC, P]),
                            hmask.unsqueeze(2).to_broadcast([P, HPC, P]), ALU.mult).then_inc(qbd_half_ready, 1)

        def mask_prep(n):
            b = n["j"] * NS + n["s"]
            par = n["s"] % 2
            wait(dve, mask_loaded[par], 16 * (n["h"] + 1))
            wait(dve, probs_ready, 4 * (n["t"] - 2 + 1) if n["s"] >= 2 else 4 * (n["t"] - TPI + 2 + 1))
            V.tensor_scalar(kmask[par][0:1, :], kmi[par][0:1, :], 0.0, NEG, ALU.is_equal, ALU.mult).then_inc(mask_ready, 1)
            V.tensor_scalar(kmcol[par][:], mask_cols[:, bass.ds(b, 1)], 0.0, NEG * LAYER[0]["scale"], ALU.is_equal, ALU.mult).then_inc(mask_ready, 2)

        def maxima(n):
            t = n["t"]
            for half in range(2):
                wait(dve, scores_ready, 2 * t + half + 1)
                V.tensor_reduce(nm[:, 8 * half:8 * half + 8],
                                ps_s[:, 2 * half:2 * half + 2, :].rearrange("p g (h k) -> p (g h) k", h=4),
                                AX_X, ALU.max, negate=True).then_inc(maxima_part, 1)
            dve.wait_ge(maxima_part, 4 * t + 2)
            V.tensor_copy(mb[:, 0:H], nm[:]).then_inc(maxima_part, 1)
            dve.wait_ge(maxima_part, 4 * t + 3)
            V.tensor_tensor(mb[:, H:2 * H], nm[:], mb[:, 0:H], ALU.subtract).then_inc(maxima_part, 1)
            dve.wait_ge(maxima_part, 4 * t + 4)
            V.tensor_copy(mb[:, 2 * H:2 * H + 1], zeros[:, 0:1]).then_inc(maxima_ready, 1)

        def normalise(n):
            t = n["t"]
            wait(dve, av_ready, t + 1)
            V.reciprocal(rs[:], ps_o[:, 2:4, :]).then_inc(recip_ready, 1)
            dve.wait_ge(recip_ready, t + 1)
            V.tensor_tensor(oT[:], ps_o[:, 0:2, :], rs[:], ALU.mult).then_inc(ot_ready, 1)

        def norm_stats(kind, y, step, n_):
            wait_apart(dve, step, 5 * n_ + 1)
            V.bn_stats(st6[kind][:], y).then_inc(step, 1)
            wait_apart(dve, step, 5 * n_ + 2)
            V.bn_aggr(mv[kind][:], st6[kind][:]).then_inc(step, 1)
            dve.wait_ge(step, 5 * n_ + 3)
            V.tensor_scalar_add(ve[kind][:], mv[kind][:, 1:2], LN_EPS).then_inc(step, 1)

        def norm_apply(kind, dst, y, step, rs_sem, n_):
            wait(dve, rs_sem, n_ + 1)
            V.tensor_scalar(dst, y, mv[kind][:, 0:1], rstd[kind][:], ALU.subtract, ALU.mult).then_inc(step, 1)

        def relu_b(n):
            f = n["j"] * NS + n["s"]
            wait(dve, ff_up, 2 * f + 2)
            for j in range(4):
                last = V.tensor_scalar(hT[:, 4 + j, :], ps_xv[:, P * j:P * (j + 1)], bff1[:, 4 + j:5 + j], 0.0, ALU.add, ALU.max)
            last.then_inc(ff_relu_b, 1)

        def router_link(n, k, ins):
            ins.then_inc(rt_step, 1)
            wait_apart(dve, rt_step, RT * (n["j"] * NS + n["s"]) + k)

        def router_logits(n):
            wait(dve, rt_logits, n["j"] * NS + n["s"] + 1)
            router_link(n, 1, V.tensor_tensor(lg[:], ps_w[:, 0:E], rb[:], ALU.add))
            router_link(n, 2, V.max(mx8[:], lg[:]))
            router_link(n, 3, V.tensor_scalar_mul(rsm[:, 0:1], mx8[:, 0:1], -1.0))

        def router_choice(n):
            q = r_par(n)
            wait(dve, rt_exp, 2 * (n["j"] * NS + n["s"]) + 1)
            router_link(n, 4, V.reciprocal(rsm[:, 2:3], rsm[:, 1:2]))
            router_link(n, 5, V.tensor_scalar_mul(pr[:], ex[:], rsm[:, 2:3]))
            router_link(n, 6, V.max(p8[:], pr[:]))
            router_link(n, 7, V.tensor_tensor(rsm[:, 3:4], p8[:, 1:2], p8[:, 0:1], ALU.subtract))
            router_link(n, 8, V.max_index(ix8[:], p8[:], pr[:]))
            router_link(n, 9, V.tensor_copy(ixf[:], ix8[:, 0:TOPK]))
            for k_ in range(TOPK):
                router_link(n, 10 + k_, V.tensor_scalar(oh[q][:, k_, :], iota8, ixf[:, k_:k_ + 1], None, ALU.is_equal))
            router_link(n, RT, V.tensor_tensor(ohm[q][:], oh[q][:, 0, :], oh[q][:, 1, :], ALU.add))

        def router_weights(n):
            r = n["j"] * NS + n["s"]
            wait(dve, rt_exp, 2 * r + 2)
            V.tensor_scalar_add(rsm[:, 5:6], rsm[:, 4:5], 1.0).then_inc(rt_w_step, 1)
            dve.wait_ge(rt_w_step, 3 * r + 1)
            V.reciprocal(rsm[:, 6:7], rsm[:, 5:6]).then_inc(rt_w_step, 1)
            dve.wait_ge(rt_w_step, 3 * r + 2)
            V.tensor_copy(w_all[:, bass.ds(r * TOPK, 1)], rsm[:, 6:7])
            V.tensor_tensor(w_all[:, bass.ds(r * TOPK + 1, 1)], rsm[:, 4:5], rsm[:, 6:7], ALU.mult).then_inc(rt_w_step, 1)

        def positions(n):
            r = n["j"] * NS + n["s"]
            q = r_par(n)
            wait(dve, rt_rank, r + 1)
            V.tensor_tensor(rk[:], ps_w[:, D:D + E], base[:], ALU.add).then_inc(rt2_step, 1)
            dve.wait_ge(rt2_step, 6 * r + 1)
            for k_ in range(TOPK):
                V.scalar_tensor_tensor(junk[:], oh[q][:, k_, :], 1.0, rk[:], ALU.mult, ALU.mult,
                                       accum_out=posf[:, k_:k_ + 1]).then_inc(rt2_step, 1)
                dve.wait_ge(rt2_step, 6 * r + 2 + k_)
            wait(dve, xinit_ready, r + 1)
            V.tensor_copy(posu[n["s"]][:], posf[:]).then_inc(rt2_step, 1)
            V.tensor_tensor(base[:], base[:], ps_w[:, D + E:D + 2 * E], ALU.add).then_inc(rt2_step, 1)
            V.tensor_copy(pos_all[:, bass.ds(r * TOPK, TOPK)], posf[:]).then_inc(rt2_step, 1)

        def run(i, tau, t, first, last):
            at_ = parts(i, tau, first, last)
            now, prev, ff, rk_, nxt = at_(0), at_(-1), at_(-2), at_(-3), at_(1)
            if first and tau == 0:
                vz_evac(now)
                dve.wait_ge(ld_cols, 32)
                qk_lo(now)
                mask_prep(now)
                dve.wait_ge(ld_rows, 16 * len(row_names))
                for dst, add in (("L0_xattn_beta1", "L0_xattn_b_ff2"), ("L1_xattn_beta", "L2_xattn_sa_bo"), ("L2_xattn_ln1_b", "L2_xattn_ca_bo")):
                    last_ = V.tensor_tensor(rows[dst], rows[dst], rows[add], ALU.add)
                last_.then_inc(rows_ready, 1)
            old = at_(-4)
            routing = rk_["ok"] and rk_["l"] == 3
            ranking = old["ok"] and old["l"] == 3
            if ranking and not routing:
                positions(old)
            if now["ok"]:
                maxima(now)
            if ranking and routing:
                positions(old)
            if ff["ok"]:
                norm_stats(0, yb[0][:], ln_step, ff["t"])
            if routing:
                if first and rk_["s"] == 0:
                    dve.wait_ge(ld_router, 16 * 2)
                router_logits(rk_)
            if rk_["ok"] and rk_["l"] == 0:
                f = rk_["j"] * NS + rk_["s"]
                wait(dve, ff_down, f + 1)
                wait(dve, xr_ready, rk_["t"] + 1)
                V.tensor_tensor(yb[1][:], ps_w[:, 0:D], xr[rk_["s"]][:], ALU.add).then_inc(ffln_step, 1)
                norm_stats(1, yb[1][:], ffln_step, f)
                norm_apply(1, xn[rk_["s"]][:], yb[1][:], ffln_step, ffrstd_ready, f)
            if prev["ok"]:
                normalise(prev)
            if ff["ok"]:
                norm_apply(0, xn[ff["s"]][:], yb[0][:], ln_step, rstd_ready, ff["t"])
            if nxt["ok"]:
                if nxt["l"] == 0:
                    mask_prep(nxt)
                vz_evac(nxt)
            if routing:
                router_choice(rk_)
            if nxt["ok"]:
                if nxt["l"] > 0:
                    expand_half(nxt)
                qk_lo(nxt)
            if prev["ok"]:
                wait(dve, wo_ready, prev["t"] + 1)
                residual_ready(prev)
                wait(dve, ln_step, 5 * prev["t"])
                V.tensor_tensor(yb[0][:], ps_w[:, 0:D], xr[prev["s"]][:], ALU.add).then_inc(ln_step, 1)
            if routing:
                router_weights(rk_)
            if ff["ok"] and ff["l"] == 0:
                relu_b(ff)

        def residual_ready(n):
            l, j = n["l"], n["j"]
            f = j * NS + n["s"]
            if l == 0:
                wait(dve, xinit_ready, f + 1)
            elif l == 1:
                wait(dve, ffxr_ready, f + 1)
            else:
                wait(dve, xr_ready, n["t"] - NS + 1)
        slots(run, dve)

        step = [0]

        def tlink(ins):
            ins.then_inc(table_step, 1)
            step[0] += 1
            dve.wait_ge(table_step, step[0])
        dve.wait_ge(rt2_step, 6 * B)
        tlink(V.tensor_copy(tails[:], base[:]))
        assert step[0] == TABLE_TAILS
        cnt, incl, excl, n_t = tt[:, 0], tt[:, 1], tt[:, 2], tt[:, 3]
        tlink(V.tensor_tensor(cnt, base[:], consts[:, C_EBASE:C_TILE], ALU.subtract))
        tlink(V.tensor_scalar_add(tti[:, 0], cnt, float(P - 1)))
        tlink(V.tensor_scalar(tti[:, 1], tti[:, 0], 7, None, ALU.arith_shift_right))
        tlink(V.tensor_copy(n_t, tti[:, 1]))
        tlink(V.tensor_scalar(tt[:, 4], n_t, 0.0, 1.0, ALU.mult, ALU.add))
        tlink(V.tensor_tensor_scan(incl, tt[:, 4], n_t, 0.0, ALU.mult, ALU.add))
        eid, ex_, row_, addr = tb[:, 0], tb[:, 1], tb[:, 2], tb[:, 3]
        tlink(V.memset(tb[:, 0:2], 0.0))
        for e in range(E):
            tlink(V.tensor_scalar(tb[:, 4], tile_iota, incl[:, e:e + 1], None, ALU.is_ge))
            tlink(V.tensor_tensor(eid, eid, tb[:, 4], ALU.add))
            tlink(V.scalar_tensor_tensor(ex_, tb[:, 4], n_t[:, e:e + 1], ex_, ALU.mult, ALU.add))
        tlink(V.tensor_tensor(row_, tile_iota, ex_, ALU.subtract))
        tlink(V.tensor_scalar_mul(row_, row_, float(P)))
        tlink(V.scalar_tensor_tensor(addr, eid, float(SPAN), row_, ALU.mult, ALU.add))
        tlink(V.tensor_copy(tbi[:, 0, 0:TILES], addr))
        tlink(V.tensor_scalar_min(tbi[:, 1, 0:TILES], eid, float(E - 1)))
        tlink(V.tensor_copy(tbi[:, 1, TILES:TILES + 1], tbi[:, 1, TILES - 1:TILES]))
        tlink(V.tensor_copy(tbi[:, 2, TILES - 3:TILES], tbi[:, 0, TILES - 1:TILES].to_broadcast([P, 3])))
        tlink(V.tensor_copy(tbi[:, 2, 0:TILES - 3], tbi[:, 0, 3:TILES]))
        assert step[0] == TABLE_ALL
        tlink(V.tensor_scalar(shift[:], n_t, float(P), -float(SPAN), ALU.mult, ALU.add))
        pos_in = yb[1][:, 0:B * TOPK]
        moved = yb[1][:, P:P + B * TOPK]
        tlink(V.tensor_copy(pos_in, pos_all[:]))
        for e in range(1, E):
            tlink(V.tensor_scalar(moved, pos_in, float(e * SPAN), shift[:, e - 1:e], ALU.is_ge, ALU.mult))
            tlink(V.tensor_tensor(pos_all[:], pos_all[:], moved, ALU.add))

        dve.wait_ge(ld_b2, 16)

        def tile_evac(k, par):
            wait(dve, b_xt_psum, k + 1)
            V.tensor_copy(xgT[par], ps_xv[:, 0:D].rearrange("p (c q) -> p c q", c=KC)).then_inc(b_xt_sb, 1)

        def tile_bias(k, par):
            e = dve.value_load(tbi[0:1, 1, bass.ds(k, 1)], min_val=0, max_val=E - 1)
            V.tensor_copy(b1s[par][:], b1T[:, bass.ds(e * FC, FC)]).then_inc(b_b1, 1)

        def tile_y(k, par, use):
            e = dve.value_load(tbi[0:1, 1, bass.ds(k, 1)], min_val=0, max_val=E - 1)
            wait(dve, b_down, k + 1)
            wait(dve, b_stored[par], 16 * use)
            V.tensor_tensor(ys[par], ps_w[:, 0:D], b2.rearrange("p e d -> p (e d)")[:, bass.ds(e * D, D)], ALU.add).then_inc(b_y, 1)

        tile_bias(0, 0)
        tile_evac(0, 0)
        tile_evac(1, 1)

        def tile_pair(j):
            for d in (1, 2):
                k = 2 * j + d
                tile_bias(k, d % 2)
                tile_evac(k + 1, (d + 1) % 2)
                tile_y(k - 1, (d - 1) % 2, j)
        pairs(tile_pair, dve)
        tile_y(TILES - 1, 0, (TILES - 1) // 2)

        dve.wait_ge(ld_l3, 16 * 11)
        V.tensor_copy(w3k[:], w3kv_raw[:, 0].unsqueeze(2).to_broadcast([P, KC, HPC, HD])).then_inc(b_y, 1)

        def index_prep(n):
            b = n["b"]
            wait(dve, c_gathered[n["p"]], 32 * n["h"])
            for k_ in range(TOPK):
                last = V.tensor_copy(pidx[n["p"]][k_][:], pos_all[:, bass.ds(b * TOPK + k_, 1)])
            last.then_inc(c_idx, 1)

        def combine(n):
            b, p = n["b"], n["p"]
            wait(dve, c_gathered[p], 32 * (n["h"] + 1))
            wait(dve, c_loaded[p], 16 * (n["h"] + 1))
            V.tensor_copy(wsel[p][:], w_all[:, bass.ds(b * TOPK, TOPK)])
            V.tensor_copy(rsm[:, 0:1], zeros[:, 0:1]).then_inc(rt_w_step, 1)
            dve.wait_ge(rt_w_step, 3 * B + b + 1)
            V.scalar_tensor_tensor(gq, yg[p][0], wsel[p][:, 0:1], x2l[p], ALU.mult, ALU.add).then_inc(c_ln, 1)
            dve.wait_ge(c_ln, 6 * b + 1)
            V.scalar_tensor_tensor(yb[0][:], yg[p][1], wsel[p][:, 1:2], gq, ALU.mult, ALU.add).then_inc(c_ln, 1)
            wait_apart(dve, c_ln, 6 * b + 2)
            V.bn_stats(st6[2][:], yb[0][:]).then_inc(c_ln, 1)
            wait_apart(dve, c_ln, 6 * b + 3)
            V.bn_aggr(mv[2][:], st6[2][:]).then_inc(c_ln, 1)
            dve.wait_ge(c_ln, 6 * b + 4)
            V.tensor_scalar_add(ve[2][:], mv[2][:, 1:2], LN_EPS).then_inc(c_ln, 1)

        def combine_apply(n):
            b = n["b"]
            wait(dve, c_rstd, b + 1)
            wait(dve, c_xr, b - NS + 1)
            V.tensor_scalar(xn[n["s"]][:], yb[0][:], mv[2][:, 0:1], rstd[2][:], ALU.subtract, ALU.mult).then_inc(c_ln, 1)

        def gate_link(n, k, ins):
            ins.then_inc(c_gstep, 1)
            dve.wait_ge(c_gstep, 9 * n["b"] + k)

        def gate_open(n):
            wait(dve, c_gate, n["b"] + 1)
            gate_link(n, 1, V.tensor_tensor(gu, ps_w[:, 0:D], row3["L3_xattn_bg"][:], ALU.add))
            gate_link(n, 2, V.tensor_tensor(gd, at[n["s"]], xr[n["s"]][:], ALU.subtract))

        def gate_apply(n):
            wait(dve, c_exp, n["b"] + 1)
            gate_link(n, 3, V.tensor_scalar_add(ge, ge, 1.0))
            gate_link(n, 4, V.reciprocal(gq, ge))
            gate_link(n, 5, V.tensor_tensor(gu, gu, gq, ALU.mult))
            gate_link(n, 6, V.tensor_tensor(gd, gd, gu, ALU.mult))
            gate_link(n, 7, V.tensor_tensor(go, gd, xr[n["s"]][:], ALU.add))
            gate_link(n, 8, V.scalar_tensor_tensor(gd, go, 1.0 / D, go, ALU.mult, ALU.mult, accum_out=ssq[:]))
            gate_link(n, 9, V.tensor_scalar_add(ve[3][:], ssq[:], RMS_EPS))

        def rms_apply(n):
            b = n["b"]
            wait(dve, c_rms, 5 * b + 4)
            V.scalar_tensor_tensor(xh[n["p"]], go, rstd[3][:], row3["L3_xattn_rms_w"][:], ALU.mult, ALU.mult).then_inc(c_rms, 1)

        def finish(n):
            b = n["b"]
            wait(dve, c_mean, b + 1)
            wait(dve, c_out[n["p"]], 16 * n["h"])
            V.tensor_tensor(fin[n["p"]], xh[n["p"]], ps_w[:, D:2 * D], ALU.subtract).then_inc(c_fin, 1)

        def run_c(j, st, b, first, last):
            c = cparts(j, st, first, last)
            now, prev, g_, m_, nxt, nn = c(0), c(-1), c(-3), c(-4), c(1), c(2)
            if first and st == 0:
                for q in (now, nxt):
                    index_prep(q)
                    combine(q)
                    combine_apply(q)
                index_prep(nn)
                vz_evac(now)
                qk_lo(now)
            if now["ok"]:
                maxima(now)
            if nxt["ok"] and not (first and st == 0):
                combine_apply(nxt)
            if m_["ok"]:
                rms_apply(m_)
            if g_["ok"]:
                gate_open(g_)
            if prev["ok"]:
                normalise(prev)
            if nxt["ok"]:
                vz_evac(nxt)
            if c(3)["ok"]:
                index_prep(c(3))
            if g_["ok"]:
                gate_apply(g_)
            if nxt["ok"]:
                qk_lo(nxt)
            if prev["ok"]:
                wait(dve, wo_ready, prev["t"] + 1)
            if m_["ok"]:
                finish(m_)
            if prev["ok"]:
                V.tensor_tensor(at[prev["s"]], ps_w[:, 0:D], row3["L3_xattn_bo"][:], ALU.add).then_inc(c_at, 1)
            if nn["ok"]:
                combine(nn)
        cslots(run_c, dve)

    @block.gpsimd
    def _(pool):
        G = nc.gpsimd

        pool.wait_ge(bd_zero, 1)
        for h in range(HPC):
            load_block(pool, 2, "wv", h, ld_bd_pool)
        for h in range(HPC // 2, HPC):
            load_block(pool, 0, "wq", h, ld_bd_pool)

        def expand(n):
            t, p = n["t"], n["p"]
            wait(pool, qk_sb, t + 1)
            for c in range(KC // 2):
                last = G.tensor_tensor(qbd[p][:, c].bitcast(F32R), qT[:, c, :].unsqueeze(1).to_broadcast([P, HPC, P]),
                                       hmask.unsqueeze(2).to_broadcast([P, HPC, P]), ALU.mult)
            last.then_inc(qbd_ready, 1)

        def expand_lo(n):
            t = n["t"]
            wait(pool, qk_lo_ready, t + 1)
            wait(pool, st_ready, 4 * t)
            for c in range(KC):
                last = G.tensor_tensor(qbd_lo[:, c].bitcast(F32R), qT_lo[:, c, :].unsqueeze(1).to_broadcast([P, HPC, P]),
                                       hmask.unsqueeze(2).to_broadcast([P, HPC, P]), ALU.mult)
            last.then_inc(qbd_lo_ready, 1)

        def x_init(n):
            f = n["j"] * NS + n["s"]
            wait(pool, x_loaded[n["s"] % 2], 16 * (n["h"] + 1))
            wait(pool, x2_stored[n["s"]], 16 * n["j"])
            wait(pool, scattered[n["s"]], 32 * n["j"])
            G.tensor_tensor(xr[n["s"]][:], xin[n["s"] % 2][:], rows["L0_xattn_b_out"], ALU.add).then_inc(xinit_ready, 1)

        def root(kind, step, value, done):
            wait(pool, step, value)
            G.tensor_tensor(rstd[kind][:], ve[kind][:], neghalf[:], ALU.pow).then_inc(done, 1)

        def residual(n, g, b_, step, value, part, done, count):
            wait(pool, step, value)
            G.tensor_tensor(xr[n["s"]][:], xn[n["s"]][:], g, ALU.mult).then_inc(part, 1)
            wait(pool, part, count + 1)
            G.tensor_tensor(xr[n["s"]][:], xr[n["s"]][:], b_, ALU.add).then_inc(done, 1)

        def scatter(n):
            r = n["j"] * NS + n["s"]
            wait_apart(pool, rt2_step, 6 * r + 6)
            wait_apart(pool, xr_ready, n["t"] + 1)
            for k_ in range(TOPK):
                G.indirect_dma_start(sorted_x, bass.IndirectOffsetOnAxis(posu[n["s"]][:, k_:k_ + 1], 0),
                                     xr[n["s"]][:], None).then_inc(scattered[n["s"]], 16)

        def run(i, tau, t, first, last):
            at_ = parts(i, tau, first, last)
            prev, ff, rk_, nxt, now = at_(-1), at_(-2), at_(-3), at_(1), at_(0)
            if first and tau == 0:
                pool.wait_ge(ld_const, 32)
                pool.wait_ge(consts_ready, 1)
                expand(now)
                expand_lo(now)
                pool.wait_ge(rows_ready, 1)
                x_init(now)
            if ff["ok"]:
                root(0, ln_step, 5 * ff["t"] + 4, rstd_ready)
            old = at_(-4)
            if old["ok"] and old["l"] == 3:
                scatter(old)
            ff_behind = rk_["ok"] and rk_["l"] == 0
            f = rk_["j"] * NS + rk_["s"]
            if ff_behind:
                root(1, ffln_step, 5 * f + 4, ffrstd_ready)
            if nxt["ok"]:
                expand(nxt)
            if now["ok"] and now["l"] == 0 and not (first and tau == 0):
                x_init(now)
            if ff["ok"]:
                g, b_ = XR_GAIN[ff["l"]]
                residual(ff, rows[g], rows[b_], ln_step, 5 * ff["t"] + 5, xr_part, xr_ready, ff["t"])
            if ff_behind:
                residual(rk_, rows["L0_xattn_g2"], rows["L0_xattn_beta2"], ffln_step, 5 * f + 5, ffxr_part, ffxr_ready, f)
            if nxt["ok"]:
                expand_lo(nxt)
        slots(run, pool)

        pool.wait_ge(rt_rank, B)
        pool.wait_ge(rt2_step, 6 * B)
        pool.wait_ge(xr_ready, NT)

        def load_w2(e, j0, j1):
            pool.dma_start(arena[:, :].rearrange("p (e j n) -> p e j n", e=E, j=FC)[:, e, j0:j1],
                           a["L2_xattn_e_w2"][e].rearrange("(j p) n -> p j n", p=P)[:, j0:j1]).then_inc(ld_experts, 16)
        load_w2(0, 0, FC)
        pool.wait_ge(ld_experts, 16)
        for e in range(W1_EARLY, E):
            pool.dma_start(w1[:, e], a["L2_xattn_e_w1"][e].rearrange("(c p) n -> p c n", p=P)).then_inc(ld_experts, 16)
        load_w2(1, 0, FC)
        pool.wait_ge(ld_experts, 16 + 48)
        for e in range(2, E):
            for j0, j1 in ((0, 3), (3, 6), (6, FC)):
                load_w2(e, j0, j1)
            pool.wait_ge(ld_experts, 16 + 48 * e)

        def gather(n):
            b, p = n["b"], n["p"]
            wait_apart(pool, c_idx, b + 1)
            wait_apart(pool, c_ln, 6 * (b - 2) + 2)
            for k_ in range(TOPK):
                G.indirect_dma_start(yg[p][k_], None, sorted_y,
                                     bass.IndirectOffsetOnAxis(pidx[p][k_][:], 0)).then_inc(c_gathered[p], 16)

        def c_root(n):
            root(2, c_ln, 6 * n["b"] + 5, c_rstd)

        def c_residual(n):
            wait(pool, c_gstep, 9 * (n["b"] - NS) + 7)
            residual(n, row3["L2_xattn_ln3_g"][:], row3["L2_xattn_ln3_b"][:], c_ln, 6 * n["b"] + 6, c_xr_part, c_xr, n["b"])

        for par in range(2):
            pool.wait_ge(b_stored[par], 16 * ((TILES + 1 - par) // 2))
        pool.wait_ge(ld_l3, 16 * 11)

        def run_c(j, st, b, first, last):
            c = cparts(j, st, first, last)
            now, g_, nxt, nn = c(0), c(-3), c(1), c(2)
            if first and st == 0:
                for q in (now, nxt):
                    gather(q)
                    c_root(q)
                gather(nn)
                expand(now)
                expand_lo(now)
            if nxt["ok"]:
                expand(nxt)
            if c(3)["ok"]:
                gather(c(3))
            if nxt["ok"]:
                expand_lo(nxt)
            if g_["ok"]:
                wait(pool, c_gstep, 9 * g_["b"] + 9)
                G.tensor_tensor(rstd[3][:], ve[3][:], neghalf[:], ALU.pow).then_inc(c_rms, 4)
            if nn["ok"]:
                c_root(nn)
            if now["ok"]:
                c_residual(now)
        cslots(run_c, pool)


TABLE_TAILS = 1
TABLE_ALL = TABLE_TAILS + 6 + 1 + 3 * E + 8


_NAMES = ["L0_xattn_wv", "L0_xattn_wk", "L0_xattn_wq", "L0_xattn_w_out", "L0_xattn_b_out", "L0_xattn_g1",
          "L0_xattn_beta1", "L0_xattn_w_ff1", "L0_xattn_b_ff1", "L0_xattn_w_ff2", "L0_xattn_b_ff2", "L0_xattn_g2",
          "L0_xattn_beta2", "L1_xattn_Wq", "L1_xattn_Wk", "L1_xattn_Wv", "L1_xattn_Wo", "L1_xattn_gamma",
          "L1_xattn_beta", "L2_xattn_sa_wq", "L2_xattn_sa_bq", "L2_xattn_sa_wk", "L2_xattn_sa_bk", "L2_xattn_sa_wv",
          "L2_xattn_sa_bv", "L2_xattn_sa_wo", "L2_xattn_sa_bo", "L2_xattn_ca_wq", "L2_xattn_ca_bq", "L2_xattn_ca_wk",
          "L2_xattn_ca_bk", "L2_xattn_ca_wv", "L2_xattn_ca_bv", "L2_xattn_ca_wo", "L2_xattn_ca_bo", "L2_xattn_ln1_g",
          "L2_xattn_ln1_b", "L2_xattn_ln2_g", "L2_xattn_ln2_b", "L2_xattn_ln3_g", "L2_xattn_ln3_b",
          "L2_xattn_router_w", "L2_xattn_router_b", "L2_xattn_e_w1", "L2_xattn_e_b1", "L2_xattn_e_w2",
          "L2_xattn_e_b2", "L3_xattn_Wq", "L3_xattn_bq", "L3_xattn_Wk", "L3_xattn_bk", "L3_xattn_Wv", "L3_xattn_bv",
          "L3_xattn_Wo", "L3_xattn_bo", "L3_xattn_Wg", "L3_xattn_bg", "L3_xattn_rms_w"]


def kernel(**inputs):
    import numpy as _np
    import concourse.bacc as _bacc
    from concourse import mybir as _mybir
    from concourse.bass_utils import run_bass_kernel_spmd as _run

    nc = _bacc.Bacc("TRN2", target_bir_lowering=False, num_devices=1)
    given = {"x": inputs["x"], "ctx": inputs["ctx_1024"], "mask": _np.asarray(inputs["mask_Bx1x1xS2_if1"]).reshape(B, P),
             "consts": constants()}
    given["mask_cols"] = _np.ascontiguousarray(given["mask"].T)
    chunks = lambda v: _np.asarray(v).reshape(-1, P).T
    given["cols"] = _np.concatenate(
        [chunks(inputs[n]) for n in COL_NAMES] + [chunks(inputs["L0_xattn_b_ff1"])]
        + [_np.tile(_np.asarray(inputs["L3_xattn_bk"]), HPC).reshape(P, 1)]
        + [_np.asarray(inputs["L2_xattn_e_b1"]).reshape(E * FC, P).T], axis=1)
    given.update({n: inputs[n] for n in _NAMES})
    arrays, args = {}, {}
    for name, v in given.items():
        v = _np.ascontiguousarray(v)
        arrays[f"in_{name}"] = v
        args[name] = nc.dram_tensor(f"in_{name}", v.shape, _mybir.dt.from_np(v.dtype), kind="ExternalInput").ap()
    out = nc.dram_tensor("out_0", (B, P, D), F32, kind="ExternalOutput").ap()
    build(nc, args, out)
    r = _run(nc, [arrays], core_ids=[0])
    return r.results[0]["out_0"]
```
